# Optimizing a Trainium2 kernel written in Bass

```python
import numpy as np
import jax
import jax.numpy as jnp

def _softmax(x, axis=-1):
    return jax.nn.softmax(x, axis=axis)

def _gelu(x):
    return jax.nn.gelu(x, approximate=True)

def _silu(x):
    return jax.nn.silu(x)

def _sigmoid(x):
    return jax.nn.sigmoid(x)

def _layernorm(x, axis=-1, eps=1e-05):
    m = jnp.mean(x, axis=axis, keepdims=True)
    v = jnp.var(x, axis=axis, keepdims=True)
    return (x - m) / jnp.sqrt(v + eps)

def _scatter_add(tgt, idx, src, axis=0):
    return tgt.at[idx].add(src)

def _segment_sum(src, seg, n):
    return jax.ops.segment_sum(src, seg, n)
kernel_name = 'mk_recurrent_d1_jaxref_r4_e9087c'

def setup_inputs(seed: int=0):
    np.random.seed(seed)
    _w = jnp.asarray

    def _L0_attn_setup():
        import jax, jax.numpy as jnp
        import numpy as np
        B, T, D = (4, 512, 256)
        H = 4
        K = D
        V = D
        DK = K // H
        DV = V // H
        LOW = 16
        GLN = 16.0

        def _layernorm(x, w, b, eps=1e-05):
            mu = x.mean(-1, keepdims=True)
            xc = x - mu
            var = (xc * xc).mean(-1, keepdims=True)
            return xc * jax.lax.rsqrt(var + eps) * w + b

        def _rmsnorm(x, w, eps=1e-05):
            ms = (x * x).mean(-1, keepdims=True)
            return x * jax.lax.rsqrt(ms + eps) * w

        def _gla_scan(q, k, v, gk):
            scale = DK ** (-0.5)
            qT = jnp.moveaxis(q * scale, 1, 0)
            kT = jnp.moveaxis(k, 1, 0)
            vT = jnp.moveaxis(v, 1, 0)
            gT = jnp.moveaxis(gk, 1, 0)

            def step(h, inp):
                qt, kt, vt, gt = inp
                h = h * jnp.exp(gt)[..., None] + kt[..., :, None] * vt[..., None, :]
                o = jnp.einsum('bhk,bhkv->bhv', qt, h)
                return (h, o)
            h0 = jnp.zeros((q.shape[0], H, DK, DV), q.dtype)
            _, oT = jax.lax.scan(step, h0, (qT, kT, vT, gT))
            return jnp.moveaxis(oT, 0, 1)
        key = jax.random.key(seed)
        ks = jax.random.split(key, 12)
        rn = lambda k, s: jax.random.normal(k, s, jnp.float32) * 0.02
        return {'x': jax.random.normal(ks[0], (B, T, D), jnp.float32), 'ln1_w': jnp.ones((D,), jnp.float32), 'ln1_b': jnp.zeros((D,), jnp.float32), 'Wq': rn(ks[1], (D, K)), 'Wk': rn(ks[2], (D, K)), 'Wv': rn(ks[3], (D, V)), 'Wg': rn(ks[4], (D, V)), 'Wgk1': rn(ks[5], (D, LOW)), 'Wgk2': rn(ks[6], (LOW, K)), 'bgk2': jnp.zeros((K,), jnp.float32), 'rms_w': jnp.ones((DV,), jnp.float32), 'Wo': rn(ks[7], (V, D)), 'ln2_w': jnp.ones((D,), jnp.float32), 'ln2_b': jnp.zeros((D,), jnp.float32), 'W1': rn(ks[8], (D, 3 * D)), 'b1': jnp.zeros((3 * D,), jnp.float32), 'W2': rn(ks[9], (3 * D, D)), 'b2': jnp.zeros((D,), jnp.float32)}
    _L0_attn_in = _L0_attn_setup()

    def _L0_ffn_setup():
        import jax, jax.numpy as jnp
        import numpy as np

        def _bitlinear(x, w_latent):
            scale = jax.lax.stop_gradient(jnp.clip(jnp.mean(jnp.abs(w_latent), axis=1, keepdims=True), 1e-05, None))
            tern = jnp.clip(jnp.round(w_latent / scale), -1.0, 1.0)
            w = w_latent + jax.lax.stop_gradient(tern - w_latent)
            return x @ (w * scale).T
        key = jax.random.key(seed)
        ks = jax.random.split(key, 6)
        dim, hidden, rank = (256, 1024, 16)
        B, S = (4, 1024)
        x = jax.random.normal(ks[0], (B, S, dim), dtype=jnp.float32)
        w_fc = 0.02 * jax.random.normal(ks[1], (hidden, dim), dtype=jnp.float32)
        w_proj = 0.02 * jax.random.normal(ks[2], (dim, hidden), dtype=jnp.float32)
        u = 0.02 * jax.random.normal(ks[3], (hidden, rank), dtype=jnp.float32)
        v = 0.02 * jax.random.normal(ks[4], (rank, dim), dtype=jnp.float32)
        fast_b = jax.random.normal(ks[5], (rank, rank), dtype=jnp.float32)
        gate = jnp.float32(0.05)
        return {'x': x, 'fast_b': fast_b, 'w_fc': w_fc, 'w_proj': w_proj, 'u': u, 'v': v, 'gate': gate}
    _L0_ffn_in = _L0_ffn_setup()
    _d = {'L0_attn_x': _L0_attn_in['x'], 'L0_attn_ln1_w': _L0_attn_in['ln1_w'], 'L0_attn_ln1_b': _L0_attn_in['ln1_b'], 'L0_attn_Wq': _L0_attn_in['Wq'], 'L0_attn_Wk': _L0_attn_in['Wk'], 'L0_attn_Wv': _L0_attn_in['Wv'], 'L0_attn_Wg': _L0_attn_in['Wg'], 'L0_attn_Wgk1': _L0_attn_in['Wgk1'], 'L0_attn_Wgk2': _L0_attn_in['Wgk2'], 'L0_attn_bgk2': _L0_attn_in['bgk2'], 'L0_attn_rms_w': _L0_attn_in['rms_w'], 'L0_attn_Wo': _L0_attn_in['Wo'], 'L0_attn_ln2_w': _L0_attn_in['ln2_w'], 'L0_attn_ln2_b': _L0_attn_in['ln2_b'], 'L0_attn_W1': _L0_attn_in['W1'], 'L0_attn_b1': _L0_attn_in['b1'], 'L0_attn_W2': _L0_attn_in['W2'], 'L0_attn_b2': _L0_attn_in['b2'], 'L0_ffn_fast_b': _L0_ffn_in['fast_b'], 'L0_ffn_w_fc': _L0_ffn_in['w_fc'], 'L0_ffn_w_proj': _L0_ffn_in['w_proj'], 'L0_ffn_u': _L0_ffn_in['u'], 'L0_ffn_v': _L0_ffn_in['v'], 'L0_ffn_gate': _L0_ffn_in['gate']}
    _x0 = _d['L0_attn_x']
    _d['L0_attn_x'] = jax.random.normal(jax.random.fold_in(jax.random.key(seed), 1), (4, 1024, 256), dtype=_x0.dtype)
    del _x0
    return _d

def reference(L0_attn_x, L0_attn_ln1_w, L0_attn_ln1_b, L0_attn_Wq, L0_attn_Wk, L0_attn_Wv, L0_attn_Wg, L0_attn_Wgk1, L0_attn_Wgk2, L0_attn_bgk2, L0_attn_rms_w, L0_attn_Wo, L0_attn_ln2_w, L0_attn_ln2_b, L0_attn_W1, L0_attn_b1, L0_attn_W2, L0_attn_b2, L0_ffn_fast_b, L0_ffn_w_fc, L0_ffn_w_proj, L0_ffn_u, L0_ffn_v, L0_ffn_gate):

    def _L0_attn_ref(x, ln1_w, ln1_b, Wq, Wk, Wv, Wg, Wgk1, Wgk2, bgk2, rms_w, Wo, ln2_w, ln2_b, W1, b1, W2, b2):
        import jax, jax.numpy as jnp
        import numpy as np
        B, T, D = (4, 512, 256)
        H = 4
        K = D
        V = D
        DK = K // H
        DV = V // H
        LOW = 16
        GLN = 16.0

        def _layernorm(x, w, b, eps=1e-05):
            mu = x.mean(-1, keepdims=True)
            xc = x - mu
            var = (xc * xc).mean(-1, keepdims=True)
            return xc * jax.lax.rsqrt(var + eps) * w + b

        def _rmsnorm(x, w, eps=1e-05):
            ms = (x * x).mean(-1, keepdims=True)
            return x * jax.lax.rsqrt(ms + eps) * w

        def _gla_scan(q, k, v, gk):
            scale = DK ** (-0.5)
            qT = jnp.moveaxis(q * scale, 1, 0)
            kT = jnp.moveaxis(k, 1, 0)
            vT = jnp.moveaxis(v, 1, 0)
            gT = jnp.moveaxis(gk, 1, 0)

            def step(h, inp):
                qt, kt, vt, gt = inp
                h = h * jnp.exp(gt)[..., None] + kt[..., :, None] * vt[..., None, :]
                o = jnp.einsum('bhk,bhkv->bhv', qt, h)
                return (h, o)
            h0 = jnp.zeros((q.shape[0], H, DK, DV), q.dtype)
            _, oT = jax.lax.scan(step, h0, (qT, kT, vT, gT))
            return jnp.moveaxis(oT, 0, 1)
        b, t = (x.shape[0], x.shape[1])
        xn = _layernorm(x, ln1_w, ln1_b)
        q = (xn @ Wq).reshape(b, t, H, DK)
        k = (xn @ Wk).reshape(b, t, H, DK)
        v = (xn @ Wv).reshape(b, t, H, DV)
        gk = (jax.nn.log_sigmoid(xn @ Wgk1 @ Wgk2 + bgk2) / GLN).reshape(b, t, H, DK)
        o = _gla_scan(q, k, v, gk)
        g = (xn @ Wg).reshape(b, t, H, DV)
        o = _rmsnorm(o, rms_w) * (g * jax.nn.sigmoid(g))
        o = o.reshape(b, t, V) @ Wo
        x = x + o
        xn2 = _layernorm(x, ln2_w, ln2_b)
        h = jax.nn.leaky_relu(xn2 @ W1 + b1, 0.01)
        h = h * h
        x = x + (h @ W2 + b2)
        return x

    def _L0_ffn_ref(x, fast_b, w_fc, w_proj, u, v, gate):
        import jax, jax.numpy as jnp
        import numpy as np

        def _bitlinear(x, w_latent):
            scale = jax.lax.stop_gradient(jnp.clip(jnp.mean(jnp.abs(w_latent), axis=1, keepdims=True), 1e-05, None))
            tern = jnp.clip(jnp.round(w_latent / scale), -1.0, 1.0)
            w = w_latent + jax.lax.stop_gradient(tern - w_latent)
            return x @ (w * scale).T
        h = _bitlinear(x, w_fc) + gate * (x @ v.T @ fast_b.T @ u.T)
        r = jnp.maximum(h, 0.0)
        return _bitlinear(r * r, w_proj)
    x = L0_attn_x
    xn = _layernorm(x, axis=-1)
    s = _L0_attn_ref(xn, L0_attn_ln1_w, L0_attn_ln1_b, L0_attn_Wq, L0_attn_Wk, L0_attn_Wv, L0_attn_Wg, L0_attn_Wgk1, L0_attn_Wgk2, L0_attn_bgk2, L0_attn_rms_w, L0_attn_Wo, L0_attn_ln2_w, L0_attn_ln2_b, L0_attn_W1, L0_attn_b1, L0_attn_W2, L0_attn_b2)
    g = _silu(_L0_ffn_ref(xn, L0_ffn_fast_b, L0_ffn_w_fc, L0_ffn_w_proj, L0_ffn_u, L0_ffn_v, L0_ffn_gate))
    x = x + s * g
    return x

_drawn_inputs = setup_inputs


def setup_inputs(seed=0):
    import zlib

    import numpy as np

    out = dict(_drawn_inputs(seed))
    spreads = {'L0_attn_ln1_w': (1.0, 0.6),
     'L0_attn_ln1_b': (0.0, 0.8),
     'L0_attn_bgk2': (0.0, 0.8),
     'L0_attn_rms_w': (1.0, 0.6),
     'L0_attn_ln2_w': (1.0, 0.6),
     'L0_attn_ln2_b': (0.0, 0.8),
     'L0_attn_b1': (0.0, 0.8),
     'L0_attn_b2': (0.0, 0.8)}
    factors = {'L0_attn_Wq': 8.0,
     'L0_attn_Wk': 8.0,
     'L0_attn_Wv': 8.0,
     'L0_attn_Wg': 8.0,
     'L0_attn_Wgk1': 8.0,
     'L0_attn_Wgk2': 8.0,
     'L0_attn_Wo': 8.0,
     'L0_attn_W1': 8.0,
     'L0_attn_W2': 8.0,
     'L0_ffn_fast_b': 8.0,
     'L0_ffn_u': 8.0,
     'L0_ffn_v': 8.0}
    for name, (base, spread) in spreads.items():
        noise = np.random.default_rng([zlib.crc32(name.encode()), seed]).standard_normal(out[name].shape)
        drawn = base * np.exp(spread * noise) if base else spread * noise
        out[name] = jnp.asarray(drawn.astype(out[name].dtype))
    for name, factor in factors.items():
        out[name] = (out[name] * factor).astype(out[name].dtype)
    return out
```

```python
from contextlib import ExitStack

import concourse.bass as bass
from concourse import mybir

F32 = mybir.dt.float32
F32R = mybir.dt.float32r
ACT = mybir.ActivationFunctionType
ALU = mybir.AluOpType
AX = mybir.AxisListType

P = 128
B, T, D = 4, 1024, 256
H, DK = 4, 64
LOW = 16
F1, FH = 3 * D, 4 * D
NT = 4
TB = NT * P
NB = B * T // TB
KD = D // P
M1, MH = F1 // P, FH // P
MID = P // 2 - 1
EPS = 1e-5
GLN = 16.0
CLAMP = 40.0

FRONT, BACK = "front", "back"
STEP = [
    ("T", 0), ("T", 1), ("W1", 0), ("XN", 0), ("W1", 1), ("L", 0), ("W2", 0), ("W1", 2),
    ("PU", 0), ("Z", 0), ("Z", 1), ("W2", 1), ("W1", 3), ("SCAN", 0), ("SCAN", 1), ("W2", 2), ("W1", 4),
    ("PG", 0), ("W2", 3), ("W1", 5), ("W2", 4), ("Q", 0), ("Q", 1), ("W2", 5), ("K", 0), ("K", 1),
    ("OUT", 0), ("VG", 0), ("SC", 0), ("VG", 1), ("SIG", 0), ("FC", 0), ("VG", 2), ("VG", 3),
    ("SIG", 1), ("SL", 0), ("ST", 0), ("AV", 0), ("FC", 1), ("PJ", 0), ("SC", 1), ("FC", 2),
    ("YT", 0), ("PJ", 1), ("ST", 1), ("AV", 1), ("SL", 1), ("WO", 0), ("FC", 3), ("PJ", 2),
    ("XT", 0), ("SC", 2), ("FC", 4), ("YT", 1), ("PJ", 3), ("ST", 2), ("AV", 2), ("WO", 1),
    ("LN", 0), ("FC", 5), ("PJ", 4), ("XT", 1), ("SC", 3), ("FC", 6), ("YT", 2), ("PJ", 5),
    ("ST", 3), ("AV", 3), ("WO", 2), ("FC", 7), ("PJ", 6), ("XT", 2), ("YT", 3), ("PJ", 7),
    ("WO", 3), ("XT", 3), ("PF", 0),
]
BACK_STAGES = ("W1", "W2", "PU", "PG", "OUT")
PER = {k: sum(s[0] == k for s in STEP) for k, _ in STEP}
RING_STAGES = ("T", "L", "Z", "Q", "K", "VG", "W1", "FC")
RING = 3
PROJ_STAGES = ("SC", "WO")
TURN_STAGES = ("SC", "YT", "XT")


def stages_of(front, back):
    return [s for s in STEP if (back if s[0] in BACK_STAGES else front)]


def tenant(stages, stage, kinds, banks):
    mine = [s for s in stages if s[0] in kinds]
    at = mine.index(stage)
    if at >= banks:
        return at % banks, mine[at - banks], False
    ends = [s for s in stages_of(True, False) if s[0] in kinds]
    return at % banks, ends[len(ends) - banks + at], True


def recurrent_block_kernel(nc, x, ln1_w, ln1_b, wq, wk, wv, wg, wgk1, wgk2, bgk2, rms_w, wo,
                           ln2_w, ln2_b, w1, b1, w2, b2, fast_b, w_fc, w_proj, u, v, gate, out):
    x_blocks = x.rearrange("b (m t p) d -> (b m) p t d", t=NT, p=P)
    out_blocks = out.rearrange("b (m t p) d -> (b m) p t d", t=NT, p=P)

    with ExitStack() as ctx:
        def sb(name, *shape, dt=F32):
            return ctx.enter_context(nc.sbuf_tensor(name, [P, *shape], dt))

        def sem(name):
            return ctx.enter_context(nc.semaphore(name))

        def f(ap):
            return ap.bitcast(F32)

        wqk_hi, wqk_lo = (sb(f"wqk_{s}", KD, 2 * D, dt=F32R) for s in ("hi", "lo"))
        wvg_hi, wvg_lo = (sb(f"wvg_{s}", KD, 2 * D, dt=F32R) for s in ("hi", "lo"))
        wl_hi, wl_lo = (sb(f"wl_{s}", KD, P, dt=F32R) for s in ("hi", "lo"))
        w1_hi, w1_lo = (sb(f"w1_{s}", KD, F1, dt=F32R) for s in ("hi", "lo"))
        w2_hi, w2_lo = (sb(f"w2_{s}", M1, D, dt=F32R) for s in ("hi", "lo"))
        wo_hi, wo_lo = (sb(f"wo_{s}", KD, D, dt=F32R) for s in ("hi", "lo"))
        wz = sb("wz", D, dt=F32R)
        wu = sb("wu", FH, dt=F32R)
        tern_fc = sb("tern_fc", KD, FH, dt=F32R)
        tern_pj = sb("tern_pj", MH, D, dt=F32R)
        ident, mask, pair_mask = sb("ident", P), sb("mask", P), sb("pair_mask", P)
        vg_bias, b2_row, pj_scale_row = sb("vg_bias", 2 * D), sb("b2_row", D), sb("pj_scale_row", D)
        cols = sb("cols", 64)
        c_at = [0]

        def col(n):
            c_at[0] += n
            return cols[:, c_at[0] - n:c_at[0]]

        l1w, l1b, l2w, l2b, bz, b1c, rmsc = col(KD), col(KD), col(KD), col(KD), col(KD), col(M1), col(1)
        NV = c_at[0]
        gatec, qk_bias, b1_bias = col(1), col(2 * KD), col(M1)
        bz_up = col(KD)
        lb, lb_lo, sign_hi, is_lo = col(1), col(1), col(1), col(1)
        keep = sb("keep", NB)
        small = sb("small", 64)
        s_at = [0]

        def tiny(n):
            s_at[0] += n
            return small[:, s_at[0] - n:s_at[0]]

        fc_scale, fc_half, fc_nhalf, fc_g = tiny(MH), tiny(MH), tiny(MH), tiny(MH)
        pj_scale, pj_half, pj_nhalf = tiny(KD), tiny(KD), tiny(KD)
        half_neg = tiny(NT)
        pad = tiny(1)
        eps_col, eps_head = tiny(NT), tiny(H)

        x_in, x_hat, xn0 = sb("x_in", NT, D), sb("x_hat", NT, D), sb("xn0", NT, D)
        xT_hi, xT_lo = sb("xT_hi", KD, TB, dt=F32R), sb("xT_lo", KD, TB, dt=F32R)
        low = sb("low", TB, dt=F32R)
        gates = sb("gates", 3, KD, TB)
        ug, wgt, G = gates[:, 0], gates[:, 1], gates[:, 2]
        qf, kf = sb("qf", KD, TB), sb("kf", KD, TB)
        q_hi, q_lo = sb("q_hi", KD, TB, dt=F32R), sb("q_lo", KD, TB, dt=F32R)
        k_hi, k_lo = sb("k_hi", KD, TB, dt=F32R), sb("k_lo", KD, TB, dt=F32R)
        low_hi, low_f = k_hi[:, 1], kf[:, 1]
        vg = sb("vg", NT, 2 * D)
        v_hi, v_lo = sb("v_hi", NT, D, dt=F32R), sb("v_lo", NT, D, dt=F32R)
        sgm = sb("sgm", NT, D)
        kt_hi, kt_lo = sb("kt_hi", D, dt=F32R), sb("kt_lo", D, dt=F32R)
        a_f = sb("a_f", 2, KD, P)
        a_hi, a_lo = sb("a_hi", 2, KD, P, dt=F32R), sb("a_lo", 2, KD, P, dt=F32R)
        y1, y2 = sb("y1", D), sb("y2", D)
        y_hi, y_lo = sb("y_hi", KD, P, dt=F32R), sb("y_lo", KD, P, dt=F32R)
        x1, xn2 = sb("x1", NT, D), sb("xn2", D)
        x2_hi, x2_lo = sb("x2_hi", KD, TB, dt=F32R), sb("x2_lo", KD, TB, dt=F32R)
        ring_f = sb("ring_f", 2, 2, TB)
        ring_hi, ring_lo = sb("ring_hi", 2, TB, dt=F32R), sb("ring_lo", 2, TB, dt=F32R)
        S, Sd, Sr, kv = sb("S", KD, P), sb("Sd", KD, P), sb("Sr", KD, P), sb("kv", KD, P)
        Sr_hi, Sr_lo = sb("Sr_hi", KD, P, dt=F32R), sb("Sr_lo", KD, P, dt=F32R)
        ffn, x_res = sb("ffn", NT, D), sb("x_res", NT, D)
        bn, mv = sb("bn", NT, 6), sb("mv", NT, 2)
        bn2, mv2, st2 = sb("bn2", 6), sb("mv2", 2), sb("st2", 2)
        st = sb("st", 8, NT)
        rr_c = sb("rr_c", NT)
        dec_r, dec_t = sb("dec_r", KD, NT), sb("dec_t", KD, NT)
        ss, ro = sb("ss", H), sb("ro", 2, H)
        mean = mv[:, :, 0]
        var = mv[:, :, 1]

        def pb(name, *shape):
            return ctx.enter_context(nc.psum_tensor(name, [P, *shape], F32))

        ring = [pb(f"ring{i}", TB) for i in range(RING)]
        acc = [pb(f"acc{i}", 2, D) for i in range(2)]
        okv = pb("okv", 2, KD, P)
        both = pb("both", 2, 2, KD, P)
        scores = both[:, :, 0]
        proj = both[:, 0, 1]
        turn = both[:, 1, 1]

        names = """ld_qkvg ld_small ld_fc ld_pj ld_w1 ld_w2 ld_wo ld_low zeroed ident_ok
            p_masks p_const bias_b bias_mm bias_ok fold1 fold_qk fold_vg fold_w1 fold_w2 fold_wo
            w_hi w_ready fc_s fc_s2 fc_a fc_t pj_s pj_s2 pj_a pj_t tp_full tp_free u_t u_tc m_mm
            m_f m_hi m_rep l_vt l_f l_w lb_mm lb_ok z_w cols_mm cols_ok w_cst
            x_dma res_dma out_dma bn_ok mv_ok ln_a ln_b ln_c ln_d ln_e ln_f ln_g xh xn_ok
            T_full x_hi x_lo L_full l_ev p_ready Z_full z_u z_w2 z_e z_l g_sc g_fin g_rel e_p e_m
            e_r dk dec_ok Q_full q_f qs_hi qs_lo K_full k_f ks_hi ks_lo VG_full vg_f vs_hi vs_lo
            g_u g_s1 g_s2 g_s3 g_sil kts_hi kts_lo SC_full a_m as_hi as_lo
            sr_f sd_f srs_hi srs_lo s_new KV_full o_sq o_ss o_t o_r y_1 y_2 kv_ev
            YT_full ys_hi ys_lo WO_full x_1 x1_bn x1_mv x1_t x1_r xn2_f x1_b XT_full x2s_hi
            x2s_lo FC_full fc_act fc_hi fc_h fc_lo PJ_full f_f f_u f_1 f_2 f_3 f_g
            W1_full w_u w_l ws_hi w_h w_lo W2_full s_f s_g out_ok""".split()
        s = {n: sem(n) for n in names}

        FREED = {"T": "x_lo", "L": "l_ev", "Z": "z_w2", "Q": "q_f", "K": "k_f", "VG": "vg_f",
                 "W1": "w_u", "FC": "fc_act", "SC": "a_m", "WO": "x_1", "YT": "ys_lo", "XT": "x2s_lo"}

        block = ctx.enter_context(nc.Block())

        def at(n, per, j):
            return n * per + j

        def wait_tenant(pe, stages, stage, n, kinds, banks):
            bank, (kind, j), before = tenant(stages, stage, kinds, banks)
            m = n - 1 if kind in BACK_STAGES else n
            if before:
                m = m - 1
                if isinstance(m, int) and m < 0:
                    return bank
            pe.wait_ge(s[FREED[kind]], at(m, PER[kind], j + 1))
            return bank

        def tile4(bank_pair, t):
            return bank_pair[t // 2][:, t % 2, :]

        @block.sync
        def _(sp):
            def two(dst, w, name):
                sp.dma_start(dst, w.rearrange("(k p) n -> p k n", p=P)).then_inc(s[name], 16)

            sp.dma_start(x_in[:, :, :], x_blocks[0]).then_inc(s["x_dma"], 16)
            two(qf[:, :, 0:D], wq, "ld_qkvg")
            two(qf[:, :, D:2 * D], wk, "ld_qkvg")
            two(kf[:, :, 0:D], wv, "ld_qkvg")
            two(kf[:, :, D:2 * D], wg, "ld_qkvg")
            sp.dma_start(vg[:, :, :].rearrange("p t (a d) -> p (t a) d", a=2),
                         w_fc.rearrange("(m p) d -> p m d", p=P)).then_inc(s["ld_fc"], 16)
            sp.dma_start(ring_f[:, :, :, :].rearrange("p a b n -> p a (b n)"),
                         w_proj.rearrange("(m p) n -> p m n", p=P)).then_inc(s["ld_pj"], 16)
            gflat = gates[:, :, :, :].rearrange("p a b n -> p (a b n)")
            two(gflat[:, 0:KD * F1].rearrange("p (k n) -> p k n", k=KD), w1, "ld_w1")
            two(gflat[:, KD * F1:2 * KD * F1].rearrange("p (k n) -> p k n", k=M1), w2, "ld_w2")
            two(x1[:, 0:2, :], wo, "ld_wo")

            def step(n, front, back):
                if front:
                    nxt = x_blocks[(n + 1) % NB] if isinstance(n, int) else \
                        x_blocks[sp.snap(n + 1)]
                    sp.wait_ge(s["xh"], at(n, 1, 1))
                    sp.dma_start(x_in[:, :, :], nxt).then_inc(s["x_dma"], 16)
                if back:
                    m = n - 1
                    dst = out_blocks[m] if isinstance(n, int) else out_blocks[sp.snap(n - 1)]
                    src = x_blocks[m] if isinstance(n, int) else x_blocks[sp.snap(n - 1)]
                    if not isinstance(n, int) or m >= 1:
                        sp.wait_ge(s["out_dma"], m * 16)
                    sp.dma_start(x_res[:, :, :], src).then_inc(s["res_dma"], 16)
                    sp.wait_ge(s["out_ok"], at(m, 1, 1))
                    sp.dma_start(dst, x_res[:, :, :]).then_inc(s["out_dma"], 16)

            sp.wait_ge(s["w_ready"], 1)
            step(0, True, False)
            step(1, True, True)
            with sp.Fori(2, NB - 1) as n:
                step(n, True, True)
            step(NB - 1, True, True)
            step(NB, False, True)
            sp.wait_ge(s["out_dma"], NB * 16)
            sp.wait_ge(s["x_dma"], (NB + 1) * 16)

        @block.gpsimd
        def _(gp):
            gp.memset(ident[:, :], 0.0).then_inc(s["p_masks"], 1)
            gp.memset(mask[:, :], 1.0).then_inc(s["p_masks"], 1)
            gp.memset(sgm[:, :, :], 0.0).then_inc(s["zeroed"], 1)
            gp.memset(ffn[:, :, :], 0.0).then_inc(s["zeroed"], 1)
            gp.wait_ge(s["p_masks"], 2)
            gp.affine_select(out=ident[:, :], in_=ident[:, :], compare_op=ALU.not_equal, fill=1.0,
                             base=0, pattern=[[-1, P]], channel_multiplier=1).then_inc(s["ident_ok"], 1)
            gp.affine_select(out=mask[:, :], in_=mask[:, :], compare_op=ALU.is_ge, fill=0.0,
                             base=0, pattern=[[1, P]], channel_multiplier=-1).then_inc(s["ident_ok"], 1)
            gp.memset(half_neg, -0.5)
            gp.memset(eps_col, EPS)
            gp.memset(eps_head, EPS * DK).then_inc(s["p_const"], 1)
            gp.memset(S[:, :, :], 0.0).then_inc(s["s_new"], 1)

            def pow_chain_in(n):
                gp.wait_ge(s["mv_ok"], at(n, 1, 1))
                gp.tensor_tensor(st[:, 0, :], var, eps_col, ALU.add).then_inc(s["ln_a"], 1)
                gp.wait_ge(s["ln_a"], at(n, 1, 1))
                gp.tensor_tensor(st[:, 1, :], st[:, 0, :], half_neg, ALU.pow).then_inc(s["ln_b"], 1)
                gp.wait_ge(s["ln_b"], at(n, 1, 1))
                gp.tensor_tensor(st[:, 2, :], var, st[:, 1, :], ALU.mult).then_inc(s["ln_c"], 1)
                gp.wait_ge(s["ln_c"], at(n, 1, 1))
                gp.tensor_tensor(st[:, 3, :], st[:, 2, :], st[:, 1, :], ALU.mult).then_inc(s["ln_d"], 1)
                gp.wait_ge(s["ln_d"], at(n, 1, 1))
                gp.tensor_tensor(st[:, 4, :], st[:, 3, :], eps_col, ALU.add).then_inc(s["ln_e"], 1)
                gp.wait_ge(s["ln_e"], at(n, 1, 1))
                gp.tensor_tensor(st[:, 5, :], st[:, 4, :], half_neg, ALU.pow).then_inc(s["ln_f"], 1)
                gp.wait_ge(s["ln_f"], at(n, 1, 1))
                gp.tensor_tensor(st[:, 6, :], st[:, 5, :], st[:, 1, :], ALU.mult).then_inc(s["ln_g"], 1)
                gp.tensor_tensor(st[:, 7, :], st[:, 5, :], st[:, 4, :], ALU.mult).then_inc(s["ln_g"], 1)

            gp.wait_ge(s["p_const"], 1)
            pow_chain_in(0)

            def step(n, front, back):
                b = n - 1
                for kind, j in stages_of(front, back):
                    if kind == "LN":
                        pow_chain_in(n + 1)
                    elif kind == "Q":
                        gp.wait_ge(s["qs_hi"], at(n, KD, j + 1))
                        gp.tensor_tensor(q_lo[:, j, :], qf[:, j, :], f(q_hi[:, j, :]),
                                         ALU.subtract).then_inc(s["qs_lo"], 1)
                    elif kind == "K":
                        gp.wait_ge(s["ks_hi"], at(n, KD, j + 1))
                        gp.tensor_tensor(k_lo[:, j, :], kf[:, j, :], f(k_hi[:, j, :]),
                                         ALU.subtract).then_inc(s["ks_lo"], 1)
                    elif kind == "VG":
                        gp.wait_ge(s["vs_hi"], at(n, NT, j + 1))
                        gp.tensor_tensor(v_lo[:, j, :], vg[:, j, 0:D], f(v_hi[:, j, :]),
                                         ALU.subtract).then_inc(s["vs_lo"], 1)
                    elif kind == "SL":
                        two = slice(2 * j, 2 * j + 2)
                        gp.wait_ge(s["g_s3"], at(n, 2, j + 1))
                        gp.wait_ge(s["vs_lo"], at(n, NT, 2 * j + 2))
                        gp.tensor_tensor(vg[:, two, 0:D], vg[:, two, D:2 * D], sgm[:, two, :],
                                         ALU.mult).then_inc(s["g_sil"], 1)
                    elif kind == "SC":
                        gp.wait_ge(s["as_hi"], at(n, NT, j + 1))
                        gp.tensor_tensor(a_lo[:, :, :, :], a_f[:, :, :, :], f(a_hi[:, :, :, :]),
                                         ALU.subtract).then_inc(s["as_lo"], 1)
                    elif kind == "ST":
                        gp.wait_ge(s["s_new"], at(n, NT, j + 1))
                        if j == 0:
                            gp.wait_ge(s["dec_ok"], at(n, 1, 1))
                        gp.tensor_tensor(Sr[:, :, :], S[:, :, :],
                                         dec_r[:, :, j:j + 1].broadcast_to([P, KD, P]),
                                         ALU.mult).then_inc(s["sr_f"], 1)
                        gp.tensor_tensor(Sd[:, :, :], S[:, :, :],
                                         dec_t[:, :, j:j + 1].broadcast_to([P, KD, P]),
                                         ALU.mult).then_inc(s["sd_f"], 1)
                        gp.wait_ge(s["srs_hi"], at(n, NT, j + 1))
                        gp.tensor_tensor(Sr_lo[:, :, :], Sr[:, :, :], f(Sr_hi[:, :, :]),
                                         ALU.subtract).then_inc(s["srs_lo"], 1)
                    elif kind == "AV":
                        gp.wait_ge(s["o_ss"], at(n, NT, j + 1))
                        gp.tensor_tensor(ro[:, 0, :], ss[:, :], eps_head, ALU.add).then_inc(s["o_t"], 1)
                        gp.wait_ge(s["o_t"], at(n, NT, j + 1))
                        gp.tensor_tensor(ro[:, 1, :], ro[:, 0, :], half_neg, ALU.pow).then_inc(s["o_r"], 1)
                        gp.wait_ge(s["y_1"], at(n, NT, j + 1))
                        if j % 2 == 0:
                            gp.wait_ge(s["g_sil"], at(n, 2, j // 2 + 1))
                        gp.tensor_tensor(y2[:, :], y1[:, :], vg[:, j, 0:D], ALU.mult).then_inc(s["y_2"], 1)
                    elif kind == "WO":
                        gp.wait_ge(s["x1_mv"], at(n, NT, j + 1))
                        gp.tensor_tensor(st2[:, 0:1], mv2[:, 1:2], eps_col[:, 0:1], ALU.add).then_inc(s["x1_t"], 1)
                        gp.wait_ge(s["x1_t"], at(n, NT, j + 1))
                        gp.tensor_tensor(st2[:, 1:2], st2[:, 0:1], half_neg[:, 0:1],
                                         ALU.pow).then_inc(s["x1_r"], 1)
                        gp.wait_ge(s["xn2_f"], at(n, NT, j + 1))
                        gp.tensor_tensor(x1[:, j, :], x1[:, j, :], b2_row[:, :],
                                         ALU.add).then_inc(s["x1_b"], 1)
                    elif kind == "FC":
                        gp.wait_ge(s["fc_act"], at(n, MH, j + 1))
                        gp.tensor_tensor(ring_f[:, j % 2, 1, :], ring_f[:, j % 2, 0, :],
                                         ring_f[:, j % 2, 0, :], ALU.mult).then_inc(s["fc_h"], 1)
                    elif kind == "PG":
                        gp.wait_ge(s["f_3"], at(b, 1, 1))
                        gp.tensor_tensor(ffn[:, :, :], ffn[:, :, :], sgm[:, :, :],
                                         ALU.mult).then_inc(s["f_g"], 1)
                    elif kind == "W1":
                        gp.wait_ge(s["w_l"], at(b, M1, j + 1))
                        gp.tensor_tensor(ring_f[:, j % 2, 1, :], ring_f[:, j % 2, 0, :],
                                         ring_f[:, j % 2, 0, :], ALU.mult).then_inc(s["w_h"], 1)
                    elif kind == "OUT":
                        gp.wait_ge(s["s_f"], at(b, NT, NT))
                        gp.wait_ge(s["f_g"], at(b, 1, 1))
                        gp.tensor_tensor(x1[:, :, :], x1[:, :, :], ffn[:, :, :],
                                         ALU.mult).then_inc(s["s_g"], 1)
                        gp.wait_ge(s["s_g"], at(b, 1, 1))
                        gp.wait_ge(s["res_dma"], at(b, 16, 16))
                        gp.tensor_tensor(x_res[:, :, :], x1[:, :, :], x_res[:, :, :],
                                         ALU.add).then_inc(s["out_ok"], 1)

            step(0, True, False)
            with gp.Fori(1, NB) as n:
                step(n, True, True)
            step(NB, False, True)

        @block.scalar
        def _(ac):
            ac.preload_act_table_set("natural_log_exp_and_others")
            vec = xn0[:, 2, P:2 * P]
            row, small_loads = 0, []
            for w, k in ((ln1_w, KD), (ln1_b, KD), (ln2_w, KD), (ln2_b, KD), (bgk2, KD), (b1, M1)):
                small_loads.append((vec[row:row + k, :], w.rearrange("(k p) -> k p", p=P)))
                row += k
            small_loads += [(vec[row:row + 1, e * DK:(e + 1) * DK], rms_w.rearrange("(a n) -> a n", a=1))
                            for e in range(2)]
            small_loads += [
                (gatec, gate.rearrange("(a n) -> a n", a=1).broadcast_to([P, 1])),
                (b2_row[:, :], b2.rearrange("(a n) -> a n", a=1).broadcast_to([P, D])),
                (xn0[:, 0, 0:KD * LOW].rearrange("p (k r) -> p k r", k=KD), wgk1.rearrange("(k p) r -> p k r", p=P)),
                (xn0[:, 1, 0:MH * LOW].rearrange("p (m r) -> p m r", m=MH), u.rearrange("(m p) r -> p m r", p=P)),
                (xn0[0:LOW, 2, 0:LOW], fast_b),
            ]
            for dst, src in small_loads:
                ac.dma_start(dst, src).then_inc(s["ld_small"], 16)
            ac.wait_ge(s["zeroed"], 2)
            for g in range(4):
                ac.dma_start(sgm[32 * g + LOW:32 * g + 2 * LOW, 0, :], v).then_inc(s["ld_low"], 16)
                ac.dma_start(sgm[32 * g:32 * g + LOW, 1, :], wgk2).then_inc(s["ld_low"], 16)

            gflat = gates[:, :, :, :].rearrange("p a b n -> p (a b n)")
            w1_st = gflat[:, 0:KD * F1].rearrange("p (k n) -> p k n", k=KD)
            w2_st = gflat[:, KD * F1:2 * KD * F1].rearrange("p (k n) -> p k n", k=M1)

            ac.wait_ge(s["l_w"], 1)
            ac.activation(wl_hi[:, :, :], xn0[:, 3, :].rearrange("p (k n) -> p k n", k=KD), ACT.Copy)\
              .then_inc(s["w_hi"], 1)
            ac.wait_ge(s["fold_qk"], 1)
            ac.activation(wqk_hi[:, :, :], qf[:, :, :], ACT.Copy).then_inc(s["w_hi"], 1)
            ac.wait_ge(s["fold_vg"], 1)
            ac.activation(wvg_hi[:, :, :], kf[:, :, :], ACT.Copy).then_inc(s["w_hi"], 1)
            ac.wait_ge(s["fold_wo"], 1)
            ac.activation(wo_hi[:, :, :], x1[:, 0:2, :], ACT.Copy).then_inc(s["w_hi"], 1)
            ac.wait_ge(s["fold_w1"], 1)
            ac.activation(w1_hi[:, :, :], w1_st, ACT.Copy).then_inc(s["w_hi"], 1)
            ac.wait_ge(s["ld_w2"], 16)
            ac.activation(w2_hi[:, :, :], w2_st, ACT.Copy).then_inc(s["w_hi"], 1)
            for i in range(8):
                ac.wait_ge(s["tp_full"], i + 1)
                if i < 4:
                    k, half = i // 2, i % 2
                    dst = tern_fc[:, k, half * TB:(half + 1) * TB]
                else:
                    dst = tern_pj[:, 2 * (i - 4):2 * (i - 4) + 2, :].rearrange("p a b -> p (a b)")
                ac.activation(dst, ring[i % RING][:, :], ACT.Copy).then_inc(s["tp_free"], 1)
            for i in range(2):
                ac.wait_ge(s["tp_full"], 9 + i)
                ac.activation(wu[:, i * TB:(i + 1) * TB], ring[(8 + i) % RING][:, :], ACT.Copy)\
                  .then_inc(s["tp_free"], 1)

            def log_sigmoid_exp(n, per, j, buf, ready, first, second, third):
                ac.wait_ge(s[ready], at(n, per, j))
                ac.activation(buf, buf, ACT.Exp, scale=-1.0).then_inc(s[first], 1)
                ac.wait_ge(s[first], at(n, per, j))
                ac.activation(buf, buf, ACT.Ln, bias=1.0).then_inc(s[second], 1)
                ac.wait_ge(s[second], at(n, per, j))
                ac.activation(buf, buf, ACT.Exp, scale=-1.0).then_inc(s[third], 1)

            def step(n, front, back):
                b = n - 1
                stages = stages_of(front, back)

                def bank(kind, j):
                    return ring[tenant(stages, (kind, j), RING_STAGES, RING)[0]][:, :]

                for kind, j in stages:
                    if kind == "T":
                        ac.wait_ge(s["T_full"], at(n, KD, j + 1))
                        ac.activation(xT_hi[:, j, :], bank(kind, j), ACT.Copy).then_inc(s["x_hi"], 1)
                    elif kind == "L":
                        ac.wait_ge(s["L_full"], at(n, 1, 1))
                        ac.activation(low_hi[:, :], bank(kind, j), ACT.Identity, bias=lb)
                        ac.activation(low_f, bank(kind, j), ACT.Identity, bias=lb_lo, scale=is_lo)\
                          .then_inc(s["l_ev"], 1)
                    elif kind == "Z":
                        ac.wait_ge(s["z_u"], at(n, KD, j + 1))
                        ac.activation(ug[:, j, :], ug[:, j, :], ACT.Exp, scale=-1.0).then_inc(s["z_e"], 1)
                        ac.wait_ge(s["z_e"], at(n, KD, j + 1))
                        ac.activation(ug[:, j, :], ug[:, j, :], ACT.Ln, bias=1.0).then_inc(s["z_l"], 1)
                    elif kind == "SCAN":
                        ac.wait_ge(s["g_rel"], at(n, KD, j + 1))
                        ac.activation(ug[:, j, :], wgt[:, j, :], ACT.Exp, scale=1.0 / GLN)\
                          .then_inc(s["e_p"], 1)
                        ac.activation(dec_r[:, j, :],
                                      G[:, j, :].rearrange("p (c t) -> p c t", t=P)[:, :, MID],
                                      ACT.Exp, scale=1.0 / GLN).then_inc(s["e_r"], 1)
                        ac.wait_ge(s["e_p"], at(n, KD, j + 1))
                        ac.activation(wgt[:, j, :], wgt[:, j, :], ACT.Exp, scale=-1.0 / GLN)\
                          .then_inc(s["e_m"], 1)
                    elif kind == "Q":
                        ac.wait_ge(s["q_f"], at(n, KD, j + 1))
                        ac.activation(q_hi[:, j, :], qf[:, j, :], ACT.Copy).then_inc(s["qs_hi"], 1)
                    elif kind == "K":
                        ac.wait_ge(s["k_f"], at(n, KD, j + 1))
                        ac.activation(k_hi[:, j, :], kf[:, j, :], ACT.Copy).then_inc(s["ks_hi"], 1)
                    elif kind == "VG":
                        ac.wait_ge(s["vg_f"], at(n, NT, j + 1))
                        ac.activation(v_hi[:, j, :], vg[:, j, 0:D], ACT.Copy).then_inc(s["vs_hi"], 1)
                    elif kind == "SIG":
                        log_sigmoid_exp(n, 2, j + 1, sgm[:, 2 * j:2 * j + 2, :], "g_u", "g_s1",
                                        "g_s2", "g_s3")
                    elif kind == "SC":
                        ac.wait_ge(s["SC_full"], at(n, NT, j + 1))
                        ac.activation(kt_hi[:, :], turn.rearrange("p a b -> p (a b)"),
                                      ACT.Copy).then_inc(s["kts_hi"], 1)
                        ac.wait_ge(s["a_m"], at(n, NT, j + 1))
                        ac.activation(a_hi[:, :, :, :], a_f[:, :, :, :], ACT.Copy).then_inc(s["as_hi"], 1)
                    elif kind == "ST":
                        ac.wait_ge(s["sr_f"], at(n, NT, j + 1))
                        ac.activation(Sr_hi[:, :, :], Sr[:, :, :], ACT.Copy).then_inc(s["srs_hi"], 1)
                    elif kind == "AV":
                        ac.wait_ge(s["KV_full"], at(n, NT, j + 1))
                        if isinstance(n, int) and n == 0 and j == 0:
                            pass
                        else:
                            ac.wait_ge(s["y_2"], at(n, NT, j))
                        ac.activation(y1[:, :], okv[:, 0, :, :].rearrange("p a b -> p (a b)"),
                                      ACT.Square).then_inc(s["o_sq"], 1)
                    elif kind == "YT":
                        ac.wait_ge(s["YT_full"], at(n, NT, j + 1))
                        ac.activation(y_hi[:, :, :], turn, ACT.Copy).then_inc(s["ys_hi"], 1)
                    elif kind == "XT":
                        ac.wait_ge(s["XT_full"], at(n, NT, j + 1))
                        ac.activation(x2_hi[:, :, j * P:(j + 1) * P], turn, ACT.Copy)\
                          .then_inc(s["x2s_hi"], 1)
                    elif kind == "FC":
                        ac.wait_ge(s["FC_full"], at(n, MH, j + 1))
                        ac.activation(ring_f[:, j % 2, 0, :], bank(kind, j), ACT.Relu,
                                      scale=fc_scale[:, j:j + 1]).then_inc(s["fc_act"], 1)
                        ac.wait_ge(s["fc_act"], at(n, MH, j + 1))
                        ac.activation(ring_hi[:, j % 2, :], ring_f[:, j % 2, 0, :], ACT.Square)\
                          .then_inc(s["fc_hi"], 1)
                    elif kind == "PU":
                        log_sigmoid_exp(b, 1, 1, sgm[:, :, :], "f_u", "f_1", "f_2", "f_3")
                    elif kind == "W1":
                        ac.wait_ge(s["W1_full"], at(b, M1, j + 1))
                        ac.activation(ring_f[:, j % 2, 0, :], bank(kind, j), ACT.Identity,
                                      bias=b1_bias[:, j:j + 1]).then_inc(s["w_u"], 1)
                        ac.wait_ge(s["w_l"], at(b, M1, j + 1))
                        ac.activation(ring_hi[:, j % 2, :], ring_f[:, j % 2, 0, :], ACT.Square)\
                          .then_inc(s["ws_hi"], 1)

            ac.wait_ge(s["w_ready"], 1)
            step(0, True, False)
            with ac.Fori(1, NB) as n:
                step(n, True, True)
            step(NB, False, True)

        @block.vector
        def _(ve):
            own = [0]

            def layernorm_in(n):
                ve.wait_ge(s["x_dma"], at(n, 16, 16))
                for t in range(NT):
                    ve.bn_stats(bn[:, t, :], x_in[:, t, :]).then_inc(s["bn_ok"], 1)
                ve.wait_ge(s["bn_ok"], at(n, NT, NT))
                ve.memset(pad, 0.0)
                for t in range(NT):
                    i = ve.bn_aggr(mv[:, t, :], bn[:, t, :])
                i.then_inc(s["mv_ok"], 1)
                ve.wait_ge(s["ln_g"], at(n, 2, 2))
                for t in range(NT):
                    i = ve.tensor_scalar(x_hat[:, t, :], x_in[:, t, :], mv[:, t, 0:1],
                                         st[:, 6, t:t + 1], ALU.subtract, ALU.mult)
                i.then_inc(s["xh"], 1)

            for q in range(4):
                rows = slice(32 * q, 32 * q + 32)
                ve.memset(sign_hi[rows, :], -1.0 if q % 2 else 1.0)
                ve.memset(is_lo[rows, :], float(q % 2))
            ve.memset(pair_mask[:, :], 0.0).then_inc(s["fold1"], 1)
            ve.memset(keep[:, :], 1.0).then_inc(s["fold1"], 1)
            ve.wait_ge(s["fold1"], 2)
            ve.memset(pair_mask[0:DK, 0:DK], 1.0)
            ve.memset(pair_mask[DK:P, DK:P], 1.0)
            ve.memset(keep[:, :].rearrange("p (b m) -> p b m", b=B)[:, :, 0], 0.0)\
              .then_inc(s["w_cst"], 1)
            layernorm_in(0)

            ve.wait_ge(s["cols_mm"], 1)
            ve.tensor_copy(cols[:, 0:NV], proj[:, 0, 0:NV]).then_inc(s["cols_ok"], 1)
            ve.wait_ge(s["cols_ok"], 1)

            ve.wait_ge(s["ld_small"], 13 * 16)
            g1 = xn0[:, 0, 0:KD * LOW].rearrange("p (k r) -> p k r", k=KD)
            wl_st = xn0[:, 3, :].rearrange("p (k n) -> p k n", k=KD)
            lraw = ffn[:, 2, :].rearrange("p (k n) -> p k n", k=KD)
            ve.wait_ge(s["l_vt"], 1)
            ve.wait_ge(s["zeroed"], 2)
            ve.tensor_copy(wl_st, turn).then_inc(s["l_f"], 1)
            ve.wait_ge(s["l_f"], 1)
            for k in range(KD):
                for q in range(4):
                    ve.tensor_scalar(wl_st[:, k, 32 * q:32 * q + LOW], g1[:, k, :], l1w[:, k:k + 1],
                                     None, ALU.mult)
                    i = ve.tensor_copy(lraw[:, k, 32 * q:32 * q + LOW], g1[:, k, :])
            i.then_inc(s["l_w"], 1)
            for k in range(KD):
                i = ve.tensor_scalar(x_res[:, k, 0:P], ident[:, :], 0.0, l1b[:, k:k + 1], ALU.mult,
                                     ALU.add)
            i.then_inc(s["bias_b"], 1)

            ve.wait_ge(s["bias_mm"], 1)
            ve.tensor_copy(vg_bias[:, :], okv[:, :, :, :].rearrange("p a b c -> p (a b c)")).then_inc(s["bias_ok"], 1)
            ve.tensor_scalar(qk_bias[:, 0:KD], proj[:, 0, 0:KD], DK ** -0.5, None, ALU.mult)
            ve.tensor_copy(qk_bias[:, KD:2 * KD], proj[:, 0, KD:2 * KD]).then_inc(s["bias_ok"], 1)
            for k in range(KD):
                ve.tensor_scalar(qf[:, k, 0:D], qf[:, k, 0:D], l1w[:, k:k + 1], DK ** -0.5, ALU.mult, ALU.mult)
                i = ve.tensor_scalar(qf[:, k, D:2 * D], qf[:, k, D:2 * D], l1w[:, k:k + 1], None, ALU.mult)
            i.then_inc(s["fold_qk"], 1)
            for k in range(KD):
                i = ve.tensor_scalar(kf[:, k, :], kf[:, k, :], l1w[:, k:k + 1], None, ALU.mult)
            i.then_inc(s["fold_vg"], 1)
            ve.wait_ge(s["ld_wo"], 16)
            ve.tensor_scalar(x1[:, 0:2, :], x1[:, 0:2, :], rmsc, DK ** 0.5, ALU.mult, ALU.mult).then_inc(s["fold_wo"], 1)
            ve.wait_ge(s["lb_mm"], 1)
            ve.tensor_copy(lb, proj[:, 1, 0:1]).then_inc(s["lb_ok"], 1)
            ve.wait_ge(s["lb_ok"], 1)
            ve.tensor_tensor(lb_lo, lb, is_lo, ALU.mult)
            ve.tensor_scalar(bz_up, bz, CLAMP, None, ALU.add)
            ve.wait_ge(s["ld_low"], 8 * 16)
            ve.tensor_copy(low_hi[:, 0:D], sgm[:, 1, :]).then_inc(s["z_w"], 1)
            ve.wait_ge(s["z_w"], 1)
            ve.tensor_copy(wz[0:64, :], f(low_hi[0:64, 0:D]))
            ve.tensor_tensor(wz[64:P, :], sgm[64:P, 1, :], f(low_hi[64:P, 0:D]), ALU.subtract)

            gflat = gates[:, :, :, :].rearrange("p a b n -> p (a b n)")
            w1_st = gflat[:, 0:KD * F1].rearrange("p (k n) -> p k n", k=KD)
            w2_st = gflat[:, KD * F1:2 * KD * F1].rearrange("p (k n) -> p k n", k=M1)
            ve.wait_ge(s["bias_mm"], 2)
            ve.tensor_tensor(b1_bias, proj[:, 1, 8:8 + M1], b1c, ALU.add).then_inc(s["bias_ok"], 1)
            for k in range(KD):
                i = ve.tensor_scalar(w1_st[:, k, :], w1_st[:, k, :], l2w[:, k:k + 1], None, ALU.mult)
            i.then_inc(s["fold_w1"], 1)

            for i, (lo, w, hi) in enumerate((
                    (wl_lo[:, :, :], wl_st, wl_hi[:, :, :]), (wqk_lo[:, :, :], qf[:, :, :], wqk_hi[:, :, :]),
                    (wvg_lo[:, :, :], kf[:, :, :], wvg_hi[:, :, :]),
                    (wo_lo[:, :, :], x1[:, 0:2, :], wo_hi[:, :, :]), (w1_lo[:, :, :], w1_st, w1_hi[:, :, :]),
                    (w2_lo[:, :, :], w2_st, w2_hi[:, :, :]))):
                ve.wait_ge(s["w_hi"], i + 1)
                ve.tensor_tensor(lo, w, f(hi), ALU.subtract)

            wfc = vg[:, :, :].rearrange("p t (a d) -> p (t a) d", a=2)
            ve.wait_ge(s["ld_fc"], 16)
            ve.tensor_reduce(fc_half, wfc, AX.X, ALU.add, apply_absolute_value=True).then_inc(s["fc_s"], 1)
            ve.wait_ge(s["fc_s"], 1)
            ve.tensor_scalar(fc_scale, fc_half, 1.0 / D, EPS, ALU.mult, ALU.max).then_inc(s["fc_s"], 1)
            ve.wait_ge(s["fc_s"], 2)
            ve.tensor_scalar(fc_half, fc_scale, 0.5, None, ALU.mult)
            ve.tensor_scalar(fc_nhalf, fc_scale, -0.5, None, ALU.mult)
            ve.reciprocal(fc_g, fc_scale).then_inc(s["fc_s"], 1)
            ve.wait_ge(s["fc_s"], 3)
            ve.tensor_scalar(fc_g, fc_g, gatec, None, ALU.mult).then_inc(s["fc_s"], 1)
            for m in range(MH):
                if m % 4 == 0 and m:
                    ve.wait_ge(s["fc_t"], m)
                neg = x_in[:, m % 4, :]
                ve.tensor_scalar(neg, wfc[:, m, :], fc_nhalf[:, m:m + 1], None, ALU.is_lt)\
                  .then_inc(s["fc_a"], 1)
                ve.wait_ge(s["fc_a"], m + 1)
                ve.scalar_tensor_tensor(wfc[:, m, :], wfc[:, m, :], fc_half[:, m:m + 1], neg,
                                        ALU.is_gt, ALU.subtract).then_inc(s["fc_t"], 1)
            wpj = ring_f[:, :, :, :].rearrange("p a b n -> p a (b n)")
            ve.wait_ge(s["ld_pj"], 16)
            ve.tensor_reduce(pj_half, wpj, AX.X, ALU.add, apply_absolute_value=True).then_inc(s["pj_s"], 1)
            ve.wait_ge(s["pj_s"], 1)
            ve.tensor_scalar(pj_scale, pj_half, 1.0 / FH, EPS, ALU.mult, ALU.max).then_inc(s["pj_s"], 1)
            ve.wait_ge(s["pj_s"], 2)
            ve.tensor_scalar(pj_half, pj_scale, 0.5, None, ALU.mult)
            ve.tensor_scalar(pj_nhalf, pj_scale, -0.5, None, ALU.mult).then_inc(s["pj_s"], 1)
            ve.wait_ge(s["pj_s"], 3)
            ve.wait_ge(s["fc_t"], MH)
            negp = x_in.rearrange("p t d -> p (t d)")
            for m in range(KD):
                if m:
                    ve.wait_ge(s["pj_t"], m)
                ve.tensor_scalar(negp, wpj[:, m, :], pj_nhalf[:, m:m + 1], None, ALU.is_lt)\
                  .then_inc(s["pj_a"], 1)
                ve.wait_ge(s["pj_a"], m + 1)
                ve.scalar_tensor_tensor(wpj[:, m, :], wpj[:, m, :], pj_half[:, m:m + 1], negp,
                                        ALU.is_gt, ALU.subtract).then_inc(s["pj_t"], 1)
            for m in range(KD):
                i = ve.tensor_scalar(x_res[:, 2 + m, 0:P], ident[:, :], 0.0, pj_scale[:, m:m + 1],
                                     ALU.mult, ALU.add)
            i.then_inc(s["pj_s2"], 1)
            ve.wait_ge(s["u_t"], 1)
            uT = x_in[0:LOW, :, :].rearrange("p t d -> p (t d)")
            ve.wait_ge(s["pj_t"], KD)
            for i in range(2):
                j = ve.tensor_copy(uT[:, i * TB:(i + 1) * TB], acc[i][0:LOW, :, :].rearrange("p a b -> p (a b)"))
            j.then_inc(s["u_tc"], 1)
            ve.wait_ge(s["m_mm"], 1)
            mf = xn0[:, 0, 0:MH * LOW].rearrange("p (m r) -> p m r", m=MH)
            mh = low_hi[:, 0:MH * LOW].rearrange("p (m r) -> p m r", m=MH)
            ve.wait_ge(s["fc_s"], 4)
            ve.tensor_tensor(mf, okv[:, 0, 0, :].rearrange("p (m r) -> p m r", m=MH),
                             fc_g.rearrange("p (m a) -> p m a", a=1).broadcast_to([P, MH, LOW]), ALU.mult).then_inc(s["m_f"], 1)
            ve.wait_ge(s["m_f"], 1)
            ve.tensor_copy(mh, mf).then_inc(s["m_hi"], 1)
            ve.wait_ge(s["m_hi"], 1)
            m_rep = vg[:, :, :].rearrange("p t (a d) -> p (t a) d", a=2)[:, :, 0:P]
            ve.wait_ge(s["tp_full"], 4)
            ve.memset(m_rep, 0.0).then_inc(s["m_rep"], 1)
            ve.wait_ge(s["m_rep"], 1)
            for q in range(4):
                dst = m_rep[:, :, 32 * q + LOW:32 * q + 2 * LOW]
                if q < 2:
                    ve.tensor_copy(dst, f(mh))
                else:
                    i = ve.tensor_tensor(dst, mf, f(mh), ALU.subtract)
            i.then_inc(s["m_rep"], 1)
            ve.wait_ge(s["bias_mm"], 3)
            ve.tensor_copy(pj_scale_row[:, :], turn.rearrange("p a b -> p (a b)")).then_inc(s["bias_ok"], 1)
            ve.wait_ge(s["tp_free"], 10)
            ve.wait_ge(s["bias_ok"], 4)
            ve.engine_nop().then_inc(s["w_ready"], 1)

            def step(n, front, back):
                b = n - 1
                stages = stages_of(front, back)

                def bank(kind, j):
                    return ring[tenant(stages, (kind, j), RING_STAGES, RING)[0]][:, :]

                for kind, j in stages:
                    if kind == "LN":
                        layernorm_in(n + 1)
                    elif kind == "XN":
                        ve.tensor_copy(rr_c[:, :], st[:, 4, :])
                        for t in range(NT):
                            i = ve.tensor_scalar(xn0[:, t, :], x_hat[:, t, :], st[:, 7, t:t + 1], None,
                                                 ALU.mult)
                        i.then_inc(s["xn_ok"], 1)
                    elif kind == "T":
                        ve.wait_ge(s["x_hi"], at(n, KD, j + 1))
                        ve.tensor_tensor(xT_lo[:, j, :], bank(kind, j), f(xT_hi[:, j, :]),
                                         ALU.subtract).then_inc(s["x_lo"], 1)
                    elif kind == "L":
                        ve.wait_ge(s["l_ev"], at(n, 1, 1))
                        ve.scalar_tensor_tensor(low[:, :], f(low_hi[:, :]), sign_hi, low_f, ALU.mult,
                                                ALU.add).then_inc(s["p_ready"], 1)
                    elif kind == "Z":
                        ve.wait_ge(s["Z_full"], at(n, KD, j + 1))
                        ve.tensor_scalar(ug[:, j, :], bank(kind, j), bz[:, j:j + 1], -CLAMP, ALU.add,
                                         ALU.max).then_inc(s["z_u"], 1)
                        ve.tensor_scalar(wgt[:, j, :], bank(kind, j), bz_up[:, j:j + 1], 0.0, ALU.add,
                                         ALU.min).then_inc(s["z_w2"], 1)
                    elif kind == "SCAN":
                        ve.wait_ge(s["z_w2"], at(n, KD, j + 1))
                        ve.wait_ge(s["z_l"], at(n, KD, j + 1))
                        for c in range(NT):
                            part = slice(c * P, (c + 1) * P)
                            i = ve.tensor_tensor_scan(G[:, j, part], wgt[:, j, part], ug[:, j, part],
                                                      0.0, ALU.add, ALU.subtract)
                        i.then_inc(s["g_sc"], 1)
                        ve.wait_ge(s["g_sc"], at(n, KD, j + 1))
                        gc = G[:, j, :].rearrange("p (c t) -> p c t", t=P)
                        ve.tensor_tensor(wgt[:, j, :].rearrange("p (c t) -> p c t", t=P), gc,
                                         gc[:, :, MID:MID + 1].broadcast_to([P, NT, P]),
                                         ALU.subtract).then_inc(s["g_rel"], 1)
                        if j == KD - 1:
                            ve.wait_ge(s["e_r"], at(n, KD, KD))
                            ve.tensor_scalar(dec_r[:, :, 0], dec_r[:, :, 0],
                                             keep[:, bass.ds(n, 1)] if not isinstance(n, int)
                                             else keep[:, n:n + 1], None, ALU.mult).then_inc(s["dk"], 1)
                            ve.wait_ge(s["dk"], at(n, 1, 1))
                            ve.wait_ge(s["e_p"], at(n, KD, KD))
                            ends = ug[:, :, :].rearrange("p k (c t) -> p k c t", t=P)[:, :, :, P - 1]
                            ve.tensor_tensor(dec_t[:, :, :], dec_r[:, :, :], ends,
                                             ALU.mult).then_inc(s["dec_ok"], 1)
                    elif kind == "Q":
                        ve.wait_ge(s["Q_full"], at(n, KD, j + 1))
                        ve.wait_ge(s["e_p"], at(n, KD, j + 1))
                        ve.scalar_tensor_tensor(qf[:, j, :], bank(kind, j), qk_bias[:, j:j + 1],
                                                ug[:, j, :], ALU.add, ALU.mult).then_inc(s["q_f"], 1)
                    elif kind == "K":
                        ve.wait_ge(s["K_full"], at(n, KD, j + 1))
                        ve.wait_ge(s["e_m"], at(n, KD, j + 1))
                        ve.scalar_tensor_tensor(kf[:, j, :], bank(kind, j),
                                                qk_bias[:, KD + j:KD + j + 1], wgt[:, j, :],
                                                ALU.add, ALU.mult).then_inc(s["k_f"], 1)
                    elif kind == "VG":
                        ve.wait_ge(s["VG_full"], at(n, NT, j + 1))
                        ve.tensor_tensor(vg[:, j, :], bank(kind, j), vg_bias[:, :],
                                         ALU.add).then_inc(s["vg_f"], 1)
                    elif kind == "SIG":
                        two = slice(2 * j, 2 * j + 2)
                        ve.wait_ge(s["vg_f"], at(n, NT, 2 * j + 2))
                        ve.tensor_scalar(sgm[:, two, :], vg[:, two, D:2 * D], -CLAMP, None,
                                         ALU.max).then_inc(s["g_u"], 1)
                    elif kind == "PU":
                        ve.wait_ge(s["f_f"], at(b, NT, NT))
                        ve.tensor_scalar(sgm[:, :, :], ffn[:, :, :], -CLAMP, None,
                                         ALU.max).then_inc(s["f_u"], 1)
                    elif kind == "SC":
                        ve.wait_ge(s["kts_hi"], at(n, NT, j + 1))
                        ve.tensor_tensor(kt_lo[:, :], turn.rearrange("p a b -> p (a b)"),
                                         f(kt_hi[:, :]), ALU.subtract).then_inc(s["kts_lo"], 1)
                        ve.tensor_tensor(a_f[:, :, :, :].rearrange("p a b t -> p (a b) t"),
                                         both[:, :, :, :, :].rearrange("p a r b t -> p (a r) b t")[:, 0:3:2],
                                         mask[:, :].unsqueeze(1).broadcast_to([P, H, P]),
                                         ALU.mult).then_inc(s["a_m"], 1)
                    elif kind == "AV":
                        ve.wait_ge(s["o_sq"], at(n, NT, j + 1))
                        ve.tensor_reduce(ss[:, :], y1[:, :].rearrange("p (h d) -> p h d", h=H), AX.X,
                                         ALU.add).then_inc(s["o_ss"], 1)
                        ve.wait_ge(s["KV_full"], at(n, NT, j + 1))
                        for m in range(KD):
                            end = ug[:, m, (j + 1) * P - 1:(j + 1) * P]
                            i = ve.scalar_tensor_tensor(kv[:, m, :], okv[:, 1, m, :], end,
                                                        pair_mask[:, :], ALU.mult, ALU.mult)
                        i.then_inc(s["kv_ev"], 1)
                        ve.wait_ge(s["kv_ev"], at(n, NT, j + 1))
                        ve.wait_ge(s["sd_f"], at(n, NT, j + 1))
                        ve.tensor_tensor(S[:, :, :], Sd[:, :, :], kv[:, :, :],
                                         ALU.add).then_inc(s["s_new"], 1)
                        ve.wait_ge(s["o_r"], at(n, NT, j + 1))
                        ve.tensor_tensor(y1[:, :].rearrange("p (h d) -> p h d", h=H),
                                         okv[:, 0, :, :].rearrange("p a (b d) -> p (a b) d", d=DK),
                                         ro[:, 1, :].unsqueeze(2).broadcast_to([P, H, DK]),
                                         ALU.mult).then_inc(s["y_1"], 1)
                    elif kind == "YT":
                        ve.wait_ge(s["ys_hi"], at(n, NT, j + 1))
                        ve.tensor_tensor(y_lo[:, :, :], turn, f(y_hi[:, :, :]),
                                         ALU.subtract).then_inc(s["ys_lo"], 1)
                    elif kind == "WO":
                        ve.wait_ge(s["WO_full"], at(n, NT, j + 1))
                        if j == 0:
                            ve.wait_ge(s["xn_ok"], at(n, 1, 1))
                        ve.tensor_tensor(x1[:, j, :], proj.rearrange("p a b -> p (a b)"),
                                         xn0[:, j, :], ALU.add).then_inc(s["x_1"], 1)
                        ve.wait_ge(s["x_1"], at(n, NT, j + 1))
                        ve.bn_stats(bn2[:, :], x1[:, j, :]).then_inc(s["x1_bn"], 1)
                        ve.wait_ge(s["x1_bn"], at(n, NT, j + 1))
                        ve.memset(pad, 0.0)
                        ve.bn_aggr(mv2[:, :], bn2[:, :]).then_inc(s["x1_mv"], 1)
                        ve.wait_ge(s["x1_r"], at(n, NT, j + 1))
                        ve.tensor_scalar(xn2[:, :], x1[:, j, :], mv2[:, 0:1], st2[:, 1:2],
                                         ALU.subtract, ALU.mult).then_inc(s["xn2_f"], 1)
                    elif kind == "XT":
                        ve.wait_ge(s["x2s_hi"], at(n, NT, j + 1))
                        ve.tensor_tensor(x2_lo[:, :, j * P:(j + 1) * P], turn,
                                         f(x2_hi[:, :, j * P:(j + 1) * P]),
                                         ALU.subtract).then_inc(s["x2s_lo"], 1)
                    elif kind == "FC":
                        ve.wait_ge(s["fc_hi"], at(n, MH, j + 1))
                        ve.wait_ge(s["fc_h"], at(n, MH, j + 1))
                        ve.tensor_tensor(ring_lo[:, j % 2, :], ring_f[:, j % 2, 1, :],
                                         f(ring_hi[:, j % 2, :]), ALU.subtract).then_inc(s["fc_lo"], 1)
                    elif kind == "PF":
                        ve.wait_ge(s["PJ_full"], at(n, 1, 1))
                        for t in range(NT):
                            ve.scalar_tensor_tensor(ffn[:, t, :], tile4(acc, t), rr_c[:, t:t + 1],
                                                    pj_scale_row[:, :], ALU.mult,
                                                    ALU.mult).then_inc(s["f_f"], 1)
                    elif kind == "W1":
                        ve.wait_ge(s["w_u"], at(b, M1, j + 1))
                        ve.scalar_tensor_tensor(ring_f[:, j % 2, 0, :], ring_f[:, j % 2, 0, :], 0.01,
                                                ring_f[:, j % 2, 0, :], ALU.mult,
                                                ALU.max).then_inc(s["w_l"], 1)
                        ve.wait_ge(s["ws_hi"], at(b, M1, j + 1))
                        ve.wait_ge(s["w_h"], at(b, M1, j + 1))
                        ve.tensor_tensor(ring_lo[:, j % 2, :], ring_f[:, j % 2, 1, :],
                                         f(ring_hi[:, j % 2, :]), ALU.subtract).then_inc(s["w_lo"], 1)
                    elif kind == "OUT":
                        ve.wait_ge(s["W2_full"], at(b, 1, 1))
                        ve.wait_ge(s["x1_b"], at(b, NT, NT))
                        for t in range(NT):
                            ve.tensor_tensor(x1[:, t, :], tile4(acc, t), x1[:, t, :],
                                             ALU.add).then_inc(s["s_f"], 1)

            step(0, True, False)
            with ve.Fori(1, NB) as n:
                step(n, True, True)
            step(NB, False, True)

        @block.tensor
        def _(pe):
            def split3(dst, l_hi, l_lo, r_hi, r_lo, start, stop):
                pe.matmul(dst, l_hi, r_hi, start=start, stop=False, skip_group_check=True)
                pe.matmul(dst, l_lo, r_hi, start=False, stop=False, skip_group_check=True)
                return pe.matmul(dst, l_hi, r_lo, start=False, stop=stop, skip_group_check=True)

            def turned(dst, src):
                return pe.transpose(dst, src, ident[:, :])

            pe.wait_ge(s["ident_ok"], 2)
            pe.wait_ge(s["ld_small"], 13 * 16)
            pe.transpose(proj[:, 0, 0:NV], xn0[0:NV, 2, P:2 * P], ident[0:NV, 0:NV]).then_inc(s["cols_mm"], 1)
            pe.wait_ge(s["ld_low"], 8 * 16)
            for k in range(KD):
                i = turned(turn[:, k, :], sgm[:, 0, k * P:(k + 1) * P])
            i.then_inc(s["l_vt"], 1)
            for m in range(MH):
                i = turned(acc[m // 4][0:LOW, (m % 4) // 2, (m % 2) * P:(m % 2 + 1) * P],
                           xn0[:, 1, m * LOW:(m + 1) * LOW])
            i.then_inc(s["u_t"], 1)
            pe.wait_ge(s["bias_b"], 1)
            pe.wait_ge(s["ld_qkvg"], 4 * 16)
            vgb = okv[:, :, :, :].rearrange("p a b c -> p (a b c)")
            for k in range(KD):
                pe.matmul(vgb, x_res[:, k, 0:P], kf[:, k, :], start=k == 0, stop=k == KD - 1)
            pe.wait_ge(s["cols_ok"], 1)
            for c in range(2 * KD):
                for k in range(KD):
                    i = pe.matmul(proj[:, 0, c:c + 1], qf[:, k, c * P:(c + 1) * P], l1b[:, k:k + 1],
                                  start=k == 0, stop=k == KD - 1)
            i.then_inc(s["bias_mm"], 1)
            pe.wait_ge(s["l_w"], 1)
            pe.wait_ge(s["bias_ok"], 2)
            for k in range(KD):
                i = pe.matmul(proj[:, 1, 0:1], ffn[:, 2, k * P:(k + 1) * P], l1b[:, k:k + 1],
                              start=k == 0, stop=k == KD - 1)
            i.then_inc(s["lb_mm"], 1)
            gflat = gates[:, :, :, :].rearrange("p a b n -> p (a b n)")
            pe.wait_ge(s["ld_w1"], 16)
            pe.wait_ge(s["lb_ok"], 1)
            for c in range(M1):
                for k in range(KD):
                    i = pe.matmul(proj[:, 1, 8 + c:9 + c], gflat[:, k * F1 + c * P:k * F1 + (c + 1) * P],
                                  l2b[:, k:k + 1], start=k == 0, stop=k == KD - 1)
            i.then_inc(s["bias_mm"], 1)
            wfc = vg[:, :, :].rearrange("p t (a d) -> p (t a) d", a=2)
            wpj = ring_f[:, :, :, :].rearrange("p a b n -> p a (b n)")
            for i in range(8):
                if i == 0:
                    pe.wait_ge(s["fc_t"], MH)
                if i == 4:
                    pe.wait_ge(s["pj_t"], KD)
                if i >= RING:
                    pe.wait_ge(s["tp_free"], i + 1 - RING)
                for q in range(4):
                    if i < 4:
                        k, m = i // 2, 4 * (i % 2) + q
                        src = wfc[:, m, k * P:(k + 1) * P]
                    else:
                        m, o = 2 * (i - 4) + q // 2, q % 2
                        src = wpj[:, o, m * P:(m + 1) * P]
                    j = turned(ring[i % RING][:, q * P:(q + 1) * P], src)
                j.then_inc(s["tp_full"], 1)
            pe.wait_ge(s["pj_s2"], 1)
            for m in range(KD):
                i = pe.matmul(turn[:, m, :], x_res[:, 2 + m, 0:P], ident[:, :], start=True, stop=True)
            i.then_inc(s["bias_mm"], 1)
            pe.wait_ge(s["u_tc"], 1)
            pe.wait_ge(s["bias_ok"], 1)
            uT = x_in[0:LOW, :, :].rearrange("p t d -> p (t d)")
            for m in range(MH):
                i = pe.matmul(okv[:, 0, 0, m * LOW:(m + 1) * LOW], uT[:, m * P:(m + 1) * P],
                              xn0[0:LOW, 2, 0:LOW], start=True, stop=True)
            i.then_inc(s["m_mm"], 1)
            pe.wait_ge(s["m_rep"], 2)
            for i in range(2):
                pe.wait_ge(s["tp_free"], 6 + i)
                for q in range(4):
                    j = turned(ring[(8 + i) % RING][:, q * P:(q + 1) * P], wfc[:, 4 * i + q, 0:P])
                j.then_inc(s["tp_full"], 1)
            pe.wait_ge(s["w_ready"], 1)

            def step(n, front, back):
                b = n - 1
                stages = stages_of(front, back)
                for stage in stages:
                    kind, j = stage
                    if kind in RING_STAGES:
                        if kind == "T" and j == 0:
                            pe.wait_ge(s["xh"], at(n, 1, 1))
                        dst = ring[wait_tenant(pe, stages, stage, n, RING_STAGES, RING)][:, :]
                    for kinds in (PROJ_STAGES, TURN_STAGES):
                        if kind in kinds:
                            wait_tenant(pe, stages, stage, n, kinds, 1)
                    if kind == "T":
                        for t in range(NT):
                            i = turned(dst[:, t * P:(t + 1) * P], x_hat[:, t, j * P:(j + 1) * P])
                        i.then_inc(s["T_full"], 1)
                    elif kind == "L":
                        pe.wait_ge(s["x_lo"], at(n, KD, KD))
                        for k in range(KD):
                            i = split3(dst, wl_hi[:, k, :], wl_lo[:, k, :], xT_hi[:, k, :],
                                       xT_lo[:, k, :], k == 0, k == KD - 1)
                        i.then_inc(s["L_full"], 1)
                    elif kind == "Z":
                        if j == 0:
                            pe.wait_ge(s["p_ready"], at(n, 1, 1))
                        pe.matmul(dst, wz[:, j * P:(j + 1) * P], low[:, :], start=True, stop=True)\
                          .then_inc(s["Z_full"], 1)
                    elif kind in ("Q", "K"):
                        c = (j if kind == "Q" else KD + j) * P
                        for k in range(KD):
                            i = split3(dst, wqk_hi[:, k, c:c + P], wqk_lo[:, k, c:c + P],
                                       xT_hi[:, k, :], xT_lo[:, k, :], k == 0, k == KD - 1)
                        i.then_inc(s[kind + "_full"], 1)
                    elif kind == "VG":
                        tok = slice(j * P, (j + 1) * P)
                        for k in range(KD):
                            i = split3(dst, xT_hi[:, k, tok], xT_lo[:, k, tok], wvg_hi[:, k, :],
                                       wvg_lo[:, k, :], k == 0, k == KD - 1)
                        i.then_inc(s["VG_full"], 1)
                    elif kind == "SC":
                        tok = slice(j * P, (j + 1) * P)
                        if j == 0:
                            pe.wait_ge(s["k_f"], at(n, KD, KD))
                        for m in range(KD):
                            i = turned(turn[:, m, :], kf[:, m, tok])
                        if j == 0:
                            pe.wait_ge(s["qs_lo"], at(n, KD, KD))
                            pe.wait_ge(s["ks_lo"], at(n, KD, KD))
                        for m in range(KD):
                            for a, (ks, qs) in enumerate(((k_hi, q_hi), (k_lo, q_hi), (k_hi, q_lo))):
                                for e in range(2):
                                    rows = slice(e * DK, (e + 1) * DK)
                                    i = pe.matmul(scores[:, e, m, :], ks[rows, m, tok],
                                                  qs[rows, m, tok], start=a == 0, stop=a == 2,
                                                  skip_group_check=True)
                        i.then_inc(s["SC_full"], 1)
                    elif kind == "AV":
                        pe.wait_ge(s["as_lo"], at(n, NT, j + 1))
                        pe.wait_ge(s["vs_lo"], at(n, NT, j + 1))
                        pe.wait_ge(s["srs_lo"], at(n, NT, j + 1))
                        if not (isinstance(n, int) and n == 0 and j == 0):
                            pe.wait_ge(s["y_1"], at(n, NT, j))
                        tok = slice(j * P, (j + 1) * P)
                        for m in range(KD):
                            for e in range(2):
                                h = 2 * m + e
                                split3(okv[:, 0, m, e * DK:(e + 1) * DK], a_hi[:, e, m, :], a_lo[:, e, m, :],
                                       v_hi[:, j, h * DK:(h + 1) * DK], v_lo[:, j, h * DK:(h + 1) * DK],
                                       e == 0, False)
                            i = split3(okv[:, 0, m, :], q_hi[:, m, tok], q_lo[:, m, tok],
                                       Sr_hi[:, m, :], Sr_lo[:, m, :], False, True)
                        pe.wait_ge(s["kts_lo"], at(n, NT, j + 1))
                        for m in range(KD):
                            c = slice(m * P, (m + 1) * P)
                            i = split3(okv[:, 1, m, :], kt_hi[:, c], kt_lo[:, c], v_hi[:, j, c],
                                       v_lo[:, j, c], True, True)
                        i.then_inc(s["KV_full"], 1)
                    elif kind == "YT":
                        pe.wait_ge(s["y_2"], at(n, NT, j + 1))
                        for m in range(KD):
                            i = turned(turn[:, m, :], y2[:, m * P:(m + 1) * P])
                        i.then_inc(s["YT_full"], 1)
                    elif kind == "WO":
                        pe.wait_ge(s["ys_lo"], at(n, NT, j + 1))
                        o = proj.rearrange("p a b -> p (a b)")
                        for k in range(KD):
                            i = split3(o, y_hi[:, k, :], y_lo[:, k, :], wo_hi[:, k, :], wo_lo[:, k, :],
                                       k == 0, k == KD - 1)
                        i.then_inc(s["WO_full"], 1)
                    elif kind == "XT":
                        pe.wait_ge(s["xn2_f"], at(n, NT, j + 1))
                        for m in range(KD):
                            i = turned(turn[:, m, :], xn2[:, m * P:(m + 1) * P])
                        i.then_inc(s["XT_full"], 1)
                    elif kind == "FC":
                        c = slice(j * P, (j + 1) * P)
                        pe.matmul(dst, wu[:, c], low[:, :], start=True, stop=False, skip_group_check=True)
                        for k in range(KD):
                            pe.matmul(dst, tern_fc[:, k, c], xT_hi[:, k, :], start=False, stop=False,
                                      skip_group_check=True)
                            i = pe.matmul(dst, tern_fc[:, k, c], xT_lo[:, k, :], start=False,
                                          stop=k == KD - 1, skip_group_check=True)
                        i.then_inc(s["FC_full"], 1)
                    elif kind == "PJ":
                        pe.wait_ge(s["fc_lo"], at(n, MH, j + 1))
                        if j == 0 and not (isinstance(n, int) and n == 0):
                            pe.wait_ge(s["s_f"], at(b, NT, NT))
                        for t in range(NT):
                            tok = slice(t * P, (t + 1) * P)
                            pe.matmul(tile4(acc, t), ring_hi[:, j % 2, tok], tern_pj[:, j, :],
                                      start=j == 0 and t % 2 == 0, stop=False, skip_group_check=True)
                            i = pe.matmul(tile4(acc, t), ring_lo[:, j % 2, tok], tern_pj[:, j, :],
                                          start=False, stop=j == MH - 1, skip_group_check=True)
                        if j == MH - 1:
                            i.then_inc(s["PJ_full"], 1)
                    elif kind == "W1":
                        if j == 0:
                            pe.wait_ge(s["x2s_lo"], at(b, NT, NT))
                        c = slice(j * P, (j + 1) * P)
                        for k in range(KD):
                            i = split3(dst, w1_hi[:, k, c], w1_lo[:, k, c], x2_hi[:, k, :],
                                       x2_lo[:, k, :], k == 0, k == KD - 1)
                        i.then_inc(s["W1_full"], 1)
                    elif kind == "W2":
                        pe.wait_ge(s["w_lo"], at(b, M1, j + 1))
                        if j == 0:
                            pe.wait_ge(s["f_f"], at(b, NT, NT))
                        for t in range(NT):
                            tok = slice(t * P, (t + 1) * P)
                            i = split3(tile4(acc, t), ring_hi[:, j % 2, tok], ring_lo[:, j % 2, tok],
                                       w2_hi[:, j, :], w2_lo[:, j, :], j == 0 and t % 2 == 0,
                                       j == M1 - 1)
                        if j == M1 - 1:
                            i.then_inc(s["W2_full"], 1)

            step(0, True, False)
            with pe.Fori(1, NB) as n:
                step(n, True, True)
            step(NB, False, True)


_ATTN = ["x", "ln1_w", "ln1_b", "Wq", "Wk", "Wv", "Wg", "Wgk1", "Wgk2", "bgk2", "rms_w", "Wo",
         "ln2_w", "ln2_b", "W1", "b1", "W2", "b2"]
_FFN = ["fast_b", "w_fc", "w_proj", "u", "v", "gate"]
_INS = [f"L0_attn_{n}" for n in _ATTN] + [f"L0_ffn_{n}" for n in _FFN]


def kernel(**inputs):
    import numpy as _np
    import concourse.bacc as _bacc
    from concourse import mybir as _mybir
    from concourse.bass_utils import run_bass_kernel_spmd as _run

    nc = _bacc.Bacc("TRN2", target_bir_lowering=False, num_devices=1)
    arrays, args = {}, []
    for name in _INS:
        a = _np.ascontiguousarray(inputs[name])
        if a.ndim == 0:
            a = a.reshape(1)
        arrays[f"in_{name}"] = a
        args.append(nc.dram_tensor(f"in_{name}", a.shape, _mybir.dt.from_np(a.dtype),
                                   kind="ExternalInput").ap())
    out = nc.dram_tensor("out", (B, T, D), _mybir.dt.float32, kind="ExternalOutput").ap()
    recurrent_block_kernel(nc, *args, out)
    r = _run(nc, [arrays], core_ids=[0])
    return r.results[0]["out"]
```

```python
from contextlib import ExitStack

import concourse.bass as bass
from concourse import mybir

F32 = mybir.dt.float32
F32R = mybir.dt.float32r
ACT = mybir.ActivationFunctionType
ALU = mybir.AluOpType
AX = mybir.AxisListType

P = 128
B, T, D = 4, 1024, 256
H, DK = 4, 64
LOW = 16
F1, FH = 3 * D, 4 * D
NT = 4
TB = NT * P
NB = B * T // TB
KD = D // P
M1, MH = F1 // P, FH // P
MID = P // 2 - 1
EPS = 1e-5
GLN = 16.0
CLAMP = 40.0

ORDERS = {
    "pe": """
        T0 YT3b T1 WO3b L0 VG0 XT3b VG1 Z0 VG2 W10b Z1 W11b Q0 K0 Q1 W20b W12b K1 W21b W13b W22b
        VG3 SC0 W14b W23b W15b AV0 SC1 W24b W25b FC0 FC1 YT0 AV1 WO0 SC2 PJ0 PJ1 FC2 FC3 YT1 AV2
        SC3 PJ2 FC4 PJ3 XT0 FC5 WO1 PJ4 FC6 YT2 PJ5 FC7 XT1 WO2 AV3 XT2 PJ6 PJ7
    """,
    "ac": """
        T0 YT3b T1 L0 XT3b PU0b Z0 W10b VG0 Z1 WL0b W11b VG1 EX0 WL1b K0 VG2 Q0 W12b EX1 WL2b Q1
        W13b K1 WL3b ST0 SC0 SS0 W14b SIG0 WL4b W15b VG3 AV0 WL5b SC1 ST1 SS1 FC0 YT0 FC1 AV1 SC2
        ST2 SS2 FC2 YT1 FC3 AV2 SIG1 SC3 FC4 XT0 SS3 FC5 FC6 YT2 ST3 XT1 FC7 AV3 XT2
    """,
    "ve": """
        T0 YT3b T1 WO3b WN3b PU0b L0 VG0 XT3b VG1 Z0 VG2 Z1 W10b SCAN0 WL0b W11b K0 Q0 WL1b SCAN1
        W12b Q1 SIG0 WL2b K1 DEC0 W13b XN0 WL3b SC0 VG3 SIG1 W14b WL4b W15b AV0 WL5b SC1 AY0 OUT0b
        YT0 AV1 WO0 FL0 FL1 AY1 SC2 LNA0 YT1 FL2 FL3 AV2 SC3 WN0 AY2 LNC0 FL4 XT0 WO1 FL5 WN1 YT2
        XT1 WO2 FL6 WN2 FL7 AV3 XT2 AY3 PF0
    """,
    "gp": """
        WP3b WL0b WN3b PG0b VG0 VG1 Q0 WL2b K0 Q1 K1 ST0 SS0 WL4b SL0 VG2 VG3 AP0 ST1 AY0 SS1
        OUT0b FC0 AP1 ST2 AY1 SS2 FC2 LNB0 WP0 AP2 FC4 SL1 AY2 SS3 WP1 ST3 FC6 WP2 WN0 WN1 AP3 AY3
        WN2
    """,
}


def parsed(name):
    back = name.endswith("b")
    name = name.rstrip("b")
    return name[:-1], int(name[-1]), back


ORDERS = {engine: [parsed(name) for name in order.split()] for engine, order in ORDERS.items()}
STAGES = {stage for order in ORDERS.values() for stage in order}
PER = {k: sum(s[0] == k for s in STAGES) for k, _, _ in STAGES}
RING_STAGES = ("T", "L", "Z", "Q", "K", "VG", "W1", "FC")
RING = 3
PROJ_STAGES = ("SC", "WO")
TURN_STAGES = ("SC", "YT", "XT")


def stages_of(front, back, engine="pe"):
    return [s for s in ORDERS[engine] if (back if s[2] else front)]


def tenant(stages, stage, kinds, banks):
    mine = [s for s in stages if s[0] in kinds]
    at = mine.index(stage)
    if at >= banks:
        return at % banks, mine[at - banks], False
    ends = [s for s in stages_of(True, False) if s[0] in kinds]
    return at % banks, ends[len(ends) - banks + at], True


def recurrent_block_kernel(nc, x, ln1_w, ln1_b, wq, wk, wv, wg, wgk1, wgk2, bgk2, rms_w, wo,
                           ln2_w, ln2_b, w1, b1, w2, b2, fast_b, w_fc, w_proj, u, v, gate, out):
    x_blocks = x.rearrange("b (m t p) d -> (b m) p t d", t=NT, p=P)
    out_blocks = out.rearrange("b (m t p) d -> (b m) p t d", t=NT, p=P)

    with ExitStack() as ctx:
        def sb(name, *shape, dt=F32):
            return ctx.enter_context(nc.sbuf_tensor(name, [P, *shape], dt))

        def sem(name):
            return ctx.enter_context(nc.semaphore(name))

        def f(ap):
            return ap.bitcast(F32)

        wqk_hi, wqk_lo = (sb(f"wqk_{s}", KD, 2 * D, dt=F32R) for s in ("hi", "lo"))
        wvg_hi, wvg_lo = (sb(f"wvg_{s}", KD, 2 * D, dt=F32R) for s in ("hi", "lo"))
        wl_hi, wl_lo = (sb(f"wl_{s}", KD, P, dt=F32R) for s in ("hi", "lo"))
        w1_hi, w1_lo = (sb(f"w1_{s}", KD, F1, dt=F32R) for s in ("hi", "lo"))
        w2_hi, w2_lo = (sb(f"w2_{s}", M1, D, dt=F32R) for s in ("hi", "lo"))
        wo_hi, wo_lo = (sb(f"wo_{s}", KD, D, dt=F32R) for s in ("hi", "lo"))
        wz = sb("wz", D, dt=F32R)
        wu = sb("wu", FH, dt=F32R)
        tern_fc = sb("tern_fc", KD, FH, dt=F32R)
        tern_pj = sb("tern_pj", MH, D, dt=F32R)
        ident, mask, pair_mask = sb("ident", P), sb("mask", P), sb("pair_mask", P)
        vg_bias, b2_row, pj_scale_row = sb("vg_bias", 2 * D), sb("b2_row", D), sb("pj_scale_row", D)
        cols = sb("cols", 64)
        c_at = [0]

        def col(n):
            c_at[0] += n
            return cols[:, c_at[0] - n:c_at[0]]

        l1w, l1b, l2w, l2b, bz, b1c, rmsc = col(KD), col(KD), col(KD), col(KD), col(KD), col(M1), col(1)
        NV = c_at[0]
        gatec, qk_bias, b1_bias = col(1), col(2 * KD), col(M1)
        bz_up = col(KD)
        lb, lb_lo, sign_hi, is_lo = col(1), col(1), col(1), col(1)
        keep = sb("keep", NB)
        small = sb("small", 64)
        s_at = [0]

        def tiny(n):
            s_at[0] += n
            return small[:, s_at[0] - n:s_at[0]]

        fc_scale, fc_half, fc_nhalf, fc_g = tiny(MH), tiny(MH), tiny(MH), tiny(MH)
        pj_scale, pj_half, pj_nhalf = tiny(KD), tiny(KD), tiny(KD)
        half_neg = tiny(NT)
        pad = tiny(1)
        eps_col, eps_head = tiny(NT), tiny(H)

        x_in, x_hat, xn0 = sb("x_in", NT, D), sb("x_hat", NT, D), sb("xn0", NT, D)
        xT_hi, xT_lo = sb("xT_hi", KD, TB, dt=F32R), sb("xT_lo", KD, TB, dt=F32R)
        low = sb("low", TB, dt=F32R)
        gates = sb("gates", 3, KD, TB)
        ug, wgt, G = gates[:, 0], gates[:, 1], gates[:, 2]
        qf, kf = sb("qf", KD, TB), sb("kf", KD, TB)
        q_hi, q_lo = sb("q_hi", KD, TB, dt=F32R), sb("q_lo", KD, TB, dt=F32R)
        k_hi, k_lo = sb("k_hi", KD, TB, dt=F32R), sb("k_lo", KD, TB, dt=F32R)
        low_hi, low_f = k_hi[:, 1], kf[:, 1]
        vg = sb("vg", NT, 2 * D)
        v_hi, v_lo = sb("v_hi", NT, D, dt=F32R), sb("v_lo", NT, D, dt=F32R)
        sgm = sb("sgm", NT, D)
        kt_hi, kt_lo = sb("kt_hi", D, dt=F32R), sb("kt_lo", D, dt=F32R)
        a_f = sb("a_f", 2, KD, P)
        a_hi, a_lo = sb("a_hi", 2, KD, P, dt=F32R), sb("a_lo", 2, KD, P, dt=F32R)
        y1, y2 = sb("y1", D), sb("y2", D)
        y_hi, y_lo = sb("y_hi", KD, P, dt=F32R), sb("y_lo", KD, P, dt=F32R)
        x1, xn2 = sb("x1", NT, D), sb("xn2", D)
        x2_hi, x2_lo = sb("x2_hi", KD, TB, dt=F32R), sb("x2_lo", KD, TB, dt=F32R)
        ring_f = sb("ring_f", 2, 2, TB)
        ring_hi, ring_lo = sb("ring_hi", 2, TB, dt=F32R), sb("ring_lo", 2, TB, dt=F32R)
        S, Sd, Sr, kv = sb("S", KD, P), sb("Sd", KD, P), sb("Sr", KD, P), sb("kv", KD, P)
        Sr_hi, Sr_lo = sb("Sr_hi", KD, P, dt=F32R), sb("Sr_lo", KD, P, dt=F32R)
        ffn, x_res = sb("ffn", NT, D), sb("x_res", NT, D)
        bn, mv = sb("bn", NT, 6), sb("mv", NT, 2)
        bn2, mv2, st2 = sb("bn2", 6), sb("mv2", 2), sb("st2", 2)
        st = sb("st", 8, NT)
        rr_c = sb("rr_c", NT)
        dec_r, dec_t = sb("dec_r", KD, NT), sb("dec_t", KD, NT)
        ss, ro = sb("ss", H), sb("ro", 2, H)
        fc_neg = [t[:, :, :].rearrange("p k (a d) -> p (k a) d", d=D) for t in (xT_hi, xT_lo)]
        pj_neg = [t[:, :, :].rearrange("p k n -> p (k n)") for t in (q_hi, q_lo)]
        mean = mv[:, :, 0]
        var = mv[:, :, 1]

        def pb(name, *shape):
            return ctx.enter_context(nc.psum_tensor(name, [P, *shape], F32))

        ring = [pb(f"ring{i}", TB) for i in range(RING)]
        acc = [pb(f"acc{i}", 2, D) for i in range(2)]
        okv = pb("okv", 2, KD, P)
        both = pb("both", 2, 2, KD, P)
        scores = both[:, :, 0]
        proj = both[:, 0, 1]
        turn = both[:, 1, 1]

        names = """ld_qkvg ld_small ld_fc ld_pj ld_w1 ld_w2 ld_wo ld_low zeroed ident_ok
            p_masks p_const bias_b bias_mm bias_ok fold1 fold_qk fold_vg fold_w1 fold_w2 fold_wo
            w_hi w_ready fc_s fc_s2 fc_a fc_t pj_s pj_s2 pj_a pj_t tp_full tp_free u_t u_tc m_mm
            m_f m_hi m_rep l_vt l_f l_w lb_mm lb_ok z_w cols_mm cols_ok w_cst lo_done
            x_dma res_dma out_dma bn_ok mv_ok ln_a ln_b ln_c ln_d ln_e ln_f ln_g xh xn_ok
            T_full x_hi x_lo L_full l_ev p_ready Z_full z_u z_w2 z_e z_l g_sc g_fin g_rel e_p e_m
            e_r dk dec_ok Q_full q_f qs_hi qs_lo K_full k_f ks_hi ks_lo VG_full vg_f vs_hi vs_lo
            g_u g_s1 g_s2 g_s3 g_sil kts_hi kts_lo SC_full a_m as_hi as_lo
            sr_f sd_f srs_hi srs_lo s_new KV_full o_sq o_ss o_t o_r y_1 y_2 kv_ev
            YT_full ys_hi ys_lo WO_full x_1 x1_bn x1_mv x1_t x1_r xn2_f x1_b XT_full x2s_hi
            x2s_lo FC_full fc_act fc_hi fc_h fc_h_odd fc_lo PJ_full f_f f_u f_1 f_2 f_3 f_g
            W1_full w_u w_l ws_hi w_h w_h_odd w_lo W2_full s_f s_g out_ok""".split()
        s = {n: sem(n) for n in names}

        FREED = {"T": "x_lo", "L": "l_ev", "Z": "z_w2", "Q": "q_f", "K": "k_f", "VG": "vg_f",
                 "W1": "w_u", "FC": "fc_act", "SC": "a_m", "WO": "x_1", "YT": "ys_lo", "XT": "x2s_lo"}

        block = ctx.enter_context(nc.Block())

        def at(n, per, j):
            return n * per + j

        def wait_tenant(pe, stages, stage, n, kinds, banks):
            bank, (kind, j, of_before), before = tenant(stages, stage, kinds, banks)
            m = n - 1 if of_before else n
            if before:
                m = m - 1
                if isinstance(m, int) and m < 0:
                    return bank
            pe.wait_ge(s[FREED[kind]], at(m, PER[kind], j + 1))
            return bank

        def tile4(bank_pair, t):
            return bank_pair[t // 2][:, t % 2, :]

        @block.sync
        def _(sp):
            def two(dst, w, name):
                sp.dma_start(dst, w.rearrange("(k p) n -> p k n", p=P)).then_inc(s[name], 16)

            sp.dma_start(x_in[:, :, :], x_blocks[0]).then_inc(s["x_dma"], 16)
            sp.dma_start(vg[:, :, :].rearrange("p t (a d) -> p (t a) d", a=2),
                         w_fc.rearrange("(m p) d -> p m d", p=P)).then_inc(s["ld_fc"], 16)
            sp.dma_start(ring_f[:, :, :, :].rearrange("p a b n -> p a (b n)"),
                         w_proj.rearrange("(m p) n -> p m n", p=P)).then_inc(s["ld_pj"], 16)
            two(qf[:, :, 0:D], wq, "ld_qkvg")
            two(qf[:, :, D:2 * D], wk, "ld_qkvg")
            two(kf[:, :, 0:D], wv, "ld_qkvg")
            two(kf[:, :, D:2 * D], wg, "ld_qkvg")
            two(x1[:, 0:2, :], wo, "ld_wo")
            gflat = gates[:, :, :, :].rearrange("p a b n -> p (a b n)")
            two(gflat[:, 0:KD * F1].rearrange("p (k n) -> p k n", k=KD), w1, "ld_w1")
            two(gflat[:, KD * F1:2 * KD * F1].rearrange("p (k n) -> p k n", k=M1), w2, "ld_w2")

            def step(n, front, back):
                if front:
                    nxt = x_blocks[(n + 1) % NB] if isinstance(n, int) else \
                        x_blocks[sp.snap(n + 1)]
                    sp.wait_ge(s["xh"], at(n, 1, 1))
                    sp.dma_start(x_in[:, :, :], nxt).then_inc(s["x_dma"], 16)
                if back:
                    m = n - 1
                    dst = out_blocks[m] if isinstance(n, int) else out_blocks[sp.snap(n - 1)]
                    src = x_blocks[m] if isinstance(n, int) else x_blocks[sp.snap(n - 1)]
                    if not isinstance(n, int) or m >= 1:
                        sp.wait_ge(s["out_dma"], m * 16)
                    sp.dma_start(x_res[:, :, :], src).then_inc(s["res_dma"], 16)
                    sp.wait_ge(s["out_ok"], at(m, 1, 1))
                    sp.dma_start(dst, x_res[:, :, :]).then_inc(s["out_dma"], 16)

            sp.wait_ge(s["w_ready"], 1)
            step(0, True, False)
            step(1, True, True)
            with sp.Fori(2, NB - 1) as n:
                step(n, True, True)
            step(NB - 1, True, True)
            step(NB, False, True)
            sp.wait_ge(s["out_dma"], NB * 16)
            sp.wait_ge(s["x_dma"], (NB + 1) * 16)

        @block.gpsimd
        def _(gp):
            gp.memset(ident[:, :], 0.0).then_inc(s["p_masks"], 1)
            gp.memset(mask[:, :], 1.0).then_inc(s["p_masks"], 1)
            gp.memset(sgm[:, :, :], 0.0).then_inc(s["zeroed"], 1)
            gp.memset(ffn[:, :, :], 0.0).then_inc(s["zeroed"], 1)
            gp.wait_ge(s["p_masks"], 2)
            gp.affine_select(out=ident[:, :], in_=ident[:, :], compare_op=ALU.not_equal, fill=1.0,
                             base=0, pattern=[[-1, P]], channel_multiplier=1).then_inc(s["ident_ok"], 1)
            gp.affine_select(out=mask[:, :], in_=mask[:, :], compare_op=ALU.is_ge, fill=0.0,
                             base=0, pattern=[[1, P]], channel_multiplier=-1).then_inc(s["ident_ok"], 1)
            gp.memset(half_neg, -0.5)
            gp.memset(eps_col, EPS)
            gp.memset(eps_head, EPS * DK).then_inc(s["p_const"], 1)
            gp.memset(S[:, :, :], 0.0).then_inc(s["s_new"], 1)

            def pow_chain_in(n):
                gp.wait_ge(s["mv_ok"], at(n, 1, 1))
                gp.tensor_tensor(st[:, 0, :], var, eps_col, ALU.add).then_inc(s["ln_a"], 1)
                gp.wait_ge(s["ln_a"], at(n, 1, 1))
                gp.tensor_tensor(st[:, 1, :], st[:, 0, :], half_neg, ALU.pow).then_inc(s["ln_b"], 1)
                gp.wait_ge(s["ln_b"], at(n, 1, 1))
                gp.tensor_tensor(st[:, 2, :], var, st[:, 1, :], ALU.mult).then_inc(s["ln_c"], 1)
                gp.wait_ge(s["ln_c"], at(n, 1, 1))
                gp.tensor_tensor(st[:, 3, :], st[:, 2, :], st[:, 1, :], ALU.mult).then_inc(s["ln_d"], 1)
                gp.wait_ge(s["ln_d"], at(n, 1, 1))
                gp.tensor_tensor(st[:, 4, :], st[:, 3, :], eps_col, ALU.add).then_inc(s["ln_e"], 1)
                gp.wait_ge(s["ln_e"], at(n, 1, 1))
                gp.tensor_tensor(st[:, 5, :], st[:, 4, :], half_neg, ALU.pow).then_inc(s["ln_f"], 1)
                gp.wait_ge(s["ln_f"], at(n, 1, 1))
                gp.tensor_tensor(st[:, 6, :], st[:, 5, :], st[:, 1, :], ALU.mult).then_inc(s["ln_g"], 1)
                gp.tensor_tensor(st[:, 7, :], st[:, 5, :], st[:, 4, :], ALU.mult).then_inc(s["ln_g"], 1)

            gp.wait_ge(s["p_const"], 1)
            pow_chain_in(0)

            wfc = vg[:, :, :].rearrange("p t (a d) -> p (t a) d", a=2)
            wpj = ring_f[:, :, :, :].rearrange("p a b n -> p a (b n)")
            gp.wait_ge(s["fc_s"], 3)
            for m in range(MH):
                gp.tensor_scalar(fc_neg[m // 4][:, m % 4, :], wfc[:, m, :], fc_nhalf[:, m:m + 1], None,
                                 ALU.is_lt).then_inc(s["fc_a"], 1)
            gp.wait_ge(s["pj_s"], 3)
            for m in range(KD):
                gp.tensor_scalar(pj_neg[m], wpj[:, m, :], pj_nhalf[:, m:m + 1], None,
                                 ALU.is_lt).then_inc(s["pj_a"], 1)
            gflat = gates[:, :, :, :].rearrange("p a b n -> p (a b n)")
            w1_st = gflat[:, 0:KD * F1].rearrange("p (k n) -> p k n", k=KD)
            w2_st = gflat[:, KD * F1:2 * KD * F1].rearrange("p (k n) -> p k n", k=M1)
            for i, (lo, w, hi) in enumerate((
                    (wo_lo[:, :, :], x1[:, 0:2, :], wo_hi[:, :, :]), (w1_lo[:, :, :], w1_st, w1_hi[:, :, :]),
                    (w2_lo[:, :, :], w2_st, w2_hi[:, :, :]))):
                gp.wait_ge(s["w_hi"], 4 + i)
                gp.tensor_tensor(lo, w, f(hi), ALU.subtract).then_inc(s["lo_done"], 1)

            def step(step_n, front, back):
                for kind, j, of_before in stages_of(front, back, "gp"):
                    n = step_n - 1 if of_before else step_n
                    if kind == "LNB":
                        pow_chain_in(n + 1)
                    elif kind == "Q":
                        gp.wait_ge(s["qs_hi"], at(n, KD, j + 1))
                        gp.tensor_tensor(q_lo[:, j, :], qf[:, j, :], f(q_hi[:, j, :]),
                                         ALU.subtract).then_inc(s["qs_lo"], 1)
                    elif kind == "K":
                        gp.wait_ge(s["ks_hi"], at(n, KD, j + 1))
                        gp.tensor_tensor(k_lo[:, j, :], kf[:, j, :], f(k_hi[:, j, :]),
                                         ALU.subtract).then_inc(s["ks_lo"], 1)
                    elif kind == "VG":
                        gp.wait_ge(s["vs_hi"], at(n, NT, j + 1))
                        gp.tensor_tensor(v_lo[:, j, :], vg[:, j, 0:D], f(v_hi[:, j, :]),
                                         ALU.subtract).then_inc(s["vs_lo"], 1)
                    elif kind == "SL":
                        two = slice(2 * j, 2 * j + 2)
                        gp.wait_ge(s["g_s3"], at(n, 2, j + 1))
                        gp.wait_ge(s["vs_lo"], at(n, NT, 2 * j + 2))
                        gp.tensor_tensor(vg[:, two, 0:D], vg[:, two, D:2 * D], sgm[:, two, :],
                                         ALU.mult).then_inc(s["g_sil"], 1)
                    elif kind == "SS":
                        gp.wait_ge(s["as_hi"], at(n, NT, j + 1))
                        gp.tensor_tensor(a_lo[:, :, :, :], a_f[:, :, :, :], f(a_hi[:, :, :, :]),
                                         ALU.subtract).then_inc(s["as_lo"], 1)
                    elif kind == "ST":
                        gp.wait_ge(s["s_new"], at(n, NT, j + 1))
                        if j == 0:
                            gp.wait_ge(s["dec_ok"], at(n, 1, 1))
                        gp.tensor_tensor(Sr[:, :, :], S[:, :, :],
                                         dec_r[:, :, j:j + 1].broadcast_to([P, KD, P]),
                                         ALU.mult).then_inc(s["sr_f"], 1)
                        gp.tensor_tensor(Sd[:, :, :], S[:, :, :],
                                         dec_t[:, :, j:j + 1].broadcast_to([P, KD, P]),
                                         ALU.mult).then_inc(s["sd_f"], 1)
                        gp.wait_ge(s["srs_hi"], at(n, NT, j + 1))
                        gp.tensor_tensor(Sr_lo[:, :, :], Sr[:, :, :], f(Sr_hi[:, :, :]),
                                         ALU.subtract).then_inc(s["srs_lo"], 1)
                    elif kind == "AP":
                        gp.wait_ge(s["o_ss"], at(n, NT, j + 1))
                        gp.tensor_tensor(ro[:, 0, :], ss[:, :], eps_head, ALU.add).then_inc(s["o_t"], 1)
                        gp.wait_ge(s["o_t"], at(n, NT, j + 1))
                        gp.tensor_tensor(ro[:, 1, :], ro[:, 0, :], half_neg, ALU.pow).then_inc(s["o_r"], 1)
                    elif kind == "AY":
                        gp.wait_ge(s["y_1"], at(n, NT, j + 1))
                        if j % 2 == 0:
                            gp.wait_ge(s["g_sil"], at(n, 2, j // 2 + 1))
                        gp.tensor_tensor(y2[:, :], y1[:, :], vg[:, j, 0:D], ALU.mult).then_inc(s["y_2"], 1)
                    elif kind == "WP":
                        gp.wait_ge(s["x1_mv"], at(n, NT, j + 1))
                        gp.tensor_tensor(st2[:, 0:1], mv2[:, 1:2], eps_col[:, 0:1], ALU.add).then_inc(s["x1_t"], 1)
                        gp.wait_ge(s["x1_t"], at(n, NT, j + 1))
                        gp.tensor_tensor(st2[:, 1:2], st2[:, 0:1], half_neg[:, 0:1],
                                         ALU.pow).then_inc(s["x1_r"], 1)
                    elif kind == "WN":
                        gp.wait_ge(s["xn2_f"], at(n, NT, j + 1))
                        gp.tensor_tensor(x1[:, j, :], x1[:, j, :], b2_row[:, :],
                                         ALU.add).then_inc(s["x1_b"], 1)
                    elif kind == "FC" and j % 2 == 0:
                        gp.wait_ge(s["fc_act"], at(n, MH, j + 1))
                        gp.tensor_tensor(ring_f[:, j % 2, 1, :], ring_f[:, j % 2, 0, :],
                                         ring_f[:, j % 2, 0, :], ALU.mult).then_inc(s["fc_h"], 1)
                    elif kind == "PG":
                        gp.wait_ge(s["f_3"], at(n, 1, 1))
                        gp.tensor_tensor(ffn[:, :, :], ffn[:, :, :], sgm[:, :, :],
                                         ALU.mult).then_inc(s["f_g"], 1)
                    elif kind == "WL" and j % 2 == 0:
                        gp.wait_ge(s["w_l"], at(n, M1, j + 1))
                        gp.tensor_tensor(ring_f[:, j % 2, 1, :], ring_f[:, j % 2, 0, :],
                                         ring_f[:, j % 2, 0, :], ALU.mult).then_inc(s["w_h"], 1)
                    elif kind == "OUT":
                        gp.wait_ge(s["s_f"], at(n, NT, NT))
                        gp.wait_ge(s["f_g"], at(n, 1, 1))
                        gp.tensor_tensor(x1[:, :, :], x1[:, :, :], ffn[:, :, :],
                                         ALU.mult).then_inc(s["s_g"], 1)
                        gp.wait_ge(s["s_g"], at(n, 1, 1))
                        gp.wait_ge(s["res_dma"], at(n, 16, 16))
                        gp.tensor_tensor(x_res[:, :, :], x1[:, :, :], x_res[:, :, :],
                                         ALU.add).then_inc(s["out_ok"], 1)

            step(0, True, False)
            with gp.Fori(1, NB) as n:
                step(n, True, True)
            step(NB, False, True)

        @block.scalar
        def _(ac):
            ac.preload_act_table_set("natural_log_exp_and_others")
            vec = xn0[:, 2, P:2 * P]
            row, small_loads = 0, []
            for w, k in ((ln1_w, KD), (ln1_b, KD), (ln2_w, KD), (ln2_b, KD), (bgk2, KD), (b1, M1)):
                small_loads.append((vec[row:row + k, :], w.rearrange("(k p) -> k p", p=P)))
                row += k
            small_loads += [(vec[row:row + 1, e * DK:(e + 1) * DK], rms_w.rearrange("(a n) -> a n", a=1))
                            for e in range(2)]
            small_loads += [
                (gatec, gate.rearrange("(a n) -> a n", a=1).broadcast_to([P, 1])),
                (b2_row[:, :], b2.rearrange("(a n) -> a n", a=1).broadcast_to([P, D])),
                (xn0[:, 0, 0:KD * LOW].rearrange("p (k r) -> p k r", k=KD), wgk1.rearrange("(k p) r -> p k r", p=P)),
                (xn0[:, 1, 0:MH * LOW].rearrange("p (m r) -> p m r", m=MH), u.rearrange("(m p) r -> p m r", p=P)),
                (xn0[0:LOW, 2, 0:LOW], fast_b),
            ]
            for dst, src in small_loads:
                ac.dma_start(dst, src).then_inc(s["ld_small"], 16)
            ac.wait_ge(s["zeroed"], 2)
            for g in range(4):
                ac.dma_start(sgm[32 * g + LOW:32 * g + 2 * LOW, 0, :], v).then_inc(s["ld_low"], 16)
                ac.dma_start(sgm[32 * g:32 * g + LOW, 1, :], wgk2).then_inc(s["ld_low"], 16)

            gflat = gates[:, :, :, :].rearrange("p a b n -> p (a b n)")
            w1_st = gflat[:, 0:KD * F1].rearrange("p (k n) -> p k n", k=KD)
            w2_st = gflat[:, KD * F1:2 * KD * F1].rearrange("p (k n) -> p k n", k=M1)

            def ternary(lo, hi):
                for i in range(lo, hi):
                    ac.wait_ge(s["tp_full"], i + 1)
                    if i < 4:
                        half, k = i // 2, i % 2
                        dst = tern_fc[:, k, half * TB:(half + 1) * TB]
                    else:
                        dst = tern_pj[:, 2 * (i - 4):2 * (i - 4) + 2, :].rearrange("p a b -> p (a b)")
                    ac.activation(dst, ring[i % RING][:, :], ACT.Copy).then_inc(s["tp_free"], 1)

            ternary(0, 4)
            ac.wait_ge(s["l_w"], 1)
            ac.activation(wl_hi[:, :, :], xn0[:, 3, :].rearrange("p (k n) -> p k n", k=KD), ACT.Copy)\
              .then_inc(s["w_hi"], 1)
            ac.wait_ge(s["fold_qk"], 1)
            ac.activation(wqk_hi[:, :, :], qf[:, :, :], ACT.Copy).then_inc(s["w_hi"], 1)
            ac.wait_ge(s["fold_vg"], 1)
            ac.activation(wvg_hi[:, :, :], kf[:, :, :], ACT.Copy).then_inc(s["w_hi"], 1)
            ac.wait_ge(s["fold_wo"], 1)
            ac.activation(wo_hi[:, :, :], x1[:, 0:2, :], ACT.Copy).then_inc(s["w_hi"], 1)
            ac.wait_ge(s["fold_w1"], 1)
            ac.activation(w1_hi[:, :, :], w1_st, ACT.Copy).then_inc(s["w_hi"], 1)
            ac.wait_ge(s["ld_w2"], 16)
            ac.activation(w2_hi[:, :, :], w2_st, ACT.Copy).then_inc(s["w_hi"], 1)
            ternary(4, 8)
            for i in range(2):
                ac.wait_ge(s["tp_full"], 9 + i)
                ac.activation(wu[:, i * TB:(i + 1) * TB], ring[(8 + i) % RING][:, :], ACT.Copy)\
                  .then_inc(s["tp_free"], 1)

            def log_sigmoid_exp(n, per, j, buf, ready, first, second, third):
                ac.wait_ge(s[ready], at(n, per, j))
                ac.activation(buf, buf, ACT.Exp, scale=-1.0).then_inc(s[first], 1)
                ac.wait_ge(s[first], at(n, per, j))
                ac.activation(buf, buf, ACT.Ln, bias=1.0).then_inc(s[second], 1)
                ac.wait_ge(s[second], at(n, per, j))
                ac.activation(buf, buf, ACT.Exp, scale=-1.0).then_inc(s[third], 1)

            def step(step_n, front, back):
                stages = stages_of(front, back)

                def bank(*stage):
                    return ring[tenant(stages, stage, RING_STAGES, RING)[0]][:, :]

                for kind, j, of_before in stages_of(front, back, "ac"):
                    n = step_n - 1 if of_before else step_n
                    if kind == "T":
                        ac.wait_ge(s["T_full"], at(n, KD, j + 1))
                        ac.activation(xT_hi[:, j, :], bank(kind, j, of_before), ACT.Copy).then_inc(s["x_hi"], 1)
                    elif kind == "L":
                        ac.wait_ge(s["L_full"], at(n, 1, 1))
                        ac.activation(low_hi[:, :], bank(kind, j, of_before), ACT.Identity, bias=lb)
                        ac.activation(low_f, bank(kind, j, of_before), ACT.Identity, bias=lb_lo, scale=is_lo)\
                          .then_inc(s["l_ev"], 1)
                    elif kind == "Z":
                        ac.wait_ge(s["z_u"], at(n, KD, j + 1))
                        ac.activation(ug[:, j, :], ug[:, j, :], ACT.Exp, scale=-1.0).then_inc(s["z_e"], 1)
                        ac.wait_ge(s["z_e"], at(n, KD, j + 1))
                        ac.activation(ug[:, j, :], ug[:, j, :], ACT.Ln, bias=1.0).then_inc(s["z_l"], 1)
                    elif kind == "EX":
                        ac.wait_ge(s["g_rel"], at(n, KD, j + 1))
                        ac.activation(ug[:, j, :], wgt[:, j, :], ACT.Exp, scale=1.0 / GLN)\
                          .then_inc(s["e_p"], 1)
                        ac.activation(dec_r[:, j, :],
                                      G[:, j, :].rearrange("p (c t) -> p c t", t=P)[:, :, MID],
                                      ACT.Exp, scale=1.0 / GLN).then_inc(s["e_r"], 1)
                        ac.wait_ge(s["e_p"], at(n, KD, j + 1))
                        ac.activation(wgt[:, j, :], wgt[:, j, :], ACT.Exp, scale=-1.0 / GLN)\
                          .then_inc(s["e_m"], 1)
                    elif kind == "Q":
                        ac.wait_ge(s["q_f"], at(n, KD, j + 1))
                        ac.activation(q_hi[:, j, :], qf[:, j, :], ACT.Copy).then_inc(s["qs_hi"], 1)
                    elif kind == "K":
                        ac.wait_ge(s["k_f"], at(n, KD, j + 1))
                        ac.activation(k_hi[:, j, :], kf[:, j, :], ACT.Copy).then_inc(s["ks_hi"], 1)
                    elif kind == "VG":
                        ac.wait_ge(s["vg_f"], at(n, NT, j + 1))
                        ac.activation(v_hi[:, j, :], vg[:, j, 0:D], ACT.Copy).then_inc(s["vs_hi"], 1)
                    elif kind == "SIG":
                        log_sigmoid_exp(n, 2, j + 1, sgm[:, 2 * j:2 * j + 2, :], "g_u", "g_s1",
                                        "g_s2", "g_s3")
                    elif kind == "SC":
                        ac.wait_ge(s["SC_full"], at(n, NT, j + 1))
                        ac.activation(kt_hi[:, :], turn.rearrange("p a b -> p (a b)"),
                                      ACT.Copy).then_inc(s["kts_hi"], 1)
                    elif kind == "SS":
                        ac.wait_ge(s["a_m"], at(n, NT, j + 1))
                        ac.activation(a_hi[:, :, :, :], a_f[:, :, :, :], ACT.Copy).then_inc(s["as_hi"], 1)
                    elif kind == "ST":
                        ac.wait_ge(s["sr_f"], at(n, NT, j + 1))
                        ac.activation(Sr_hi[:, :, :], Sr[:, :, :], ACT.Copy).then_inc(s["srs_hi"], 1)
                    elif kind == "AV":
                        ac.wait_ge(s["KV_full"], at(n, NT, j + 1))
                        if isinstance(n, int) and n == 0 and j == 0:
                            pass
                        else:
                            ac.wait_ge(s["y_2"], at(n, NT, j))
                        ac.activation(y1[:, :], okv[:, 0, :, :].rearrange("p a b -> p (a b)"),
                                      ACT.Square).then_inc(s["o_sq"], 1)
                    elif kind == "YT":
                        ac.wait_ge(s["YT_full"], at(n, NT, j + 1))
                        ac.activation(y_hi[:, :, :], turn, ACT.Copy).then_inc(s["ys_hi"], 1)
                    elif kind == "XT":
                        ac.wait_ge(s["XT_full"], at(n, NT, j + 1))
                        ac.activation(x2_hi[:, :, j * P:(j + 1) * P], turn, ACT.Copy)\
                          .then_inc(s["x2s_hi"], 1)
                    elif kind == "FC":
                        ac.wait_ge(s["FC_full"], at(n, MH, j + 1))
                        ac.activation(ring_f[:, j % 2, 0, :], bank(kind, j, of_before), ACT.Relu,
                                      scale=fc_scale[:, j:j + 1]).then_inc(s["fc_act"], 1)
                        ac.wait_ge(s["fc_act"], at(n, MH, j + 1))
                        ac.activation(ring_hi[:, j % 2, :], ring_f[:, j % 2, 0, :], ACT.Square)\
                          .then_inc(s["fc_hi"], 1)
                        if j % 2:
                            ac.activation(ring_f[:, j % 2, 1, :], ring_f[:, j % 2, 0, :], ACT.Square)\
                              .then_inc(s["fc_h_odd"], 1)
                    elif kind == "PU":
                        log_sigmoid_exp(n, 1, 1, sgm[:, :, :], "f_u", "f_1", "f_2", "f_3")
                    elif kind == "W1":
                        ac.wait_ge(s["W1_full"], at(n, M1, j + 1))
                        ac.activation(ring_f[:, j % 2, 0, :], bank(kind, j, of_before), ACT.Identity,
                                      bias=b1_bias[:, j:j + 1]).then_inc(s["w_u"], 1)
                    elif kind == "WL":
                        ac.wait_ge(s["w_l"], at(n, M1, j + 1))
                        ac.activation(ring_hi[:, j % 2, :], ring_f[:, j % 2, 0, :], ACT.Square)\
                          .then_inc(s["ws_hi"], 1)
                        if j % 2:
                            ac.activation(ring_f[:, j % 2, 1, :], ring_f[:, j % 2, 0, :], ACT.Square)\
                              .then_inc(s["w_h_odd"], 1)

            ac.wait_ge(s["w_ready"], 1)
            step(0, True, False)
            with ac.Fori(1, NB) as n:
                step(n, True, True)
            step(NB, False, True)

        @block.vector
        def _(ve):
            own = [0]

            def token_stats(n):
                ve.wait_ge(s["x_dma"], at(n, 16, 16))
                for t in range(NT):
                    ve.bn_stats(bn[:, t, :], x_in[:, t, :]).then_inc(s["bn_ok"], 1)
                ve.wait_ge(s["bn_ok"], at(n, NT, NT))
                ve.memset(pad, 0.0)
                for t in range(NT):
                    i = ve.bn_aggr(mv[:, t, :], bn[:, t, :])
                i.then_inc(s["mv_ok"], 1)

            def normed(n):
                ve.wait_ge(s["ln_g"], at(n, 2, 2))
                for t in range(NT):
                    i = ve.tensor_scalar(x_hat[:, t, :], x_in[:, t, :], mv[:, t, 0:1],
                                         st[:, 6, t:t + 1], ALU.subtract, ALU.mult)
                i.then_inc(s["xh"], 1)

            for q in range(4):
                rows = slice(32 * q, 32 * q + 32)
                ve.memset(sign_hi[rows, :], -1.0 if q % 2 else 1.0)
                ve.memset(is_lo[rows, :], float(q % 2))
            ve.memset(pair_mask[:, :], 0.0).then_inc(s["fold1"], 1)
            ve.memset(keep[:, :], 1.0).then_inc(s["fold1"], 1)
            ve.wait_ge(s["fold1"], 2)
            ve.memset(pair_mask[0:DK, 0:DK], 1.0)
            ve.memset(pair_mask[DK:P, DK:P], 1.0)
            ve.memset(keep[:, :].rearrange("p (b m) -> p b m", b=B)[:, :, 0], 0.0)\
              .then_inc(s["w_cst"], 1)
            token_stats(0)

            wfc = vg[:, :, :].rearrange("p t (a d) -> p (t a) d", a=2)
            wpj = ring_f[:, :, :, :].rearrange("p a b n -> p a (b n)")
            ve.wait_ge(s["ld_fc"], 16)
            ve.tensor_reduce(fc_half, wfc, AX.X, ALU.add, apply_absolute_value=True).then_inc(s["fc_s"], 1)
            ve.wait_ge(s["fc_s"], 1)
            ve.tensor_scalar(fc_scale, fc_half, 1.0 / D, EPS, ALU.mult, ALU.max).then_inc(s["fc_s"], 1)
            ve.wait_ge(s["fc_s"], 2)
            ve.tensor_scalar(fc_nhalf, fc_scale, -0.5, None, ALU.mult).then_inc(s["fc_s"], 1)
            ve.tensor_scalar(fc_half, fc_scale, 0.5, None, ALU.mult)
            ve.reciprocal(fc_g, fc_scale).then_inc(s["fc_s"], 1)
            normed(0)
            ve.wait_ge(s["ld_pj"], 16)
            ve.tensor_reduce(pj_half, wpj, AX.X, ALU.add, apply_absolute_value=True).then_inc(s["pj_s"], 1)
            ve.wait_ge(s["pj_s"], 1)
            ve.tensor_scalar(pj_scale, pj_half, 1.0 / FH, EPS, ALU.mult, ALU.max).then_inc(s["pj_s"], 1)
            ve.wait_ge(s["pj_s"], 2)
            ve.tensor_scalar(pj_nhalf, pj_scale, -0.5, None, ALU.mult).then_inc(s["pj_s"], 1)
            ve.tensor_scalar(pj_half, pj_scale, 0.5, None, ALU.mult).then_inc(s["pj_s"], 1)
            ve.wait_ge(s["fc_s"], 4)
            for m in range(MH):
                ve.wait_ge(s["fc_a"], m + 1)
                ve.scalar_tensor_tensor(wfc[:, m, :], wfc[:, m, :], fc_half[:, m:m + 1],
                                        f(fc_neg[m // 4][:, m % 4, :]), ALU.is_gt,
                                        ALU.subtract).then_inc(s["fc_t"], 1)
            ve.wait_ge(s["pj_s"], 4)
            ve.wait_ge(s["ident_ok"], 2)
            for m in range(KD):
                i = ve.tensor_scalar(x_res[:, 2 + m, 0:P], ident[:, :], 0.0, pj_scale[:, m:m + 1],
                                     ALU.mult, ALU.add)
            i.then_inc(s["pj_s2"], 1)
            for m in range(KD):
                ve.wait_ge(s["pj_a"], m + 1)
                ve.scalar_tensor_tensor(wpj[:, m, :], wpj[:, m, :], pj_half[:, m:m + 1], f(pj_neg[m]),
                                        ALU.is_gt, ALU.subtract).then_inc(s["pj_t"], 1)


            ve.wait_ge(s["cols_mm"], 1)
            ve.tensor_copy(cols[:, 0:NV], proj[:, 0, 0:NV]).then_inc(s["cols_ok"], 1)
            ve.wait_ge(s["cols_ok"], 1)

            ve.wait_ge(s["ld_small"], 13 * 16)
            ve.tensor_scalar(fc_g, fc_g, gatec, None, ALU.mult).then_inc(s["fc_s"], 1)

            g1 = xn0[:, 0, 0:KD * LOW].rearrange("p (k r) -> p k r", k=KD)
            wl_st = xn0[:, 3, :].rearrange("p (k n) -> p k n", k=KD)
            lraw = ffn[:, 2, :].rearrange("p (k n) -> p k n", k=KD)
            ve.wait_ge(s["l_vt"], 1)
            ve.wait_ge(s["zeroed"], 2)
            ve.tensor_copy(wl_st, turn).then_inc(s["l_f"], 1)
            ve.wait_ge(s["l_f"], 1)
            for k in range(KD):
                for q in range(4):
                    ve.tensor_scalar(wl_st[:, k, 32 * q:32 * q + LOW], g1[:, k, :], l1w[:, k:k + 1],
                                     None, ALU.mult)
                    i = ve.tensor_copy(lraw[:, k, 32 * q:32 * q + LOW], g1[:, k, :])
            i.then_inc(s["l_w"], 1)
            for k in range(KD):
                i = ve.tensor_scalar(x_res[:, k, 0:P], ident[:, :], 0.0, l1b[:, k:k + 1], ALU.mult,
                                     ALU.add)
            i.then_inc(s["bias_b"], 1)

            ve.wait_ge(s["bias_mm"], 1)
            ve.tensor_copy(vg_bias[:, :], okv[:, :, :, :].rearrange("p a b c -> p (a b c)")).then_inc(s["bias_ok"], 1)
            ve.tensor_scalar(qk_bias[:, 0:KD], proj[:, 0, 0:KD], DK ** -0.5, None, ALU.mult)
            ve.tensor_copy(qk_bias[:, KD:2 * KD], proj[:, 0, KD:2 * KD]).then_inc(s["bias_ok"], 1)
            for k in range(KD):
                ve.tensor_scalar(qf[:, k, 0:D], qf[:, k, 0:D], l1w[:, k:k + 1], DK ** -0.5, ALU.mult, ALU.mult)
                i = ve.tensor_scalar(qf[:, k, D:2 * D], qf[:, k, D:2 * D], l1w[:, k:k + 1], None, ALU.mult)
            i.then_inc(s["fold_qk"], 1)
            for k in range(KD):
                i = ve.tensor_scalar(kf[:, k, :], kf[:, k, :], l1w[:, k:k + 1], None, ALU.mult)
            i.then_inc(s["fold_vg"], 1)
            ve.wait_ge(s["ld_wo"], 16)
            ve.tensor_scalar(x1[:, 0:2, :], x1[:, 0:2, :], rmsc, DK ** 0.5, ALU.mult, ALU.mult).then_inc(s["fold_wo"], 1)
            ve.wait_ge(s["lb_mm"], 1)
            ve.tensor_copy(lb, proj[:, 1, 0:1]).then_inc(s["lb_ok"], 1)
            ve.wait_ge(s["lb_ok"], 1)
            ve.tensor_tensor(lb_lo, lb, is_lo, ALU.mult)
            ve.tensor_scalar(bz_up, bz, CLAMP, None, ALU.add)
            ve.wait_ge(s["ld_low"], 8 * 16)
            ve.tensor_copy(low_hi[:, 0:D], sgm[:, 1, :]).then_inc(s["z_w"], 1)
            ve.wait_ge(s["z_w"], 1)
            ve.tensor_copy(wz[0:64, :], f(low_hi[0:64, 0:D]))
            ve.tensor_tensor(wz[64:P, :], sgm[64:P, 1, :], f(low_hi[64:P, 0:D]), ALU.subtract)

            gflat = gates[:, :, :, :].rearrange("p a b n -> p (a b n)")
            w1_st = gflat[:, 0:KD * F1].rearrange("p (k n) -> p k n", k=KD)
            w2_st = gflat[:, KD * F1:2 * KD * F1].rearrange("p (k n) -> p k n", k=M1)
            ve.wait_ge(s["bias_mm"], 2)
            ve.tensor_tensor(b1_bias, proj[:, 1, 8:8 + M1], b1c, ALU.add).then_inc(s["bias_ok"], 1)
            for k in range(KD):
                i = ve.tensor_scalar(w1_st[:, k, :], w1_st[:, k, :], l2w[:, k:k + 1], None, ALU.mult)
            i.then_inc(s["fold_w1"], 1)

            for i, (lo, w, hi) in enumerate((
                    (wl_lo[:, :, :], wl_st, wl_hi[:, :, :]), (wqk_lo[:, :, :], qf[:, :, :], wqk_hi[:, :, :]),
                    (wvg_lo[:, :, :], kf[:, :, :], wvg_hi[:, :, :]))):
                ve.wait_ge(s["w_hi"], i + 1)
                ve.tensor_tensor(lo, w, f(hi), ALU.subtract)

            ve.wait_ge(s["u_t"], 1)
            uT = x_in[0:LOW, :, :].rearrange("p t d -> p (t d)")
            for i in range(2):
                j = ve.tensor_copy(uT[:, i * TB:(i + 1) * TB], acc[i][0:LOW, :, :].rearrange("p a b -> p (a b)"))
            j.then_inc(s["u_tc"], 1)
            ve.wait_ge(s["m_mm"], 1)
            mf = xn0[:, 0, 0:MH * LOW].rearrange("p (m r) -> p m r", m=MH)
            mh = low_hi[:, 0:MH * LOW].rearrange("p (m r) -> p m r", m=MH)
            ve.wait_ge(s["fc_s"], 5)
            ve.tensor_tensor(mf, okv[:, 0, 0, :].rearrange("p (m r) -> p m r", m=MH),
                             fc_g.rearrange("p (m a) -> p m a", a=1).broadcast_to([P, MH, LOW]), ALU.mult).then_inc(s["m_f"], 1)
            ve.wait_ge(s["m_f"], 1)
            ve.tensor_copy(mh, mf).then_inc(s["m_hi"], 1)
            ve.wait_ge(s["m_hi"], 1)
            m_rep = vg[:, :, :].rearrange("p t (a d) -> p (t a) d", a=2)[:, :, 0:P]
            ve.wait_ge(s["tp_full"], 4)
            ve.memset(m_rep, 0.0).then_inc(s["m_rep"], 1)
            ve.wait_ge(s["m_rep"], 1)
            for q in range(4):
                dst = m_rep[:, :, 32 * q + LOW:32 * q + 2 * LOW]
                if q < 2:
                    ve.tensor_copy(dst, f(mh))
                else:
                    i = ve.tensor_tensor(dst, mf, f(mh), ALU.subtract)
            i.then_inc(s["m_rep"], 1)
            ve.wait_ge(s["bias_mm"], 3)
            ve.tensor_copy(pj_scale_row[:, :], turn.rearrange("p a b -> p (a b)")).then_inc(s["bias_ok"], 1)
            ve.wait_ge(s["lo_done"], 3)
            ve.wait_ge(s["tp_free"], 10)
            ve.wait_ge(s["bias_ok"], 4)
            ve.engine_nop().then_inc(s["w_ready"], 1)

            def step(step_n, front, back):
                stages = stages_of(front, back)

                def bank(*stage):
                    return ring[tenant(stages, stage, RING_STAGES, RING)[0]][:, :]

                for kind, j, of_before in stages_of(front, back, "ve"):
                    n = step_n - 1 if of_before else step_n
                    if kind == "LNA":
                        token_stats(n + 1)
                    elif kind == "LNC":
                        normed(n + 1)
                    elif kind == "XN":
                        ve.tensor_copy(rr_c[:, :], st[:, 4, :])
                        for t in range(NT):
                            i = ve.tensor_scalar(xn0[:, t, :], x_hat[:, t, :], st[:, 7, t:t + 1], None,
                                                 ALU.mult)
                        i.then_inc(s["xn_ok"], 1)
                    elif kind == "T":
                        ve.wait_ge(s["x_hi"], at(n, KD, j + 1))
                        ve.tensor_tensor(xT_lo[:, j, :], bank(kind, j, of_before), f(xT_hi[:, j, :]),
                                         ALU.subtract).then_inc(s["x_lo"], 1)
                    elif kind == "L":
                        ve.wait_ge(s["l_ev"], at(n, 1, 1))
                        ve.scalar_tensor_tensor(low[:, :], f(low_hi[:, :]), sign_hi, low_f, ALU.mult,
                                                ALU.add).then_inc(s["p_ready"], 1)
                    elif kind == "Z":
                        ve.wait_ge(s["Z_full"], at(n, KD, j + 1))
                        ve.tensor_scalar(ug[:, j, :], bank(kind, j, of_before), bz[:, j:j + 1], -CLAMP, ALU.add,
                                         ALU.max).then_inc(s["z_u"], 1)
                        ve.tensor_scalar(wgt[:, j, :], bank(kind, j, of_before), bz_up[:, j:j + 1], 0.0, ALU.add,
                                         ALU.min).then_inc(s["z_w2"], 1)
                    elif kind == "SCAN":
                        ve.wait_ge(s["z_w2"], at(n, KD, j + 1))
                        ve.wait_ge(s["z_l"], at(n, KD, j + 1))
                        for c in range(NT):
                            part = slice(c * P, (c + 1) * P)
                            i = ve.tensor_tensor_scan(G[:, j, part], wgt[:, j, part], ug[:, j, part],
                                                      0.0, ALU.add, ALU.subtract)
                        i.then_inc(s["g_sc"], 1)
                        ve.wait_ge(s["g_sc"], at(n, KD, j + 1))
                        gc = G[:, j, :].rearrange("p (c t) -> p c t", t=P)
                        ve.tensor_tensor(wgt[:, j, :].rearrange("p (c t) -> p c t", t=P), gc,
                                         gc[:, :, MID:MID + 1].broadcast_to([P, NT, P]),
                                         ALU.subtract).then_inc(s["g_rel"], 1)
                    elif kind == "DEC":
                        ve.wait_ge(s["e_r"], at(n, KD, KD))
                        ve.tensor_scalar(dec_r[:, :, 0], dec_r[:, :, 0],
                                         keep[:, bass.ds(n, 1)] if not isinstance(n, int)
                                         else keep[:, n:n + 1], None, ALU.mult).then_inc(s["dk"], 1)
                        ve.wait_ge(s["dk"], at(n, 1, 1))
                        ve.wait_ge(s["e_p"], at(n, KD, KD))
                        ends = ug[:, :, :].rearrange("p k (c t) -> p k c t", t=P)[:, :, :, P - 1]
                        ve.tensor_tensor(dec_t[:, :, :], dec_r[:, :, :], ends,
                                         ALU.mult).then_inc(s["dec_ok"], 1)
                    elif kind == "Q":
                        ve.wait_ge(s["Q_full"], at(n, KD, j + 1))
                        ve.wait_ge(s["e_p"], at(n, KD, j + 1))
                        ve.scalar_tensor_tensor(qf[:, j, :], bank(kind, j, of_before), qk_bias[:, j:j + 1],
                                                ug[:, j, :], ALU.add, ALU.mult).then_inc(s["q_f"], 1)
                    elif kind == "K":
                        ve.wait_ge(s["K_full"], at(n, KD, j + 1))
                        ve.wait_ge(s["e_m"], at(n, KD, j + 1))
                        ve.scalar_tensor_tensor(kf[:, j, :], bank(kind, j, of_before),
                                                qk_bias[:, KD + j:KD + j + 1], wgt[:, j, :],
                                                ALU.add, ALU.mult).then_inc(s["k_f"], 1)
                    elif kind == "VG":
                        ve.wait_ge(s["VG_full"], at(n, NT, j + 1))
                        ve.tensor_tensor(vg[:, j, :], bank(kind, j, of_before), vg_bias[:, :],
                                         ALU.add).then_inc(s["vg_f"], 1)
                    elif kind == "SIG":
                        two = slice(2 * j, 2 * j + 2)
                        ve.wait_ge(s["vg_f"], at(n, NT, 2 * j + 2))
                        if j == 0 and not (isinstance(n, int) and n == 0):
                            ve.wait_ge(s["f_g"], at(n, 1, 0))
                        ve.tensor_scalar(sgm[:, two, :], vg[:, two, D:2 * D], -CLAMP, None,
                                         ALU.max).then_inc(s["g_u"], 1)
                    elif kind == "PU":
                        ve.wait_ge(s["f_f"], at(n, NT, NT))
                        ve.tensor_scalar(sgm[:, :, :], ffn[:, :, :], -CLAMP, None,
                                         ALU.max).then_inc(s["f_u"], 1)
                    elif kind == "SC":
                        ve.wait_ge(s["kts_hi"], at(n, NT, j + 1))
                        ve.tensor_tensor(kt_lo[:, :], turn.rearrange("p a b -> p (a b)"),
                                         f(kt_hi[:, :]), ALU.subtract).then_inc(s["kts_lo"], 1)
                        ve.tensor_tensor(a_f[:, :, :, :].rearrange("p a b t -> p (a b) t"),
                                         both[:, :, :, :, :].rearrange("p a r b t -> p (a r) b t")[:, 0:3:2],
                                         mask[:, :].unsqueeze(1).broadcast_to([P, H, P]),
                                         ALU.mult).then_inc(s["a_m"], 1)
                    elif kind == "AV":
                        ve.wait_ge(s["o_sq"], at(n, NT, j + 1))
                        ve.tensor_reduce(ss[:, :], y1[:, :].rearrange("p (h d) -> p h d", h=H), AX.X,
                                         ALU.add).then_inc(s["o_ss"], 1)
                        ve.wait_ge(s["KV_full"], at(n, NT, j + 1))
                        for m in range(KD):
                            end = ug[:, m, (j + 1) * P - 1:(j + 1) * P]
                            i = ve.scalar_tensor_tensor(kv[:, m, :], okv[:, 1, m, :], end,
                                                        pair_mask[:, :], ALU.mult, ALU.mult)
                        i.then_inc(s["kv_ev"], 1)
                        ve.wait_ge(s["kv_ev"], at(n, NT, j + 1))
                        ve.wait_ge(s["sd_f"], at(n, NT, j + 1))
                        ve.tensor_tensor(S[:, :, :], Sd[:, :, :], kv[:, :, :],
                                         ALU.add).then_inc(s["s_new"], 1)
                    elif kind == "AY":
                        ve.wait_ge(s["o_r"], at(n, NT, j + 1))
                        ve.tensor_tensor(y1[:, :].rearrange("p (h d) -> p h d", h=H),
                                         okv[:, 0, :, :].rearrange("p a (b d) -> p (a b) d", d=DK),
                                         ro[:, 1, :].unsqueeze(2).broadcast_to([P, H, DK]),
                                         ALU.mult).then_inc(s["y_1"], 1)
                    elif kind == "YT":
                        ve.wait_ge(s["ys_hi"], at(n, NT, j + 1))
                        ve.tensor_tensor(y_lo[:, :, :], turn, f(y_hi[:, :, :]),
                                         ALU.subtract).then_inc(s["ys_lo"], 1)
                    elif kind == "WO":
                        ve.wait_ge(s["WO_full"], at(n, NT, j + 1))
                        if j == 0:
                            ve.wait_ge(s["xn_ok"], at(n, 1, 1))
                            if not (isinstance(n, int) and n == 0):
                                ve.wait_ge(s["out_ok"], at(n, 1, 0))
                        ve.tensor_tensor(x1[:, j, :], proj.rearrange("p a b -> p (a b)"),
                                         xn0[:, j, :], ALU.add).then_inc(s["x_1"], 1)
                        ve.wait_ge(s["x_1"], at(n, NT, j + 1))
                        ve.bn_stats(bn2[:, :], x1[:, j, :]).then_inc(s["x1_bn"], 1)
                        ve.wait_ge(s["x1_bn"], at(n, NT, j + 1))
                        ve.memset(pad, 0.0)
                        ve.bn_aggr(mv2[:, :], bn2[:, :]).then_inc(s["x1_mv"], 1)
                    elif kind == "WN":
                        ve.wait_ge(s["x1_r"], at(n, NT, j + 1))
                        ve.tensor_scalar(xn2[:, :], x1[:, j, :], mv2[:, 0:1], st2[:, 1:2],
                                         ALU.subtract, ALU.mult).then_inc(s["xn2_f"], 1)
                    elif kind == "XT":
                        ve.wait_ge(s["x2s_hi"], at(n, NT, j + 1))
                        ve.tensor_tensor(x2_lo[:, :, j * P:(j + 1) * P], turn,
                                         f(x2_hi[:, :, j * P:(j + 1) * P]),
                                         ALU.subtract).then_inc(s["x2s_lo"], 1)
                    elif kind == "FL":
                        if j % 2:
                            ve.wait_ge(s["fc_h_odd"], at(n, MH // 2, j // 2 + 1))
                        else:
                            ve.wait_ge(s["fc_hi"], at(n, MH, j + 1))
                            ve.wait_ge(s["fc_h"], at(n, MH // 2, j // 2 + 1))
                        ve.tensor_tensor(ring_lo[:, j % 2, :], ring_f[:, j % 2, 1, :],
                                         f(ring_hi[:, j % 2, :]), ALU.subtract).then_inc(s["fc_lo"], 1)
                    elif kind == "PF":
                        ve.wait_ge(s["PJ_full"], at(n, 1, 1))
                        for t in range(NT):
                            ve.scalar_tensor_tensor(ffn[:, t, :], tile4(acc, t), rr_c[:, t:t + 1],
                                                    pj_scale_row[:, :], ALU.mult,
                                                    ALU.mult).then_inc(s["f_f"], 1)
                    elif kind == "W1":
                        ve.wait_ge(s["w_u"], at(n, M1, j + 1))
                        ve.scalar_tensor_tensor(ring_f[:, j % 2, 0, :], ring_f[:, j % 2, 0, :], 0.01,
                                                ring_f[:, j % 2, 0, :], ALU.mult,
                                                ALU.max).then_inc(s["w_l"], 1)
                    elif kind == "WL":
                        if j % 2:
                            ve.wait_ge(s["w_h_odd"], at(n, M1 // 2, j // 2 + 1))
                        else:
                            ve.wait_ge(s["ws_hi"], at(n, M1, j + 1))
                            ve.wait_ge(s["w_h"], at(n, M1 // 2, j // 2 + 1))
                        ve.tensor_tensor(ring_lo[:, j % 2, :], ring_f[:, j % 2, 1, :],
                                         f(ring_hi[:, j % 2, :]), ALU.subtract).then_inc(s["w_lo"], 1)
                    elif kind == "OUT":
                        ve.wait_ge(s["W2_full"], at(n, 1, 1))
                        ve.wait_ge(s["x1_b"], at(n, NT, NT))
                        for t in range(NT):
                            ve.tensor_tensor(x1[:, t, :], tile4(acc, t), x1[:, t, :],
                                             ALU.add).then_inc(s["s_f"], 1)

            step(0, True, False)
            with ve.Fori(1, NB) as n:
                step(n, True, True)
            step(NB, False, True)

        @block.tensor
        def _(pe):
            def split3(dst, l_hi, l_lo, r_hi, r_lo, start, stop):
                pe.matmul(dst, l_hi, r_hi, start=start, stop=False, skip_group_check=True)
                pe.matmul(dst, l_lo, r_hi, start=False, stop=False, skip_group_check=True)
                return pe.matmul(dst, l_hi, r_lo, start=False, stop=stop, skip_group_check=True)

            def turned(dst, src):
                return pe.transpose(dst, src, ident[:, :])

            wfc = vg[:, :, :].rearrange("p t (a d) -> p (t a) d", a=2)
            wpj = ring_f[:, :, :, :].rearrange("p a b n -> p a (b n)")

            def ternary(lo, hi):
                for i in range(lo, hi):
                    if i < 4:
                        pe.wait_ge(s["fc_t"], 4 * (i // 2) + 4)
                    else:
                        pe.wait_ge(s["pj_t"], KD)
                    if i >= RING:
                        pe.wait_ge(s["tp_free"], i + 1 - RING)
                    for q in range(4):
                        if i < 4:
                            m, k = 4 * (i // 2) + q, i % 2
                            src = wfc[:, m, k * P:(k + 1) * P]
                        else:
                            m, o = 2 * (i - 4) + q // 2, q % 2
                            src = wpj[:, o, m * P:(m + 1) * P]
                        j = turned(ring[i % RING][:, q * P:(q + 1) * P], src)
                    j.then_inc(s["tp_full"], 1)

            pe.wait_ge(s["ident_ok"], 2)
            ternary(0, 4)
            pe.wait_ge(s["ld_small"], 13 * 16)
            pe.transpose(proj[:, 0, 0:NV], xn0[0:NV, 2, P:2 * P], ident[0:NV, 0:NV]).then_inc(s["cols_mm"], 1)
            pe.wait_ge(s["ld_low"], 8 * 16)
            for k in range(KD):
                i = turned(turn[:, k, :], sgm[:, 0, k * P:(k + 1) * P])
            i.then_inc(s["l_vt"], 1)
            for m in range(MH):
                i = turned(acc[m // 4][0:LOW, (m % 4) // 2, (m % 2) * P:(m % 2 + 1) * P],
                           xn0[:, 1, m * LOW:(m + 1) * LOW])
            i.then_inc(s["u_t"], 1)
            pe.wait_ge(s["bias_b"], 1)
            pe.wait_ge(s["ld_qkvg"], 4 * 16)
            vgb = okv[:, :, :, :].rearrange("p a b c -> p (a b c)")
            for k in range(KD):
                pe.matmul(vgb, x_res[:, k, 0:P], kf[:, k, :], start=k == 0, stop=k == KD - 1)
            pe.wait_ge(s["cols_ok"], 1)
            for c in range(2 * KD):
                for k in range(KD):
                    i = pe.matmul(proj[:, 0, c:c + 1], qf[:, k, c * P:(c + 1) * P], l1b[:, k:k + 1],
                                  start=k == 0, stop=k == KD - 1)
            i.then_inc(s["bias_mm"], 1)
            pe.wait_ge(s["l_w"], 1)
            pe.wait_ge(s["bias_ok"], 2)
            for k in range(KD):
                i = pe.matmul(proj[:, 1, 0:1], ffn[:, 2, k * P:(k + 1) * P], l1b[:, k:k + 1],
                              start=k == 0, stop=k == KD - 1)
            i.then_inc(s["lb_mm"], 1)
            gflat = gates[:, :, :, :].rearrange("p a b n -> p (a b n)")
            pe.wait_ge(s["ld_w1"], 16)
            pe.wait_ge(s["lb_ok"], 1)
            for c in range(M1):
                for k in range(KD):
                    i = pe.matmul(proj[:, 1, 8 + c:9 + c], gflat[:, k * F1 + c * P:k * F1 + (c + 1) * P],
                                  l2b[:, k:k + 1], start=k == 0, stop=k == KD - 1)
            i.then_inc(s["bias_mm"], 1)
            ternary(4, 8)
            pe.wait_ge(s["pj_s2"], 1)
            for m in range(KD):
                i = pe.matmul(turn[:, m, :], x_res[:, 2 + m, 0:P], ident[:, :], start=True, stop=True)
            i.then_inc(s["bias_mm"], 1)
            pe.wait_ge(s["u_tc"], 1)
            pe.wait_ge(s["bias_ok"], 1)
            uT = x_in[0:LOW, :, :].rearrange("p t d -> p (t d)")
            for m in range(MH):
                i = pe.matmul(okv[:, 0, 0, m * LOW:(m + 1) * LOW], uT[:, m * P:(m + 1) * P],
                              xn0[0:LOW, 2, 0:LOW], start=True, stop=True)
            i.then_inc(s["m_mm"], 1)
            pe.wait_ge(s["m_rep"], 2)
            for i in range(2):
                pe.wait_ge(s["tp_free"], 6 + i)
                for q in range(4):
                    j = turned(ring[(8 + i) % RING][:, q * P:(q + 1) * P], wfc[:, 4 * i + q, 0:P])
                j.then_inc(s["tp_full"], 1)
            pe.wait_ge(s["w_ready"], 1)

            def step(step_n, front, back):
                stages = stages_of(front, back)
                for stage in stages:
                    kind, j, of_before = stage
                    n = step_n - 1 if of_before else step_n
                    if kind in RING_STAGES:
                        if kind == "T" and j == 0:
                            pe.wait_ge(s["xh"], at(n, 1, 1))
                        dst = ring[wait_tenant(pe, stages, stage, step_n, RING_STAGES, RING)][:, :]
                    for kinds in (PROJ_STAGES, TURN_STAGES):
                        if kind in kinds:
                            wait_tenant(pe, stages, stage, step_n, kinds, 1)
                    if kind == "T":
                        for t in range(NT):
                            i = turned(dst[:, t * P:(t + 1) * P], x_hat[:, t, j * P:(j + 1) * P])
                        i.then_inc(s["T_full"], 1)
                    elif kind == "L":
                        pe.wait_ge(s["x_lo"], at(n, KD, KD))
                        for k in range(KD):
                            i = split3(dst, wl_hi[:, k, :], wl_lo[:, k, :], xT_hi[:, k, :],
                                       xT_lo[:, k, :], k == 0, k == KD - 1)
                        i.then_inc(s["L_full"], 1)
                    elif kind == "Z":
                        if j == 0:
                            pe.wait_ge(s["p_ready"], at(n, 1, 1))
                        pe.matmul(dst, wz[:, j * P:(j + 1) * P], low[:, :], start=True, stop=True)\
                          .then_inc(s["Z_full"], 1)
                    elif kind in ("Q", "K"):
                        c = (j if kind == "Q" else KD + j) * P
                        for k in range(KD):
                            i = split3(dst, wqk_hi[:, k, c:c + P], wqk_lo[:, k, c:c + P],
                                       xT_hi[:, k, :], xT_lo[:, k, :], k == 0, k == KD - 1)
                        i.then_inc(s[kind + "_full"], 1)
                    elif kind == "VG":
                        if j == 0:
                            pe.wait_ge(s["x_lo"], at(n, KD, KD))
                        tok = slice(j * P, (j + 1) * P)
                        for k in range(KD):
                            i = split3(dst, xT_hi[:, k, tok], xT_lo[:, k, tok], wvg_hi[:, k, :],
                                       wvg_lo[:, k, :], k == 0, k == KD - 1)
                        i.then_inc(s["VG_full"], 1)
                    elif kind == "SC":
                        tok = slice(j * P, (j + 1) * P)
                        if j == 0:
                            pe.wait_ge(s["k_f"], at(n, KD, KD))
                        for m in range(KD):
                            i = turned(turn[:, m, :], kf[:, m, tok])
                        if j == 0:
                            pe.wait_ge(s["qs_lo"], at(n, KD, KD))
                            pe.wait_ge(s["ks_lo"], at(n, KD, KD))
                        for m in range(KD):
                            for a, (ks, qs) in enumerate(((k_hi, q_hi), (k_lo, q_hi), (k_hi, q_lo))):
                                for e in range(2):
                                    rows = slice(e * DK, (e + 1) * DK)
                                    i = pe.matmul(scores[:, e, m, :], ks[rows, m, tok],
                                                  qs[rows, m, tok], start=a == 0, stop=a == 2,
                                                  skip_group_check=True)
                        i.then_inc(s["SC_full"], 1)
                    elif kind == "AV":
                        pe.wait_ge(s["as_lo"], at(n, NT, j + 1))
                        pe.wait_ge(s["vs_lo"], at(n, NT, j + 1))
                        pe.wait_ge(s["srs_lo"], at(n, NT, j + 1))
                        if not (isinstance(n, int) and n == 0 and j == 0):
                            pe.wait_ge(s["y_1"], at(n, NT, j))
                        tok = slice(j * P, (j + 1) * P)
                        for m in range(KD):
                            for e in range(2):
                                h = 2 * m + e
                                split3(okv[:, 0, m, e * DK:(e + 1) * DK], a_hi[:, e, m, :], a_lo[:, e, m, :],
                                       v_hi[:, j, h * DK:(h + 1) * DK], v_lo[:, j, h * DK:(h + 1) * DK],
                                       e == 0, False)
                            i = split3(okv[:, 0, m, :], q_hi[:, m, tok], q_lo[:, m, tok],
                                       Sr_hi[:, m, :], Sr_lo[:, m, :], False, True)
                        pe.wait_ge(s["kts_lo"], at(n, NT, j + 1))
                        for m in range(KD):
                            c = slice(m * P, (m + 1) * P)
                            i = split3(okv[:, 1, m, :], kt_hi[:, c], kt_lo[:, c], v_hi[:, j, c],
                                       v_lo[:, j, c], True, True)
                        i.then_inc(s["KV_full"], 1)
                    elif kind == "YT":
                        pe.wait_ge(s["y_2"], at(n, NT, j + 1))
                        for m in range(KD):
                            i = turned(turn[:, m, :], y2[:, m * P:(m + 1) * P])
                        i.then_inc(s["YT_full"], 1)
                    elif kind == "WO":
                        pe.wait_ge(s["ys_lo"], at(n, NT, j + 1))
                        o = proj.rearrange("p a b -> p (a b)")
                        for k in range(KD):
                            i = split3(o, y_hi[:, k, :], y_lo[:, k, :], wo_hi[:, k, :], wo_lo[:, k, :],
                                       k == 0, k == KD - 1)
                        i.then_inc(s["WO_full"], 1)
                    elif kind == "XT":
                        pe.wait_ge(s["xn2_f"], at(n, NT, j + 1))
                        for m in range(KD):
                            i = turned(turn[:, m, :], xn2[:, m * P:(m + 1) * P])
                        i.then_inc(s["XT_full"], 1)
                    elif kind == "FC":
                        c = slice(j * P, (j + 1) * P)
                        pe.matmul(dst, wu[:, c], low[:, :], start=True, stop=False, skip_group_check=True)
                        for k in range(KD):
                            pe.matmul(dst, tern_fc[:, k, c], xT_hi[:, k, :], start=False, stop=False,
                                      skip_group_check=True)
                            i = pe.matmul(dst, tern_fc[:, k, c], xT_lo[:, k, :], start=False,
                                          stop=k == KD - 1, skip_group_check=True)
                        i.then_inc(s["FC_full"], 1)
                    elif kind == "PJ":
                        pe.wait_ge(s["fc_lo"], at(n, MH, j + 1))
                        if j == 0 and not (isinstance(n, int) and n == 0):
                            pe.wait_ge(s["s_f"], at(n, NT, 0))
                        for t in range(NT):
                            tok = slice(t * P, (t + 1) * P)
                            pe.matmul(tile4(acc, t), ring_hi[:, j % 2, tok], tern_pj[:, j, :],
                                      start=j == 0 and t % 2 == 0, stop=False, skip_group_check=True)
                            i = pe.matmul(tile4(acc, t), ring_lo[:, j % 2, tok], tern_pj[:, j, :],
                                          start=False, stop=j == MH - 1, skip_group_check=True)
                        if j == MH - 1:
                            i.then_inc(s["PJ_full"], 1)
                    elif kind == "W1":
                        if j == 0:
                            pe.wait_ge(s["x2s_lo"], at(n, NT, NT))
                        c = slice(j * P, (j + 1) * P)
                        for k in range(KD):
                            i = split3(dst, w1_hi[:, k, c], w1_lo[:, k, c], x2_hi[:, k, :],
                                       x2_lo[:, k, :], k == 0, k == KD - 1)
                        i.then_inc(s["W1_full"], 1)
                    elif kind == "W2":
                        pe.wait_ge(s["w_lo"], at(n, M1, j + 1))
                        if j == 0:
                            pe.wait_ge(s["f_f"], at(n, NT, NT))
                        for t in range(NT):
                            tok = slice(t * P, (t + 1) * P)
                            i = split3(tile4(acc, t), ring_hi[:, j % 2, tok], ring_lo[:, j % 2, tok],
                                       w2_hi[:, j, :], w2_lo[:, j, :], j == 0 and t % 2 == 0,
                                       j == M1 - 1)
                        if j == M1 - 1:
                            i.then_inc(s["W2_full"], 1)

            step(0, True, False)
            with pe.Fori(1, NB) as n:
                step(n, True, True)
            step(NB, False, True)


_ATTN = ["x", "ln1_w", "ln1_b", "Wq", "Wk", "Wv", "Wg", "Wgk1", "Wgk2", "bgk2", "rms_w", "Wo",
         "ln2_w", "ln2_b", "W1", "b1", "W2", "b2"]
_FFN = ["fast_b", "w_fc", "w_proj", "u", "v", "gate"]
_INS = [f"L0_attn_{n}" for n in _ATTN] + [f"L0_ffn_{n}" for n in _FFN]


def kernel(**inputs):
    import numpy as _np
    import concourse.bacc as _bacc
    from concourse import mybir as _mybir
    from concourse.bass_utils import run_bass_kernel_spmd as _run

    nc = _bacc.Bacc("TRN2", target_bir_lowering=False, num_devices=1)
    arrays, args = {}, []
    for name in _INS:
        a = _np.ascontiguousarray(inputs[name])
        if a.ndim == 0:
            a = a.reshape(1)
        arrays[f"in_{name}"] = a
        args.append(nc.dram_tensor(f"in_{name}", a.shape, _mybir.dt.from_np(a.dtype),
                                   kind="ExternalInput").ap())
    out = nc.dram_tensor("out", (B, T, D), _mybir.dt.float32, kind="ExternalOutput").ap()
    recurrent_block_kernel(nc, *args, out)
    r = _run(nc, [arrays], core_ids=[0])
    return r.results[0]["out"]
```

```python
from contextlib import ExitStack

import concourse.bass as bass
from concourse import mybir

F32 = mybir.dt.float32
F32R = mybir.dt.float32r
ACT = mybir.ActivationFunctionType
ALU = mybir.AluOpType
AX = mybir.AxisListType

P = 128
B, T, D = 4, 1024, 256
H, DK = 4, 64
LOW = 16
F1, FH = 3 * D, 4 * D
NT = 4
TB = NT * P
NB = B * T // TB
KD = D // P
M1, MH = F1 // P, FH // P
MID = P // 2 - 1
EPS = 1e-5
SPAN = -64.0
GLN = 16.0
CLAMP = 40.0

ORDERS = {
    "pe": """
        T0 YT3b T1 WO3b L0 VG0 XT3b VG1 Z0 VG2 W10b Z1 W11b Q0 K0 Q1 W20b W12b K1 W21b W13b VG3
        W22b SC0 W14b W23b W15b AV0 SC1 W24b W25b FC0 FC1 YT0 AV1 PJ0 FC2 PJ1 SC2 FC3 PJ2 WO0 FC4
        YT1 AV2 SC3 PJ3 FC5 XT0 WO1 PJ4 FC6 YT2 PJ5 FC7 XT1 WO2 AV3 XT2 PJ6 PJ7
    """,
    "ac": """
        T0 YT3b T1 L0 XT3b PU0b Z0 W10b Z1 WL0b W11b EX0 WL1b K0 Q0 W12b EX1 WL2b Q1 K1 VG0 VG1
        W13b SIG0 WL3b VG2 SC0 ST0 SS0 W14b WL4b W15b VG3 AV0 WL5b SC1 ST1 SS1 FC0 FC1 AV1 YT0
        SIG1 FC2 SC2 ST2 SS2 FC3 YT1 FC4 AV2 SC3 SS3 XT0 FC5 ST3 YT2 FC6 XT1 FC7 AV3 XT2
    """,
    "ve": """
        T0 YT3b T1 WO3b PU0b WN3b L0 VG0 XT3b VG1 Z0 VG2 Z1 W10b SCAN0 WL0b Q0 W11b K0 SCAN1 WL1b
        W12b Q1 K1 DEC0 SIG0 WL2b W13b WL3b SC0 VG3 SIG1 W14b XN0 WL4b W15b AV0 WL5b SC1 AY0 OUT0b
        FL0 LNA0 YT0 FL1 AV1 AY1 FL2 SC2 WO0 FL3 YT1 WN0 AV2 SC3 FL4 AY2 WO1 XT0 FL5 YT2 WN1 LNC0
        XT1 WO2 FL6 FL7 WN2 AV3 XT2 AY3 PF0
    """,
    "gp": """
        WP3b PG0b WN3b Q0 K0 Q1 K1 VG0 ST0 VG1 SS0 SL0 VG2 VG3 AP0 ST1 AY0 SS1 OUT0b AP1 ST2 AY1
        SS2 WP0 LNB0 AP2 SL1 WN0 AY2 ST3 WP1 SS3 WP2 AP3 WN1 AY3 WN2
    """,
}


def parsed(name):
    back = name.endswith("b")
    name = name.rstrip("b")
    return name[:-1], int(name[-1]), back


ORDERS = {engine: [parsed(name) for name in order.split()] for engine, order in ORDERS.items()}
STAGES = {stage for order in ORDERS.values() for stage in order}
PER = {k: sum(s[0] == k for s in STAGES) for k, _, _ in STAGES}
RING_STAGES = ("T", "L", "Z", "Q", "K", "VG", "W1", "FC")
RING = 3
CHUNK_STAGES = ("SCAN", "EX", "DEC", "Q", "K", "SC", "SS", "ST", "AV")
PROJ_STAGES = ("SC", "WO")
TURN_STAGES = ("SC", "YT", "XT")


def stages_of(front, back, engine="pe"):
    return [s for s in ORDERS[engine] if (back if s[2] else front)]


def tenant(stages, stage, kinds, banks):
    mine = [s for s in stages if s[0] in kinds]
    at = mine.index(stage)
    if at >= banks:
        return at % banks, mine[at - banks], False
    ends = [s for s in stages_of(True, False) if s[0] in kinds]
    return at % banks, ends[len(ends) - banks + at], True


def recurrent_block_kernel(nc, x, ln1_w, ln1_b, wq, wk, wv, wg, wgk1, wgk2, bgk2, rms_w, wo,
                           ln2_w, ln2_b, w1, b1, w2, b2, fast_b, w_fc, w_proj, u, v, gate, out):
    x_blocks = x.rearrange("b (m t p) d -> (b m) p t d", t=NT, p=P)
    out_blocks = out.rearrange("b (m t p) d -> (b m) p t d", t=NT, p=P)

    with ExitStack() as ctx:
        def sb(name, *shape, dt=F32):
            return ctx.enter_context(nc.sbuf_tensor(name, [P, *shape], dt))

        def sem(name):
            return ctx.enter_context(nc.semaphore(name))

        def f(ap):
            return ap.bitcast(F32)

        wqk_hi, wqk_lo = (sb(f"wqk_{s}", KD, 2 * D, dt=F32R) for s in ("hi", "lo"))
        wvg_hi, wvg_lo = (sb(f"wvg_{s}", KD, 2 * D, dt=F32R) for s in ("hi", "lo"))
        wl_hi, wl_lo = (sb(f"wl_{s}", KD, P, dt=F32R) for s in ("hi", "lo"))
        w1_hi, w1_lo = (sb(f"w1_{s}", KD, F1, dt=F32R) for s in ("hi", "lo"))
        w2_hi, w2_lo = (sb(f"w2_{s}", M1, D, dt=F32R) for s in ("hi", "lo"))
        wo_hi, wo_lo = (sb(f"wo_{s}", KD, D, dt=F32R) for s in ("hi", "lo"))
        wz = sb("wz", D, dt=F32R)
        wu = sb("wu", FH, dt=F32R)
        tern_fc = sb("tern_fc", KD, FH, dt=F32R)
        tern_pj = sb("tern_pj", MH, D, dt=F32R)
        ident, mask, pair_mask = sb("ident", P), sb("mask", P), sb("pair_mask", P)
        vg_bias, b2_row, pj_scale_row = sb("vg_bias", 2 * D), sb("b2_row", D), sb("pj_scale_row", D)
        cols = sb("cols", 64)
        c_at = [0]

        def col(n):
            c_at[0] += n
            return cols[:, c_at[0] - n:c_at[0]]

        l1w, l1b, l2w, l2b, bz, b1c, rmsc = col(KD), col(KD), col(KD), col(KD), col(KD), col(M1), col(1)
        NV = c_at[0]
        gatec, qk_bias, b1_bias = col(1), col(2 * KD), col(M1)
        bz_up = col(KD)
        lb, lb_lo, sign_hi, is_lo = col(1), col(1), col(1), col(1)
        keep = sb("keep", 2 * NB)
        small = sb("small", 64)
        s_at = [0]

        def tiny(n):
            s_at[0] += n
            return small[:, s_at[0] - n:s_at[0]]

        fc_scale, fc_half, fc_nhalf, fc_g = tiny(MH), tiny(MH), tiny(MH), tiny(MH)
        pj_scale, pj_half, pj_nhalf = tiny(KD), tiny(KD), tiny(KD)
        half_neg = tiny(NT)
        pad, tok_pad = tiny(1), tiny(1)
        g_mid = tiny(KD * NT)
        eps_col, eps_head = tiny(NT), tiny(H)

        x_in, x_hat, xn0 = sb("x_in", NT, D), sb("x_hat", NT, D), sb("xn0", NT, D)
        xT_hi, xT_lo = sb("xT_hi", KD, TB, dt=F32R), sb("xT_lo", KD, TB, dt=F32R)
        low = sb("low", TB, dt=F32R)
        gates = sb("gates", 3, KD, TB)
        ug, wgt, G = gates[:, 0], gates[:, 1], gates[:, 2]
        qf, kf = sb("qf", KD, TB), sb("kf", KD, TB)
        q_hi, q_lo = sb("q_hi", KD, TB, dt=F32R), sb("q_lo", KD, TB, dt=F32R)
        k_hi, k_lo = sb("k_hi", KD, TB, dt=F32R), sb("k_lo", KD, TB, dt=F32R)
        low_hi, low_f = k_hi[:, 1], kf[:, 1]
        vg = sb("vg", NT, 2 * D)
        v_hi, v_lo = sb("v_hi", NT, D, dt=F32R), sb("v_lo", NT, D, dt=F32R)
        sgm = sb("sgm", NT, D)
        kt_hi, kt_lo = sb("kt_hi", D, dt=F32R), sb("kt_lo", D, dt=F32R)
        a_f = sb("a_f", 2, KD, P)
        a_hi, a_lo = sb("a_hi", 2, KD, P, dt=F32R), sb("a_lo", 2, KD, P, dt=F32R)
        y1, y2 = sb("y1", D), sb("y2", D)
        y_hi, y_lo = sb("y_hi", KD, P, dt=F32R), sb("y_lo", KD, P, dt=F32R)
        x1, xn2 = sb("x1", NT, D), sb("xn2", D)
        x2_hi, x2_lo = sb("x2_hi", KD, TB, dt=F32R), sb("x2_lo", KD, TB, dt=F32R)
        ring_f = sb("ring_f", 2, 2, TB)
        ring_hi, ring_lo = sb("ring_hi", 2, TB, dt=F32R), sb("ring_lo", 2, TB, dt=F32R)
        S, Sd, Sr, kv = sb("S", KD, P), sb("Sd", KD, P), sb("Sr", KD, P), sb("kv", KD, P)
        Sr_hi, Sr_lo = sb("Sr_hi", KD, P, dt=F32R), sb("Sr_lo", KD, P, dt=F32R)
        ffn, x_res = sb("ffn", NT, D), sb("x_res", NT, D)
        bn, mv = sb("bn", NT, 6), sb("mv", NT, 2)
        bn2, mv2, st2 = sb("bn2", 6), sb("mv2", 2), sb("st2", 2)
        st = sb("st", 8, NT)
        rr_c = sb("rr_c", NT)
        dec_r, dec_t = sb("dec_r", KD, NT), sb("dec_t", KD, NT)
        ss, ro = sb("ss", H), sb("ro", 2, H)
        lowest = sb("lowest", KD, NT)
        flag = sb("flag", 2)
        redo = sb("redo", 1, dt=mybir.dt.int32)
        fc_neg = [t[:, :, :].rearrange("p k (a d) -> p (k a) d", d=D) for t in (xT_hi, xT_lo)]
        pj_neg = [t[:, :, :].rearrange("p k n -> p (k n)") for t in (q_hi, q_lo)]
        tok_v = G
        tok_kv, tok_h, tok_qh = ring_f[:, 0, 0, :], ring_f[:, 0, 1, :], ring_f[:, 1, 0, :]
        tok_sel = a_f[:, 0, 0, :]
        tok_o = kf[:, :, :].rearrange("p k (a d) -> p (k a) d", d=D)
        mean = mv[:, :, 0]
        var = mv[:, :, 1]

        def pb(name, *shape):
            return ctx.enter_context(nc.psum_tensor(name, [P, *shape], F32))

        ring = [pb(f"ring{i}", TB) for i in range(RING)]
        acc = [pb(f"acc{i}", 2, D) for i in range(2)]
        okv = pb("okv", 2, KD, P)
        both = pb("both", 2, 2, KD, P)
        scores = both[:, :, 0]
        proj = both[:, 0, 1]
        turn = both[:, 1, 1]

        names = """ld_qkvg ld_small ld_fc ld_pj ld_w1 ld_w2 ld_wo ld_low zeroed ident_ok p_masks p_const
            bias_b bias_mm bias_ok fold1 fold_qk fold_vg fold_w1 fold_wo w_hi w_ready fc_s fc_a
            fc_t pj_s pj_s2 pj_a pj_t tp_full tp_free u_t u_tc m_mm m_f m_hi m_rep l_vt l_f l_w
            lb_mm lb_ok z_w cols_mm cols_ok lo_done g_min f_m f_mt f_ms redo_ok tok_s tok_vt
            tok_sl tok_bc tok_kvs tok_q tok_of tok_ok x_dma res_dma out_dma bn_ok mv_ok ln_s ln_g
            xh xn_ok T_full x_hi x_lo L_full l_ev p_ready Z_full z_u z_w2 z_e z_l g_sc g_rel e_p
            e_m e_r dk dec_ok Q_full q_f qs_hi qs_lo K_full k_f ks_hi ks_lo VG_full vg_f vs_hi
            vs_lo g_u g_s1 g_s2 g_s3 g_sil kts_hi kts_lo SC_full a_m as_hi as_lo sr_f sd_f srs_hi
            srs_lo s_new KV_full o_sq o_ss o_t o_r y_1 y_2 kv_ev YT_full ys_hi ys_lo WO_full x_1
            x1_bn x1_mv x1_t x1_r xn2_f x1_b XT_full x2s_hi x2s_lo FC_full fc_act fc_h fc_lo
            PJ_full f_f f_u f_1 f_2 f_3 f_g W1_full w_u w_l w_h w_lo W2_full s_f s_g out_ok""".split()
        s = {n: sem(n) for n in names}

        FREED = {"T": "x_lo", "L": "l_ev", "Z": "z_w2", "Q": "q_f", "K": "k_f", "VG": "vg_f",
                 "W1": "w_u", "FC": "fc_act", "SC": "a_m", "WO": "x_1", "YT": "ys_lo", "XT": "x2s_lo"}

        block = ctx.enter_context(nc.Block())

        def at(n, per, j):
            return n * per + j

        def wait_tenant(pe, stages, stage, n, kinds, banks):
            bank, (kind, j, of_before), before = tenant(stages, stage, kinds, banks)
            m = n - 1 if of_before else n
            if before:
                m = m - 1
                if isinstance(m, int) and m < 0:
                    return bank
            pe.wait_ge(s[FREED[kind]], at(m, PER[kind], j + 1))
            return bank

        def tile4(bank_pair, t):
            return bank_pair[t // 2][:, t % 2, :]

        def if_redo(eng):
            eng.wait_ge(s["redo_ok"], 1)
            return eng.If(eng.value_load(redo[0:1, 0:1], min_val=0, max_val=1) > 0)

        @block.sync
        def _(sp):
            def two(dst, w, name):
                sp.dma_start(dst, w.rearrange("(k p) n -> p k n", p=P)).then_inc(s[name], 16)

            sp.dma_start(x_in[:, :, :], x_blocks[0]).then_inc(s["x_dma"], 16)
            sp.dma_start(vg[:, :, :].rearrange("p t (a d) -> p (t a) d", a=2),
                         w_fc.rearrange("(m p) d -> p m d", p=P)).then_inc(s["ld_fc"], 16)
            sp.dma_start(ring_f[:, :, :, :].rearrange("p a b n -> p a (b n)"),
                         w_proj.rearrange("(m p) n -> p m n", p=P)).then_inc(s["ld_pj"], 16)
            two(qf[:, :, 0:D], wq, "ld_qkvg")
            two(qf[:, :, D:2 * D], wk, "ld_qkvg")
            two(kf[:, :, 0:D], wv, "ld_qkvg")
            two(kf[:, :, D:2 * D], wg, "ld_qkvg")
            two(x1[:, 0:2, :], wo, "ld_wo")
            gflat = gates[:, :, :, :].rearrange("p a b n -> p (a b n)")
            two(gflat[:, 0:KD * F1].rearrange("p (k n) -> p k n", k=KD), w1, "ld_w1")
            two(gflat[:, KD * F1:2 * KD * F1].rearrange("p (k n) -> p k n", k=M1), w2, "ld_w2")

            def step(n, front, back):
                if front:
                    nxt = x_blocks[(n + 1) % NB] if isinstance(n, int) else \
                        x_blocks[sp.snap(n + 1)]
                    sp.wait_ge(s["xh"], at(n, 1, 1))
                    sp.dma_start(x_in[:, :, :], nxt).then_inc(s["x_dma"], 16)
                if back:
                    m = n - 1
                    dst = out_blocks[m] if isinstance(n, int) else out_blocks[sp.snap(n - 1)]
                    src = x_blocks[m] if isinstance(n, int) else x_blocks[sp.snap(n - 1)]
                    if not isinstance(n, int) or m >= 1:
                        sp.wait_ge(s["out_dma"], m * 16)
                    sp.dma_start(x_res[:, :, :], src).then_inc(s["res_dma"], 16)
                    sp.wait_ge(s["out_ok"], at(m, 1, 1))
                    sp.dma_start(dst, x_res[:, :, :]).then_inc(s["out_dma"], 16)

            sp.wait_ge(s["w_ready"], 1)
            step(0, True, False)
            step(1, True, True)
            with sp.Fori(2, NB - 1) as n:
                step(n, True, True)
            step(NB - 1, True, True)
            step(NB, False, True)
            sp.wait_ge(s["out_dma"], NB * 16)
            sp.wait_ge(s["x_dma"], (NB + 1) * 16)

            def again(i, nxt):
                n = i + NB
                sp.wait_ge(s["xh"], at(n, 1, 1))
                sp.dma_start(x_in[:, :, :], nxt).then_inc(s["x_dma"], 16)
                src, dst = (x_blocks[i], out_blocks[i]) if isinstance(i, int) else \
                    (x_blocks[sp.snap(i + 0)], out_blocks[sp.snap(i + 0)])
                sp.wait_ge(s["out_dma"], n * 16)
                sp.dma_start(x_res[:, :, :], src).then_inc(s["res_dma"], 16)
                sp.wait_ge(s["out_ok"], at(n, 1, 1))
                sp.dma_start(dst, x_res[:, :, :]).then_inc(s["out_dma"], 16)

            with if_redo(sp):
                with sp.Fori(0, NB - 1) as i:
                    again(i, x_blocks[sp.snap(i + 1)])
                again(NB - 1, x_blocks[0])
                sp.wait_ge(s["out_dma"], 2 * NB * 16)
                sp.wait_ge(s["x_dma"], (2 * NB + 1) * 16)

        @block.gpsimd
        def _(gp):
            gp.memset(ident[:, :], 0.0).then_inc(s["p_masks"], 1)
            gp.memset(mask[:, :], 1.0).then_inc(s["p_masks"], 1)
            gp.memset(sgm[:, :, :], 0.0).then_inc(s["zeroed"], 1)
            gp.memset(ffn[:, :, :], 0.0).then_inc(s["zeroed"], 1)
            gp.wait_ge(s["p_masks"], 2)
            gp.affine_select(out=ident[:, :], in_=ident[:, :], compare_op=ALU.not_equal, fill=1.0,
                             base=0, pattern=[[-1, P]], channel_multiplier=1).then_inc(s["ident_ok"], 1)
            gp.affine_select(out=mask[:, :], in_=mask[:, :], compare_op=ALU.is_ge, fill=0.0,
                             base=0, pattern=[[1, P]], channel_multiplier=-1).then_inc(s["ident_ok"], 1)
            gp.memset(half_neg, -0.5)
            gp.memset(eps_col, EPS)
            gp.memset(eps_head, EPS * DK).then_inc(s["p_const"], 1)
            gp.memset(S[:, :, :], 0.0).then_inc(s["s_new"], 1)

            def pow_chain_in(n):
                gp.wait_ge(s["mv_ok"], at(n, 1, 1))
                gp.tensor_tensor(st[:, 0, :], var, eps_col, ALU.add).then_inc(s["ln_s"], 1)
                gp.wait_ge(s["ln_s"], at(n, 6, 1))
                gp.tensor_tensor(st[:, 1, :], st[:, 0, :], half_neg, ALU.pow).then_inc(s["ln_s"], 1)
                gp.wait_ge(s["ln_s"], at(n, 6, 2))
                gp.tensor_tensor(st[:, 2, :], var, st[:, 1, :], ALU.mult).then_inc(s["ln_s"], 1)
                gp.wait_ge(s["ln_s"], at(n, 6, 3))
                gp.tensor_tensor(st[:, 3, :], st[:, 2, :], st[:, 1, :], ALU.mult).then_inc(s["ln_s"], 1)
                gp.wait_ge(s["ln_s"], at(n, 6, 4))
                gp.tensor_tensor(st[:, 4, :], st[:, 3, :], eps_col, ALU.add).then_inc(s["ln_s"], 1)
                gp.wait_ge(s["ln_s"], at(n, 6, 5))
                gp.tensor_tensor(st[:, 5, :], st[:, 4, :], half_neg, ALU.pow).then_inc(s["ln_s"], 1)
                gp.wait_ge(s["ln_s"], at(n, 6, 6))
                gp.tensor_tensor(st[:, 6, :], st[:, 5, :], st[:, 1, :], ALU.mult).then_inc(s["ln_g"], 1)
                gp.tensor_tensor(st[:, 7, :], st[:, 5, :], st[:, 4, :], ALU.mult).then_inc(s["ln_g"], 1)

            gp.wait_ge(s["p_const"], 1)
            pow_chain_in(0)

            wfc = vg[:, :, :].rearrange("p t (a d) -> p (t a) d", a=2)
            wpj = ring_f[:, :, :, :].rearrange("p a b n -> p a (b n)")
            gp.wait_ge(s["fc_s"], 3)
            for m in range(MH):
                gp.tensor_scalar(fc_neg[m // 4][:, m % 4, :], wfc[:, m, :], fc_nhalf[:, m:m + 1], None,
                                 ALU.is_lt).then_inc(s["fc_a"], 1)
            gp.wait_ge(s["pj_s"], 3)
            for m in range(KD):
                gp.tensor_scalar(pj_neg[m], wpj[:, m, :], pj_nhalf[:, m:m + 1], None,
                                 ALU.is_lt).then_inc(s["pj_a"], 1)
            gflat = gates[:, :, :, :].rearrange("p a b n -> p (a b n)")
            w1_st = gflat[:, 0:KD * F1].rearrange("p (k n) -> p k n", k=KD)
            w2_st = gflat[:, KD * F1:2 * KD * F1].rearrange("p (k n) -> p k n", k=M1)
            for i, (lo, w, hi) in enumerate((
                    (wo_lo[:, :, :], x1[:, 0:2, :], wo_hi[:, :, :]), (w1_lo[:, :, :], w1_st, w1_hi[:, :, :]),
                    (w2_lo[:, :, :], w2_st, w2_hi[:, :, :]))):
                gp.wait_ge(s["w_hi"], 4 + i)
                gp.tensor_tensor(lo, w, f(hi), ALU.subtract).then_inc(s["lo_done"], 1)

            def step(step_n, front, back, chunked=True):
                for kind, j, of_before in stages_of(front, back, "gp"):
                    n = step_n - 1 if of_before else step_n
                    if not chunked and kind in CHUNK_STAGES:
                        continue
                    if kind == "LNB":
                        pow_chain_in(n + 1)
                    elif kind == "Q":
                        gp.wait_ge(s["qs_hi"], at(n, KD, j + 1))
                        gp.tensor_tensor(q_lo[:, j, :], qf[:, j, :], f(q_hi[:, j, :]),
                                         ALU.subtract).then_inc(s["qs_lo"], 1)
                    elif kind == "K":
                        gp.wait_ge(s["ks_hi"], at(n, KD, j + 1))
                        gp.tensor_tensor(k_lo[:, j, :], kf[:, j, :], f(k_hi[:, j, :]),
                                         ALU.subtract).then_inc(s["ks_lo"], 1)
                    elif kind == "VG":
                        gp.wait_ge(s["vs_hi"], at(n, NT, j + 1))
                        gp.tensor_tensor(v_lo[:, j, :], vg[:, j, 0:D], f(v_hi[:, j, :]),
                                         ALU.subtract).then_inc(s["vs_lo"], 1)
                    elif kind == "SL":
                        two = slice(2 * j, 2 * j + 2)
                        gp.wait_ge(s["g_s3"], at(n, 2, j + 1))
                        gp.wait_ge(s["vs_lo"], at(n, NT, 2 * j + 2))
                        gp.tensor_tensor(vg[:, two, 0:D], vg[:, two, D:2 * D], sgm[:, two, :],
                                         ALU.mult).then_inc(s["g_sil"], 1)
                    elif kind == "SS":
                        gp.wait_ge(s["as_hi"], at(n, NT, j + 1))
                        gp.tensor_tensor(a_lo[:, :, :, :], a_f[:, :, :, :], f(a_hi[:, :, :, :]),
                                         ALU.subtract).then_inc(s["as_lo"], 1)
                    elif kind == "ST":
                        gp.wait_ge(s["s_new"], at(n, NT, j + 1))
                        if j == 0:
                            gp.wait_ge(s["dec_ok"], at(n, 1, 1))
                        gp.tensor_tensor(Sr[:, :, :], S[:, :, :],
                                         dec_r[:, :, j:j + 1].broadcast_to([P, KD, P]),
                                         ALU.mult).then_inc(s["sr_f"], 1)
                        gp.tensor_tensor(Sd[:, :, :], S[:, :, :],
                                         dec_t[:, :, j:j + 1].broadcast_to([P, KD, P]),
                                         ALU.mult).then_inc(s["sd_f"], 1)
                        gp.wait_ge(s["srs_hi"], at(n, NT, j + 1))
                        gp.tensor_tensor(Sr_lo[:, :, :], Sr[:, :, :], f(Sr_hi[:, :, :]),
                                         ALU.subtract).then_inc(s["srs_lo"], 1)
                    elif kind == "AP":
                        gp.wait_ge(s["o_ss"], at(n, NT, j + 1))
                        gp.tensor_tensor(ro[:, 0, :], ss[:, :], eps_head, ALU.add).then_inc(s["o_t"], 1)
                        gp.wait_ge(s["o_t"], at(n, NT, j + 1))
                        gp.tensor_tensor(ro[:, 1, :], ro[:, 0, :], half_neg, ALU.pow).then_inc(s["o_r"], 1)
                    elif kind == "AY":
                        gp.wait_ge(s["y_1"], at(n, NT, j + 1))
                        if j % 2 == 0:
                            gp.wait_ge(s["g_sil"], at(n, 2, j // 2 + 1))
                        gp.tensor_tensor(y2[:, :], y1[:, :], vg[:, j, 0:D], ALU.mult).then_inc(s["y_2"], 1)
                    elif kind == "WP":
                        gp.wait_ge(s["x1_mv"], at(n, NT, j + 1))
                        gp.tensor_tensor(st2[:, 0:1], mv2[:, 1:2], eps_col[:, 0:1], ALU.add).then_inc(s["x1_t"], 1)
                        gp.wait_ge(s["x1_t"], at(n, NT, j + 1))
                        gp.tensor_tensor(st2[:, 1:2], st2[:, 0:1], half_neg[:, 0:1],
                                         ALU.pow).then_inc(s["x1_r"], 1)
                    elif kind == "WN":
                        gp.wait_ge(s["xn2_f"], at(n, NT, j + 1))
                        gp.tensor_tensor(x1[:, j, :], x1[:, j, :], b2_row[:, :],
                                         ALU.add).then_inc(s["x1_b"], 1)
                    elif kind == "PG":
                        gp.wait_ge(s["f_3"], at(n, 1, 1))
                        gp.tensor_tensor(ffn[:, :, :], ffn[:, :, :], sgm[:, :, :],
                                         ALU.mult).then_inc(s["f_g"], 1)
                    elif kind == "OUT":
                        gp.wait_ge(s["s_f"], at(n, NT, NT))
                        gp.wait_ge(s["f_g"], at(n, 1, 1))
                        gp.tensor_tensor(x1[:, :, :], x1[:, :, :], ffn[:, :, :],
                                         ALU.mult).then_inc(s["s_g"], 1)
                        gp.wait_ge(s["s_g"], at(n, 1, 1))
                        gp.wait_ge(s["res_dma"], at(n, 16, 16))
                        gp.tensor_tensor(x_res[:, :, :], x1[:, :, :], x_res[:, :, :],
                                         ALU.add).then_inc(s["out_ok"], 1)

            step(0, True, False)
            with gp.Fori(1, NB) as n:
                step(n, True, True)
            step(NB, False, True)
            with if_redo(gp):
                with gp.Fori(NB, 2 * NB) as n:
                    step(n, True, False, chunked=False)
                    step(n + 1, False, True)

        @block.scalar
        def _(ac):
            ac.preload_act_table_set("natural_log_exp_and_others")
            vec = xn0[:, 2, P:2 * P]
            row, small_loads = 0, []
            for w, k in ((ln1_w, KD), (ln1_b, KD), (ln2_w, KD), (ln2_b, KD), (bgk2, KD), (b1, M1)):
                small_loads.append((vec[row:row + k, :], w.rearrange("(k p) -> k p", p=P)))
                row += k
            small_loads += [(vec[row:row + 1, e * DK:(e + 1) * DK], rms_w.rearrange("(a n) -> a n", a=1))
                            for e in range(2)]
            small_loads += [
                (gatec, gate.rearrange("(a n) -> a n", a=1).broadcast_to([P, 1])),
                (b2_row[:, :], b2.rearrange("(a n) -> a n", a=1).broadcast_to([P, D])),
                (xn0[:, 0, 0:KD * LOW].rearrange("p (k r) -> p k r", k=KD), wgk1.rearrange("(k p) r -> p k r", p=P)),
                (xn0[:, 1, 0:MH * LOW].rearrange("p (m r) -> p m r", m=MH), u.rearrange("(m p) r -> p m r", p=P)),
                (xn0[0:LOW, 2, 0:LOW], fast_b),
            ]
            for dst, src in small_loads:
                ac.dma_start(dst, src).then_inc(s["ld_small"], 16)
            ac.wait_ge(s["zeroed"], 2)
            for g in range(4):
                ac.dma_start(sgm[32 * g + LOW:32 * g + 2 * LOW, 0, :], v).then_inc(s["ld_low"], 16)
                ac.dma_start(sgm[32 * g:32 * g + LOW, 1, :], wgk2).then_inc(s["ld_low"], 16)

            gflat = gates[:, :, :, :].rearrange("p a b n -> p (a b n)")
            w1_st = gflat[:, 0:KD * F1].rearrange("p (k n) -> p k n", k=KD)
            w2_st = gflat[:, KD * F1:2 * KD * F1].rearrange("p (k n) -> p k n", k=M1)

            def ternary(lo, hi):
                for i in range(lo, hi):
                    ac.wait_ge(s["tp_full"], i + 1)
                    if i < 4:
                        half, k = i // 2, i % 2
                        dst = tern_fc[:, k, half * TB:(half + 1) * TB]
                    else:
                        dst = tern_pj[:, 2 * (i - 4):2 * (i - 4) + 2, :].rearrange("p a b -> p (a b)")
                    ac.activation(dst, ring[i % RING][:, :], ACT.Copy).then_inc(s["tp_free"], 1)

            ternary(0, 4)
            ac.wait_ge(s["l_w"], 1)
            ac.activation(wl_hi[:, :, :], xn0[:, 3, :].rearrange("p (k n) -> p k n", k=KD), ACT.Copy)\
              .then_inc(s["w_hi"], 1)
            ac.wait_ge(s["fold_qk"], 1)
            ac.activation(wqk_hi[:, :, :], qf[:, :, :], ACT.Copy).then_inc(s["w_hi"], 1)
            ac.wait_ge(s["fold_vg"], 1)
            ac.activation(wvg_hi[:, :, :], kf[:, :, :], ACT.Copy).then_inc(s["w_hi"], 1)
            ac.wait_ge(s["fold_wo"], 1)
            ac.activation(wo_hi[:, :, :], x1[:, 0:2, :], ACT.Copy).then_inc(s["w_hi"], 1)
            ac.wait_ge(s["fold_w1"], 1)
            ac.activation(w1_hi[:, :, :], w1_st, ACT.Copy).then_inc(s["w_hi"], 1)
            ac.wait_ge(s["ld_w2"], 16)
            ac.activation(w2_hi[:, :, :], w2_st, ACT.Copy).then_inc(s["w_hi"], 1)
            ternary(4, 8)
            for i in range(2):
                ac.wait_ge(s["tp_full"], 9 + i)
                ac.activation(wu[:, i * TB:(i + 1) * TB], ring[(8 + i) % RING][:, :], ACT.Copy)\
                  .then_inc(s["tp_free"], 1)

            def log_sigmoid_exp(n, per, j, buf, ready, first, second, third):
                ac.wait_ge(s[ready], at(n, per, j))
                ac.activation(buf, buf, ACT.Exp, scale=-1.0).then_inc(s[first], 1)
                ac.wait_ge(s[first], at(n, per, j))
                ac.activation(buf, buf, ACT.Ln, bias=1.0).then_inc(s[second], 1)
                ac.wait_ge(s[second], at(n, per, j))
                ac.activation(buf, buf, ACT.Exp, scale=-1.0).then_inc(s[third], 1)

            def step(step_n, front, back, chunked=True):
                stages = stages_of(front, back)

                def bank(*stage):
                    return ring[tenant(stages, stage, RING_STAGES, RING)[0]][:, :]

                for kind, j, of_before in stages_of(front, back, "ac"):
                    n = step_n - 1 if of_before else step_n
                    if not chunked and kind in CHUNK_STAGES:
                        if kind == "EX":
                            ac.wait_ge(s["g_rel"], at(n, KD, j + 1))
                            ac.activation(ug[:, j, :], wgt[:, j, :], ACT.Exp, scale=1.0 / GLN)\
                              .then_inc(s["e_p"], 1)
                        elif kind == "AV":
                            ac.wait_ge(s["tok_ok"], n - NB + 1)
                            ac.wait_ge(s["y_2"], at(n, NT, j))
                            ac.activation(y1[:, :], tok_o[:, j, :], ACT.Square).then_inc(s["o_sq"], 1)
                        continue
                    if kind == "T":
                        ac.wait_ge(s["T_full"], at(n, KD, j + 1))
                        ac.activation(xT_hi[:, j, :], bank(kind, j, of_before), ACT.Copy).then_inc(s["x_hi"], 1)
                    elif kind == "L":
                        ac.wait_ge(s["L_full"], at(n, 1, 1))
                        ac.activation(low_hi[:, :], bank(kind, j, of_before), ACT.Identity, bias=lb)
                        ac.activation(low_f, bank(kind, j, of_before), ACT.Identity, bias=lb_lo, scale=is_lo)\
                          .then_inc(s["l_ev"], 1)
                    elif kind == "Z":
                        ac.wait_ge(s["z_u"], at(n, KD, j + 1))
                        ac.activation(ug[:, j, :], ug[:, j, :], ACT.Exp, scale=-1.0).then_inc(s["z_e"], 1)
                        ac.wait_ge(s["z_e"], at(n, KD, j + 1))
                        ac.activation(ug[:, j, :], ug[:, j, :], ACT.Ln, bias=1.0).then_inc(s["z_l"], 1)
                    elif kind == "EX":
                        ac.wait_ge(s["g_rel"], at(n, KD, j + 1))
                        ac.activation(ug[:, j, :], wgt[:, j, :], ACT.Exp, scale=1.0 / GLN)\
                          .then_inc(s["e_p"], 1)
                        ac.activation(dec_r[:, j, :],
                                      G[:, j, :].rearrange("p (c t) -> p c t", t=P)[:, :, MID],
                                      ACT.Exp, scale=1.0 / GLN).then_inc(s["e_r"], 1)
                        ac.wait_ge(s["e_p"], at(n, KD, j + 1))
                        ac.activation(wgt[:, j, :], wgt[:, j, :], ACT.Exp, scale=-1.0 / GLN)\
                          .then_inc(s["e_m"], 1)
                    elif kind == "Q":
                        ac.wait_ge(s["q_f"], at(n, KD, j + 1))
                        ac.activation(q_hi[:, j, :], qf[:, j, :], ACT.Copy).then_inc(s["qs_hi"], 1)
                    elif kind == "K":
                        ac.wait_ge(s["k_f"], at(n, KD, j + 1))
                        ac.activation(k_hi[:, j, :], kf[:, j, :], ACT.Copy).then_inc(s["ks_hi"], 1)
                    elif kind == "VG":
                        ac.wait_ge(s["vg_f"], at(n, NT, j + 1))
                        ac.activation(v_hi[:, j, :], vg[:, j, 0:D], ACT.Copy).then_inc(s["vs_hi"], 1)
                    elif kind == "SIG":
                        log_sigmoid_exp(n, 2, j + 1, sgm[:, 2 * j:2 * j + 2, :], "g_u", "g_s1",
                                        "g_s2", "g_s3")
                    elif kind == "SC":
                        ac.wait_ge(s["SC_full"], at(n, NT, j + 1))
                        ac.activation(kt_hi[:, :], turn.rearrange("p a b -> p (a b)"),
                                      ACT.Copy).then_inc(s["kts_hi"], 1)
                    elif kind == "SS":
                        ac.wait_ge(s["a_m"], at(n, NT, j + 1))
                        ac.activation(a_hi[:, :, :, :], a_f[:, :, :, :], ACT.Copy).then_inc(s["as_hi"], 1)
                    elif kind == "ST":
                        ac.wait_ge(s["sr_f"], at(n, NT, j + 1))
                        ac.activation(Sr_hi[:, :, :], Sr[:, :, :], ACT.Copy).then_inc(s["srs_hi"], 1)
                    elif kind == "AV":
                        ac.wait_ge(s["KV_full"], at(n, NT, j + 1))
                        if isinstance(n, int) and n == 0 and j == 0:
                            pass
                        else:
                            ac.wait_ge(s["y_2"], at(n, NT, j))
                        ac.activation(y1[:, :], okv[:, 0, :, :].rearrange("p a b -> p (a b)"),
                                      ACT.Square).then_inc(s["o_sq"], 1)
                    elif kind == "YT":
                        ac.wait_ge(s["YT_full"], at(n, NT, j + 1))
                        ac.activation(y_hi[:, :, :], turn, ACT.Copy).then_inc(s["ys_hi"], 1)
                    elif kind == "XT":
                        ac.wait_ge(s["XT_full"], at(n, NT, j + 1))
                        ac.activation(x2_hi[:, :, j * P:(j + 1) * P], turn, ACT.Copy)\
                          .then_inc(s["x2s_hi"], 1)
                    elif kind == "FC":
                        ac.wait_ge(s["FC_full"], at(n, MH, j + 1))
                        ac.activation(ring_f[:, j % 2, 0, :], bank(kind, j, of_before), ACT.Relu,
                                      scale=fc_scale[:, j:j + 1]).then_inc(s["fc_act"], 1)
                        ac.wait_ge(s["fc_act"], at(n, MH, j + 1))
                        ac.activation(ring_hi[:, j % 2, :], ring_f[:, j % 2, 0, :], ACT.Square)
                        ac.activation(ring_f[:, j % 2, 1, :], ring_f[:, j % 2, 0, :], ACT.Square)\
                          .then_inc(s["fc_h"], 1)
                    elif kind == "PU":
                        log_sigmoid_exp(n, 1, 1, sgm[:, :, :], "f_u", "f_1", "f_2", "f_3")
                    elif kind == "W1":
                        ac.wait_ge(s["W1_full"], at(n, M1, j + 1))
                        ac.activation(ring_f[:, j % 2, 0, :], bank(kind, j, of_before), ACT.Identity,
                                      bias=b1_bias[:, j:j + 1]).then_inc(s["w_u"], 1)
                    elif kind == "WL":
                        ac.wait_ge(s["w_l"], at(n, M1, j + 1))
                        ac.activation(ring_hi[:, j % 2, :], ring_f[:, j % 2, 0, :], ACT.Square)
                        ac.activation(ring_f[:, j % 2, 1, :], ring_f[:, j % 2, 0, :], ACT.Square)\
                          .then_inc(s["w_h"], 1)

            ac.wait_ge(s["w_ready"], 1)
            step(0, True, False)
            with ac.Fori(1, NB) as n:
                step(n, True, True)
            step(NB, False, True)
            with if_redo(ac):
                with ac.Fori(NB, 2 * NB) as n:
                    step(n, True, False, chunked=False)
                    step(n + 1, False, True)

        @block.vector
        def _(ve):
            def token_stats(n):
                ve.wait_ge(s["x_dma"], at(n, 16, 16))
                for t in range(NT):
                    ve.bn_stats(bn[:, t, :], x_in[:, t, :]).then_inc(s["bn_ok"], 1)
                ve.wait_ge(s["bn_ok"], at(n, NT, NT))
                ve.memset(pad, 0.0)
                for t in range(NT):
                    i = ve.bn_aggr(mv[:, t, :], bn[:, t, :])
                i.then_inc(s["mv_ok"], 1)

            def normed(n):
                ve.wait_ge(s["ln_g"], at(n, 2, 2))
                for t in range(NT):
                    i = ve.tensor_scalar(x_hat[:, t, :], x_in[:, t, :], mv[:, t, 0:1],
                                         st[:, 6, t:t + 1], ALU.subtract, ALU.mult)
                i.then_inc(s["xh"], 1)

            def token_scan(n):
                b = n - NB
                ve.wait_ge(s["e_p"], at(n, KD, KD))
                ve.wait_ge(s["q_f"], at(n, KD, KD))
                ve.wait_ge(s["k_f"], at(n, KD, KD))
                ve.wait_ge(s["tok_s"], b * (KD * DK + 1) + 1)
                for m in range(KD):
                    i = ve.tensor_scalar(S[:, m, 0:DK], S[:, m, 0:DK], keep[:, bass.ds(n, 1)], None,
                                         ALU.mult)
                i.then_inc(s["tok_s"], 1)
                ve.wait_ge(s["tok_vt"], b + 1)
                for m in range(KD):
                    i = ve.tensor_copy(tok_v[:, m, :], ring[1 + m][:, :])
                i.then_inc(s["tok_sl"], 1)
                for m in range(KD):
                    with ve.Fori(0, DK) as c:
                        at_c = b * (KD * DK) + m * DK + c
                        ve.tensor_copy(tok_sel.rearrange("p (e d) -> p e d", e=2),
                                       ident[:, :].rearrange("p (e d) -> p e d", e=2)[:, :, bass.ds(c, 1)]
                                       .broadcast_to([P, 2, DK])).then_inc(s["tok_sl"], 1)
                        ve.wait_ge(s["tok_bc"], at_c + 1)
                        ve.tensor_tensor(tok_kv, kf[:, m, :], ring[0][:, :], ALU.mult).then_inc(s["tok_kvs"], 1)
                        ve.wait_ge(s["tok_kvs"], 3 * at_c + 1)
                        ve.wait_ge(s["tok_s"], b * (KD * DK + 1) + 2 + m * DK + c)
                        ve.scalar_tensor_tensor(tok_kv[:, 0:1], S[:, m, bass.ds(c, 1)], ug[:, m, 0:1],
                                                tok_kv[:, 0:1], ALU.mult, ALU.add).then_inc(s["tok_kvs"], 1)
                        ve.wait_ge(s["tok_kvs"], 3 * at_c + 2)
                        ve.tensor_tensor_scan(tok_h, ug[:, m, :], tok_kv, 0.0, ALU.mult,
                                              ALU.add).then_inc(s["tok_kvs"], 1)
                        ve.wait_ge(s["tok_kvs"], 3 * at_c + 3)
                        ve.memset(tok_pad, 0.0)
                        ve.tensor_copy(S[:, m, bass.ds(c, 1)], tok_h[:, TB - 1:TB]).then_inc(s["tok_s"], 1)
                        ve.tensor_tensor(tok_qh, qf[:, m, :], tok_h, ALU.mult).then_inc(s["tok_q"], 1)
                        ve.wait_ge(s["tok_of"], at_c + 1)
                for i in range(2):
                    j = ve.tensor_copy(tok_o[:, 2 * i:2 * i + 2, :], acc[i][:, :, :])
                j.then_inc(s["tok_ok"], 1)

            for q in range(4):
                rows = slice(32 * q, 32 * q + 32)
                ve.memset(sign_hi[rows, :], -1.0 if q % 2 else 1.0)
                ve.memset(is_lo[rows, :], float(q % 2))
            ve.memset(pair_mask[:, :], 0.0).then_inc(s["fold1"], 1)
            ve.memset(keep[:, :], 1.0).then_inc(s["fold1"], 1)
            ve.memset(lowest[:, :, :], 0.0)
            ve.wait_ge(s["fold1"], 2)
            ve.memset(pair_mask[0:DK, 0:DK], 1.0)
            ve.memset(pair_mask[DK:P, DK:P], 1.0)
            ve.memset(keep[:, :].rearrange("p (b m) -> p b m", b=2 * B)[:, :, 0], 0.0)
            token_stats(0)

            wfc = vg[:, :, :].rearrange("p t (a d) -> p (t a) d", a=2)
            wpj = ring_f[:, :, :, :].rearrange("p a b n -> p a (b n)")
            ve.wait_ge(s["ld_fc"], 16)
            ve.tensor_reduce(fc_half, wfc, AX.X, ALU.add, apply_absolute_value=True).then_inc(s["fc_s"], 1)
            ve.wait_ge(s["fc_s"], 1)
            ve.tensor_scalar(fc_scale, fc_half, 1.0 / D, EPS, ALU.mult, ALU.max).then_inc(s["fc_s"], 1)
            ve.wait_ge(s["fc_s"], 2)
            ve.tensor_scalar(fc_nhalf, fc_scale, -0.5, None, ALU.mult).then_inc(s["fc_s"], 1)
            ve.tensor_scalar(fc_half, fc_scale, 0.5, None, ALU.mult)
            ve.reciprocal(fc_g, fc_scale).then_inc(s["fc_s"], 1)
            normed(0)
            ve.wait_ge(s["ld_pj"], 16)
            ve.tensor_reduce(pj_half, wpj, AX.X, ALU.add, apply_absolute_value=True).then_inc(s["pj_s"], 1)
            ve.wait_ge(s["pj_s"], 1)
            ve.tensor_scalar(pj_scale, pj_half, 1.0 / FH, EPS, ALU.mult, ALU.max).then_inc(s["pj_s"], 1)
            ve.wait_ge(s["pj_s"], 2)
            ve.tensor_scalar(pj_nhalf, pj_scale, -0.5, None, ALU.mult).then_inc(s["pj_s"], 1)
            ve.tensor_scalar(pj_half, pj_scale, 0.5, None, ALU.mult).then_inc(s["pj_s"], 1)
            ve.wait_ge(s["fc_s"], 4)
            for m in range(MH):
                ve.wait_ge(s["fc_a"], m + 1)
                ve.scalar_tensor_tensor(wfc[:, m, :], wfc[:, m, :], fc_half[:, m:m + 1],
                                        f(fc_neg[m // 4][:, m % 4, :]), ALU.is_gt,
                                        ALU.subtract).then_inc(s["fc_t"], 1)
            ve.wait_ge(s["pj_s"], 4)
            ve.wait_ge(s["ident_ok"], 2)
            for m in range(KD):
                i = ve.tensor_scalar(x_res[:, 2 + m, 0:P], ident[:, :], 0.0, pj_scale[:, m:m + 1],
                                     ALU.mult, ALU.add)
            i.then_inc(s["pj_s2"], 1)
            for m in range(KD):
                ve.wait_ge(s["pj_a"], m + 1)
                ve.scalar_tensor_tensor(wpj[:, m, :], wpj[:, m, :], pj_half[:, m:m + 1], f(pj_neg[m]),
                                        ALU.is_gt, ALU.subtract).then_inc(s["pj_t"], 1)


            ve.wait_ge(s["cols_mm"], 1)
            ve.tensor_copy(cols[:, 0:NV], proj[:, 0, 0:NV]).then_inc(s["cols_ok"], 1)
            ve.wait_ge(s["cols_ok"], 1)

            ve.wait_ge(s["ld_small"], 13 * 16)
            ve.tensor_scalar(fc_g, fc_g, gatec, None, ALU.mult).then_inc(s["fc_s"], 1)

            g1 = xn0[:, 0, 0:KD * LOW].rearrange("p (k r) -> p k r", k=KD)
            wl_st = xn0[:, 3, :].rearrange("p (k n) -> p k n", k=KD)
            lraw = ffn[:, 2, :].rearrange("p (k n) -> p k n", k=KD)
            ve.wait_ge(s["l_vt"], 1)
            ve.wait_ge(s["zeroed"], 2)
            ve.tensor_copy(wl_st, turn).then_inc(s["l_f"], 1)
            ve.wait_ge(s["l_f"], 1)
            for k in range(KD):
                for q in range(4):
                    ve.tensor_scalar(wl_st[:, k, 32 * q:32 * q + LOW], g1[:, k, :], l1w[:, k:k + 1],
                                     None, ALU.mult)
                    i = ve.tensor_copy(lraw[:, k, 32 * q:32 * q + LOW], g1[:, k, :])
            i.then_inc(s["l_w"], 1)
            for k in range(KD):
                i = ve.tensor_scalar(x_res[:, k, 0:P], ident[:, :], 0.0, l1b[:, k:k + 1], ALU.mult,
                                     ALU.add)
            i.then_inc(s["bias_b"], 1)

            ve.wait_ge(s["bias_mm"], 1)
            ve.tensor_copy(vg_bias[:, :], okv[:, :, :, :].rearrange("p a b c -> p (a b c)")).then_inc(s["bias_ok"], 1)
            ve.tensor_scalar(qk_bias[:, 0:KD], proj[:, 0, 0:KD], DK ** -0.5, None, ALU.mult)
            ve.tensor_copy(qk_bias[:, KD:2 * KD], proj[:, 0, KD:2 * KD]).then_inc(s["bias_ok"], 1)
            for k in range(KD):
                ve.tensor_scalar(qf[:, k, 0:D], qf[:, k, 0:D], l1w[:, k:k + 1], DK ** -0.5, ALU.mult, ALU.mult)
                i = ve.tensor_scalar(qf[:, k, D:2 * D], qf[:, k, D:2 * D], l1w[:, k:k + 1], None, ALU.mult)
            i.then_inc(s["fold_qk"], 1)
            for k in range(KD):
                i = ve.tensor_scalar(kf[:, k, :], kf[:, k, :], l1w[:, k:k + 1], None, ALU.mult)
            i.then_inc(s["fold_vg"], 1)
            ve.wait_ge(s["ld_wo"], 16)
            ve.tensor_scalar(x1[:, 0:2, :], x1[:, 0:2, :], rmsc, DK ** 0.5, ALU.mult, ALU.mult).then_inc(s["fold_wo"], 1)
            ve.wait_ge(s["lb_mm"], 1)
            ve.tensor_copy(lb, proj[:, 1, 0:1]).then_inc(s["lb_ok"], 1)
            ve.wait_ge(s["lb_ok"], 1)
            ve.tensor_tensor(lb_lo, lb, is_lo, ALU.mult)
            ve.tensor_scalar(bz_up, bz, CLAMP, None, ALU.add)
            ve.wait_ge(s["ld_low"], 8 * 16)
            ve.tensor_copy(low_hi[:, 0:D], sgm[:, 1, :]).then_inc(s["z_w"], 1)
            ve.wait_ge(s["z_w"], 1)
            ve.tensor_copy(wz[0:64, :], f(low_hi[0:64, 0:D]))
            ve.tensor_tensor(wz[64:P, :], sgm[64:P, 1, :], f(low_hi[64:P, 0:D]), ALU.subtract)

            gflat = gates[:, :, :, :].rearrange("p a b n -> p (a b n)")
            w1_st = gflat[:, 0:KD * F1].rearrange("p (k n) -> p k n", k=KD)
            w2_st = gflat[:, KD * F1:2 * KD * F1].rearrange("p (k n) -> p k n", k=M1)
            ve.wait_ge(s["bias_mm"], 2)
            ve.tensor_tensor(b1_bias, proj[:, 1, 8:8 + M1], b1c, ALU.add).then_inc(s["bias_ok"], 1)
            for k in range(KD):
                i = ve.tensor_scalar(w1_st[:, k, :], w1_st[:, k, :], l2w[:, k:k + 1], None, ALU.mult)
            i.then_inc(s["fold_w1"], 1)

            for i, (lo, w, hi) in enumerate((
                    (wl_lo[:, :, :], wl_st, wl_hi[:, :, :]), (wqk_lo[:, :, :], qf[:, :, :], wqk_hi[:, :, :]),
                    (wvg_lo[:, :, :], kf[:, :, :], wvg_hi[:, :, :]))):
                ve.wait_ge(s["w_hi"], i + 1)
                ve.tensor_tensor(lo, w, f(hi), ALU.subtract)

            ve.wait_ge(s["u_t"], 1)
            uT = x_in[0:LOW, :, :].rearrange("p t d -> p (t d)")
            for i in range(2):
                j = ve.tensor_copy(uT[:, i * TB:(i + 1) * TB], acc[i][0:LOW, :, :].rearrange("p a b -> p (a b)"))
            j.then_inc(s["u_tc"], 1)
            ve.wait_ge(s["m_mm"], 1)
            mf = xn0[:, 0, 0:MH * LOW].rearrange("p (m r) -> p m r", m=MH)
            mh = low_hi[:, 0:MH * LOW].rearrange("p (m r) -> p m r", m=MH)
            ve.wait_ge(s["fc_s"], 5)
            ve.tensor_tensor(mf, okv[:, 0, 0, :].rearrange("p (m r) -> p m r", m=MH),
                             fc_g.rearrange("p (m a) -> p m a", a=1).broadcast_to([P, MH, LOW]), ALU.mult).then_inc(s["m_f"], 1)
            ve.wait_ge(s["m_f"], 1)
            ve.tensor_copy(mh, mf).then_inc(s["m_hi"], 1)
            ve.wait_ge(s["m_hi"], 1)
            m_rep = vg[:, :, :].rearrange("p t (a d) -> p (t a) d", a=2)[:, :, 0:P]
            ve.wait_ge(s["tp_full"], 4)
            ve.memset(m_rep, 0.0).then_inc(s["m_rep"], 1)
            ve.wait_ge(s["m_rep"], 1)
            for q in range(4):
                dst = m_rep[:, :, 32 * q + LOW:32 * q + 2 * LOW]
                if q < 2:
                    ve.tensor_copy(dst, f(mh))
                else:
                    i = ve.tensor_tensor(dst, mf, f(mh), ALU.subtract)
            i.then_inc(s["m_rep"], 1)
            ve.wait_ge(s["bias_mm"], 3)
            ve.tensor_copy(pj_scale_row[:, :], turn.rearrange("p a b -> p (a b)")).then_inc(s["bias_ok"], 1)
            ve.wait_ge(s["lo_done"], 3)
            ve.wait_ge(s["tp_free"], 10)
            ve.wait_ge(s["bias_ok"], 4)
            ve.engine_nop().then_inc(s["w_ready"], 1)

            def step(step_n, front, back, chunked=True):
                stages = stages_of(front, back)

                def bank(*stage):
                    return ring[tenant(stages, stage, RING_STAGES, RING)[0]][:, :]

                for kind, j, of_before in stages_of(front, back, "ve"):
                    n = step_n - 1 if of_before else step_n
                    if not chunked and kind in CHUNK_STAGES:
                        if kind == "SCAN":
                            ve.wait_ge(s["z_w2"], at(n, KD, j + 1))
                            ve.wait_ge(s["z_l"], at(n, KD, j + 1))
                            ve.tensor_tensor(wgt[:, j, :], wgt[:, j, :], ug[:, j, :],
                                             ALU.subtract).then_inc(s["g_rel"], 1)
                        elif kind in ("Q", "K"):
                            dst, c = (qf, j) if kind == "Q" else (kf, KD + j)
                            ve.wait_ge(s[kind + "_full"], at(n, KD, j + 1))
                            ve.tensor_scalar(dst[:, j, :], bank(kind, j, of_before), qk_bias[:, c:c + 1],
                                             None, ALU.add).then_inc(s["q_f" if kind == "Q" else "k_f"], 1)
                        elif kind == "SC":
                            ve.engine_nop().then_inc(s["a_m"], 1)
                        elif kind == "AV":
                            if j == 0:
                                token_scan(n)
                            ve.wait_ge(s["o_sq"], at(n, NT, j + 1))
                            ve.tensor_reduce(ss[:, :], y1[:, :].rearrange("p (h d) -> p h d", h=H), AX.X,
                                             ALU.add).then_inc(s["o_ss"], 1)
                        continue
                    if kind == "LNA":
                        token_stats(n + 1)
                    elif kind == "LNC":
                        normed(n + 1)
                    elif kind == "XN":
                        ve.tensor_copy(rr_c[:, :], st[:, 4, :])
                        for t in range(NT):
                            i = ve.tensor_scalar(xn0[:, t, :], x_hat[:, t, :], st[:, 7, t:t + 1], None,
                                                 ALU.mult)
                        i.then_inc(s["xn_ok"], 1)
                    elif kind == "T":
                        ve.wait_ge(s["x_hi"], at(n, KD, j + 1))
                        ve.tensor_tensor(xT_lo[:, j, :], bank(kind, j, of_before), f(xT_hi[:, j, :]),
                                         ALU.subtract).then_inc(s["x_lo"], 1)
                    elif kind == "L":
                        ve.wait_ge(s["l_ev"], at(n, 1, 1))
                        ve.scalar_tensor_tensor(low[:, :], f(low_hi[:, :]), sign_hi, low_f, ALU.mult,
                                                ALU.add).then_inc(s["p_ready"], 1)
                    elif kind == "Z":
                        ve.wait_ge(s["Z_full"], at(n, KD, j + 1))
                        ve.tensor_scalar(ug[:, j, :], bank(kind, j, of_before), bz[:, j:j + 1], -CLAMP, ALU.add,
                                         ALU.max).then_inc(s["z_u"], 1)
                        ve.tensor_scalar(wgt[:, j, :], bank(kind, j, of_before), bz_up[:, j:j + 1], 0.0, ALU.add,
                                         ALU.min).then_inc(s["z_w2"], 1)
                    elif kind == "SCAN":
                        ve.wait_ge(s["z_w2"], at(n, KD, j + 1))
                        ve.wait_ge(s["z_l"], at(n, KD, j + 1))
                        for c in range(NT):
                            part = slice(c * P, (c + 1) * P)
                            i = ve.tensor_tensor_scan(G[:, j, part], wgt[:, j, part], ug[:, j, part],
                                                      0.0, ALU.add, ALU.subtract)
                        i.then_inc(s["g_sc"], 1)
                        ve.wait_ge(s["g_sc"], at(n, 2 * KD, 2 * j + 1))
                        gc = G[:, j, :].rearrange("p (c t) -> p c t", t=P)
                        if not (isinstance(n, int) and n == 0 and j == 0):
                            ve.wait_ge(s["g_min"], at(n, KD, j))
                        ve.tensor_tensor(lowest[:, j, :], lowest[:, j, :], gc[:, :, P - 1],
                                         ALU.min).then_inc(s["g_min"], 1)
                        mid = g_mid[:, j * NT:(j + 1) * NT]
                        ve.tensor_scalar(mid, gc[:, :, MID], SPAN * GLN, None, ALU.max).then_inc(s["g_sc"], 1)
                        ve.wait_ge(s["g_sc"], at(n, 2 * KD, 2 * j + 2))
                        ve.scalar_tensor_tensor(wgt[:, j, :].rearrange("p (c t) -> p c t", t=P), gc,
                                                SPAN * GLN, mid.unsqueeze(2).broadcast_to([P, NT, P]),
                                                ALU.max, ALU.subtract).then_inc(s["g_rel"], 1)
                    elif kind == "DEC":
                        ve.wait_ge(s["e_r"], at(n, KD, KD))
                        ve.tensor_scalar(dec_r[:, :, 0], dec_r[:, :, 0],
                                         keep[:, bass.ds(n, 1)] if not isinstance(n, int)
                                         else keep[:, n:n + 1], None, ALU.mult).then_inc(s["dk"], 1)
                        ve.wait_ge(s["dk"], at(n, 1, 1))
                        ve.wait_ge(s["e_p"], at(n, KD, KD))
                        ends = ug[:, :, :].rearrange("p k (c t) -> p k c t", t=P)[:, :, :, P - 1]
                        ve.tensor_tensor(dec_t[:, :, :], dec_r[:, :, :], ends,
                                         ALU.mult).then_inc(s["dec_ok"], 1)
                    elif kind == "Q":
                        ve.wait_ge(s["Q_full"], at(n, KD, j + 1))
                        ve.wait_ge(s["e_p"], at(n, KD, j + 1))
                        ve.scalar_tensor_tensor(qf[:, j, :], bank(kind, j, of_before), qk_bias[:, j:j + 1],
                                                ug[:, j, :], ALU.add, ALU.mult).then_inc(s["q_f"], 1)
                    elif kind == "K":
                        ve.wait_ge(s["K_full"], at(n, KD, j + 1))
                        ve.wait_ge(s["e_m"], at(n, KD, j + 1))
                        ve.scalar_tensor_tensor(kf[:, j, :], bank(kind, j, of_before),
                                                qk_bias[:, KD + j:KD + j + 1], wgt[:, j, :],
                                                ALU.add, ALU.mult).then_inc(s["k_f"], 1)
                    elif kind == "VG":
                        ve.wait_ge(s["VG_full"], at(n, NT, j + 1))
                        ve.tensor_tensor(vg[:, j, :], bank(kind, j, of_before), vg_bias[:, :],
                                         ALU.add).then_inc(s["vg_f"], 1)
                    elif kind == "SIG":
                        two = slice(2 * j, 2 * j + 2)
                        ve.wait_ge(s["vg_f"], at(n, NT, 2 * j + 2))
                        if j == 0 and not (isinstance(n, int) and n == 0):
                            ve.wait_ge(s["f_g"], at(n, 1, 0))
                        ve.tensor_scalar(sgm[:, two, :], vg[:, two, D:2 * D], -CLAMP, None,
                                         ALU.max).then_inc(s["g_u"], 1)
                    elif kind == "PU":
                        ve.wait_ge(s["f_f"], at(n, NT, NT))
                        ve.tensor_scalar(sgm[:, :, :], ffn[:, :, :], -CLAMP, None,
                                         ALU.max).then_inc(s["f_u"], 1)
                    elif kind == "SC":
                        ve.wait_ge(s["kts_hi"], at(n, NT, j + 1))
                        ve.tensor_tensor(kt_lo[:, :], turn.rearrange("p a b -> p (a b)"),
                                         f(kt_hi[:, :]), ALU.subtract).then_inc(s["kts_lo"], 1)
                        ve.tensor_tensor(a_f[:, :, :, :].rearrange("p a b t -> p (a b) t"),
                                         both[:, :, :, :, :].rearrange("p a r b t -> p (a r) b t")[:, 0:3:2],
                                         mask[:, :].unsqueeze(1).broadcast_to([P, H, P]),
                                         ALU.mult).then_inc(s["a_m"], 1)
                    elif kind == "AV":
                        ve.wait_ge(s["o_sq"], at(n, NT, j + 1))
                        ve.tensor_reduce(ss[:, :], y1[:, :].rearrange("p (h d) -> p h d", h=H), AX.X,
                                         ALU.add).then_inc(s["o_ss"], 1)
                        ve.wait_ge(s["KV_full"], at(n, NT, j + 1))
                        for m in range(KD):
                            end = ug[:, m, (j + 1) * P - 1:(j + 1) * P]
                            i = ve.scalar_tensor_tensor(kv[:, m, :], okv[:, 1, m, :], end,
                                                        pair_mask[:, :], ALU.mult, ALU.mult)
                        i.then_inc(s["kv_ev"], 1)
                        ve.wait_ge(s["kv_ev"], at(n, NT, j + 1))
                        ve.wait_ge(s["sd_f"], at(n, NT, j + 1))
                        ve.tensor_tensor(S[:, :, :], Sd[:, :, :], kv[:, :, :],
                                         ALU.add).then_inc(s["s_new"], 1)
                    elif kind == "AY":
                        ve.wait_ge(s["o_r"], at(n, NT, j + 1))
                        o = okv[:, 0, :, :].rearrange("p a (b d) -> p (a b) d", d=DK) if chunked \
                            else tok_o[:, j, :].rearrange("p (h d) -> p h d", h=H)
                        ve.tensor_tensor(y1[:, :].rearrange("p (h d) -> p h d", h=H), o,
                                         ro[:, 1, :].unsqueeze(2).broadcast_to([P, H, DK]),
                                         ALU.mult).then_inc(s["y_1"], 1)
                    elif kind == "YT":
                        ve.wait_ge(s["ys_hi"], at(n, NT, j + 1))
                        ve.tensor_tensor(y_lo[:, :, :], turn, f(y_hi[:, :, :]),
                                         ALU.subtract).then_inc(s["ys_lo"], 1)
                    elif kind == "WO":
                        ve.wait_ge(s["WO_full"], at(n, NT, j + 1))
                        if j == 0:
                            ve.wait_ge(s["xn_ok"], at(n, 1, 1))
                            if not (isinstance(n, int) and n == 0):
                                ve.wait_ge(s["out_ok"], at(n, 1, 0))
                        ve.tensor_tensor(x1[:, j, :], proj.rearrange("p a b -> p (a b)"),
                                         xn0[:, j, :], ALU.add).then_inc(s["x_1"], 1)
                        ve.wait_ge(s["x_1"], at(n, NT, j + 1))
                        ve.bn_stats(bn2[:, :], x1[:, j, :]).then_inc(s["x1_bn"], 1)
                        ve.wait_ge(s["x1_bn"], at(n, NT, j + 1))
                        ve.memset(pad, 0.0)
                        ve.bn_aggr(mv2[:, :], bn2[:, :]).then_inc(s["x1_mv"], 1)
                    elif kind == "WN":
                        ve.wait_ge(s["x1_r"], at(n, NT, j + 1))
                        ve.tensor_scalar(xn2[:, :], x1[:, j, :], mv2[:, 0:1], st2[:, 1:2],
                                         ALU.subtract, ALU.mult).then_inc(s["xn2_f"], 1)
                    elif kind == "XT":
                        ve.wait_ge(s["x2s_hi"], at(n, NT, j + 1))
                        ve.tensor_tensor(x2_lo[:, :, j * P:(j + 1) * P], turn,
                                         f(x2_hi[:, :, j * P:(j + 1) * P]),
                                         ALU.subtract).then_inc(s["x2s_lo"], 1)
                    elif kind == "FL":
                        ve.wait_ge(s["fc_h"], at(n, MH, j + 1))
                        ve.tensor_tensor(ring_lo[:, j % 2, :], ring_f[:, j % 2, 1, :],
                                         f(ring_hi[:, j % 2, :]), ALU.subtract).then_inc(s["fc_lo"], 1)
                    elif kind == "PF":
                        ve.wait_ge(s["PJ_full"], at(n, 1, 1))
                        for t in range(NT):
                            ve.scalar_tensor_tensor(ffn[:, t, :], tile4(acc, t), rr_c[:, t:t + 1],
                                                    pj_scale_row[:, :], ALU.mult,
                                                    ALU.mult).then_inc(s["f_f"], 1)
                    elif kind == "W1":
                        ve.wait_ge(s["w_u"], at(n, M1, j + 1))
                        ve.scalar_tensor_tensor(ring_f[:, j % 2, 0, :], ring_f[:, j % 2, 0, :], 0.01,
                                                ring_f[:, j % 2, 0, :], ALU.mult,
                                                ALU.max).then_inc(s["w_l"], 1)
                    elif kind == "WL":
                        ve.wait_ge(s["w_h"], at(n, M1, j + 1))
                        ve.tensor_tensor(ring_lo[:, j % 2, :], ring_f[:, j % 2, 1, :],
                                         f(ring_hi[:, j % 2, :]), ALU.subtract).then_inc(s["w_lo"], 1)
                    elif kind == "OUT":
                        ve.wait_ge(s["W2_full"], at(n, 1, 1))
                        ve.wait_ge(s["x1_b"], at(n, NT, NT))
                        for t in range(NT):
                            ve.tensor_tensor(x1[:, t, :], tile4(acc, t), x1[:, t, :],
                                             ALU.add).then_inc(s["s_f"], 1)

            step(0, True, False)
            with ve.Fori(1, NB) as n:
                step(n, True, True)
            step(NB, False, True)
            ve.wait_ge(s["g_min"], NB * KD)
            ve.tensor_reduce(flag[:, 0:1], lowest[:, :, :].rearrange("p k c -> p (k c)"), AX.X,
                             ALU.min).then_inc(s["f_m"], 1)
            ve.wait_ge(s["f_mt"], 1)
            ve.tensor_reduce(flag[0:1, 1:2], turn[0:1, 0, :], AX.X, ALU.min).then_inc(s["f_ms"], 1)
            ve.wait_ge(s["f_ms"], 1)
            ve.tensor_scalar(redo[0:1, 0:1], flag[0:1, 1:2], SPAN * GLN, None, ALU.is_lt).then_inc(s["redo_ok"], 1)
            with if_redo(ve):
                ve.memset(S[:, :, :], 0.0).then_inc(s["tok_s"], 1)
                with ve.Fori(NB, 2 * NB) as n:
                    step(n, True, False, chunked=False)
                    step(n + 1, False, True)

        @block.tensor
        def _(pe):
            def split3(dst, l_hi, l_lo, r_hi, r_lo, start, stop):
                pe.matmul(dst, l_hi, r_hi, start=start, stop=False, skip_group_check=True)
                pe.matmul(dst, l_lo, r_hi, start=False, stop=False, skip_group_check=True)
                return pe.matmul(dst, l_hi, r_lo, start=False, stop=stop, skip_group_check=True)

            def turned(dst, src):
                return pe.transpose(dst, src, ident[:, :])

            wfc = vg[:, :, :].rearrange("p t (a d) -> p (t a) d", a=2)
            wpj = ring_f[:, :, :, :].rearrange("p a b n -> p a (b n)")

            def ternary(lo, hi):
                for i in range(lo, hi):
                    if i < 4:
                        pe.wait_ge(s["fc_t"], 4 * (i // 2) + 4)
                    else:
                        pe.wait_ge(s["pj_t"], KD)
                    if i >= RING:
                        pe.wait_ge(s["tp_free"], i + 1 - RING)
                    for q in range(4):
                        if i < 4:
                            m, k = 4 * (i // 2) + q, i % 2
                            src = wfc[:, m, k * P:(k + 1) * P]
                        else:
                            m, o = 2 * (i - 4) + q // 2, q % 2
                            src = wpj[:, o, m * P:(m + 1) * P]
                        j = turned(ring[i % RING][:, q * P:(q + 1) * P], src)
                    j.then_inc(s["tp_full"], 1)

            pe.wait_ge(s["ident_ok"], 2)
            ternary(0, 4)
            pe.wait_ge(s["ld_small"], 13 * 16)
            pe.transpose(proj[:, 0, 0:NV], xn0[0:NV, 2, P:2 * P], ident[0:NV, 0:NV]).then_inc(s["cols_mm"], 1)
            pe.wait_ge(s["ld_low"], 8 * 16)
            for k in range(KD):
                i = turned(turn[:, k, :], sgm[:, 0, k * P:(k + 1) * P])
            i.then_inc(s["l_vt"], 1)
            for m in range(MH):
                i = turned(acc[m // 4][0:LOW, (m % 4) // 2, (m % 2) * P:(m % 2 + 1) * P],
                           xn0[:, 1, m * LOW:(m + 1) * LOW])
            i.then_inc(s["u_t"], 1)
            pe.wait_ge(s["bias_b"], 1)
            pe.wait_ge(s["ld_qkvg"], 4 * 16)
            vgb = okv[:, :, :, :].rearrange("p a b c -> p (a b c)")
            for k in range(KD):
                pe.matmul(vgb, x_res[:, k, 0:P], kf[:, k, :], start=k == 0, stop=k == KD - 1)
            pe.wait_ge(s["cols_ok"], 1)
            for c in range(2 * KD):
                for k in range(KD):
                    i = pe.matmul(proj[:, 0, c:c + 1], qf[:, k, c * P:(c + 1) * P], l1b[:, k:k + 1],
                                  start=k == 0, stop=k == KD - 1)
            i.then_inc(s["bias_mm"], 1)
            pe.wait_ge(s["l_w"], 1)
            pe.wait_ge(s["bias_ok"], 2)
            for k in range(KD):
                i = pe.matmul(proj[:, 1, 0:1], ffn[:, 2, k * P:(k + 1) * P], l1b[:, k:k + 1],
                              start=k == 0, stop=k == KD - 1)
            i.then_inc(s["lb_mm"], 1)
            gflat = gates[:, :, :, :].rearrange("p a b n -> p (a b n)")
            pe.wait_ge(s["ld_w1"], 16)
            pe.wait_ge(s["lb_ok"], 1)
            for c in range(M1):
                for k in range(KD):
                    i = pe.matmul(proj[:, 1, 8 + c:9 + c], gflat[:, k * F1 + c * P:k * F1 + (c + 1) * P],
                                  l2b[:, k:k + 1], start=k == 0, stop=k == KD - 1)
            i.then_inc(s["bias_mm"], 1)
            ternary(4, 8)
            pe.wait_ge(s["pj_s2"], 1)
            for m in range(KD):
                i = pe.matmul(turn[:, m, :], x_res[:, 2 + m, 0:P], ident[:, :], start=True, stop=True)
            i.then_inc(s["bias_mm"], 1)
            pe.wait_ge(s["u_tc"], 1)
            pe.wait_ge(s["bias_ok"], 1)
            uT = x_in[0:LOW, :, :].rearrange("p t d -> p (t d)")
            for m in range(MH):
                i = pe.matmul(okv[:, 0, 0, m * LOW:(m + 1) * LOW], uT[:, m * P:(m + 1) * P],
                              xn0[0:LOW, 2, 0:LOW], start=True, stop=True)
            i.then_inc(s["m_mm"], 1)
            pe.wait_ge(s["m_rep"], 2)
            for i in range(2):
                pe.wait_ge(s["tp_free"], 6 + i)
                for q in range(4):
                    j = turned(ring[(8 + i) % RING][:, q * P:(q + 1) * P], wfc[:, 4 * i + q, 0:P])
                j.then_inc(s["tp_full"], 1)
            pe.wait_ge(s["w_ready"], 1)

            def token_scan(n):
                b = n - NB
                pe.wait_ge(s["k_f"], at(n, KD, KD))
                pe.wait_ge(s["vs_lo"], at(n, NT, NT))
                for m in range(KD):
                    for t in range(NT):
                        for a, v in enumerate((v_hi, v_lo)):
                            i = pe.matmul(ring[1 + m][:, t * P:(t + 1) * P], f(v[:, t, m * P:(m + 1) * P]),
                                          ident[:, :], start=a == 0, stop=a == 1, skip_group_check=True)
                i.then_inc(s["tok_vt"], 1)
                heads = pair_mask[:, :].rearrange("p (e d) -> p e d", e=2)[:, :, 0]
                for m in range(KD):
                    with pe.Fori(0, DK) as c:
                        at_c = b * (KD * DK) + m * DK + c
                        pe.wait_ge(s["tok_sl"], b * (KD * DK + 1) + m * DK + c + 2)
                        pe.matmul(ring[0][:, :], tok_sel, tok_v[:, m, :], start=True, stop=True)\
                          .then_inc(s["tok_bc"], 1)
                        pe.wait_ge(s["tok_q"], at_c + 1)
                        for t in range(NT):
                            o = tile4(acc, t).rearrange("p (h d) -> p h d", h=H)
                            i = pe.matmul(o[:, 2 * m:2 * m + 2, bass.ds(c, 1)], tok_qh[:, t * P:(t + 1) * P],
                                          heads, start=True, stop=True, skip_group_check=True)
                        i.then_inc(s["tok_of"], 1)
                pe.wait_ge(s["tok_ok"], b + 1)

            def step(step_n, front, back, chunked=True):
                stages = stages_of(front, back)
                for stage in stages:
                    kind, j, of_before = stage
                    n = step_n - 1 if of_before else step_n
                    if not chunked and kind in ("SC", "AV"):
                        if kind == "AV" and j == 0:
                            token_scan(n)
                        continue
                    if kind in RING_STAGES:
                        if kind == "T" and j == 0:
                            pe.wait_ge(s["xh"], at(n, 1, 1))
                        dst = ring[wait_tenant(pe, stages, stage, step_n, RING_STAGES, RING)][:, :]
                    for kinds in (PROJ_STAGES, TURN_STAGES):
                        if kind in kinds:
                            wait_tenant(pe, stages, stage, step_n, kinds, 1)
                    if kind == "T":
                        for t in range(NT):
                            i = turned(dst[:, t * P:(t + 1) * P], x_hat[:, t, j * P:(j + 1) * P])
                        i.then_inc(s["T_full"], 1)
                    elif kind == "L":
                        pe.wait_ge(s["x_lo"], at(n, KD, KD))
                        for k in range(KD):
                            i = split3(dst, wl_hi[:, k, :], wl_lo[:, k, :], xT_hi[:, k, :],
                                       xT_lo[:, k, :], k == 0, k == KD - 1)
                        i.then_inc(s["L_full"], 1)
                    elif kind == "Z":
                        if j == 0:
                            pe.wait_ge(s["p_ready"], at(n, 1, 1))
                        pe.matmul(dst, wz[:, j * P:(j + 1) * P], low[:, :], start=True, stop=True)\
                          .then_inc(s["Z_full"], 1)
                    elif kind in ("Q", "K"):
                        c = (j if kind == "Q" else KD + j) * P
                        for k in range(KD):
                            i = split3(dst, wqk_hi[:, k, c:c + P], wqk_lo[:, k, c:c + P],
                                       xT_hi[:, k, :], xT_lo[:, k, :], k == 0, k == KD - 1)
                        i.then_inc(s[kind + "_full"], 1)
                    elif kind == "VG":
                        if j == 0:
                            pe.wait_ge(s["x_lo"], at(n, KD, KD))
                        tok = slice(j * P, (j + 1) * P)
                        for k in range(KD):
                            i = split3(dst, xT_hi[:, k, tok], xT_lo[:, k, tok], wvg_hi[:, k, :],
                                       wvg_lo[:, k, :], k == 0, k == KD - 1)
                        i.then_inc(s["VG_full"], 1)
                    elif kind == "SC":
                        tok = slice(j * P, (j + 1) * P)
                        if j == 0:
                            pe.wait_ge(s["k_f"], at(n, KD, KD))
                        for m in range(KD):
                            i = turned(turn[:, m, :], kf[:, m, tok])
                        if j == 0:
                            pe.wait_ge(s["qs_lo"], at(n, KD, KD))
                            pe.wait_ge(s["ks_lo"], at(n, KD, KD))
                        for m in range(KD):
                            for a, (ks, qs) in enumerate(((k_hi, q_hi), (k_lo, q_hi), (k_hi, q_lo))):
                                for e in range(2):
                                    rows = slice(e * DK, (e + 1) * DK)
                                    i = pe.matmul(scores[:, e, m, :], ks[rows, m, tok],
                                                  qs[rows, m, tok], start=a == 0, stop=a == 2,
                                                  skip_group_check=True)
                        i.then_inc(s["SC_full"], 1)
                    elif kind == "AV":
                        pe.wait_ge(s["as_lo"], at(n, NT, j + 1))
                        pe.wait_ge(s["vs_lo"], at(n, NT, j + 1))
                        pe.wait_ge(s["srs_lo"], at(n, NT, j + 1))
                        if not (isinstance(n, int) and n == 0 and j == 0):
                            pe.wait_ge(s["y_1"], at(n, NT, j))
                        tok = slice(j * P, (j + 1) * P)
                        for m in range(KD):
                            for e in range(2):
                                h = 2 * m + e
                                split3(okv[:, 0, m, e * DK:(e + 1) * DK], a_hi[:, e, m, :], a_lo[:, e, m, :],
                                       v_hi[:, j, h * DK:(h + 1) * DK], v_lo[:, j, h * DK:(h + 1) * DK],
                                       e == 0, False)
                            i = split3(okv[:, 0, m, :], q_hi[:, m, tok], q_lo[:, m, tok],
                                       Sr_hi[:, m, :], Sr_lo[:, m, :], False, True)
                        pe.wait_ge(s["kts_lo"], at(n, NT, j + 1))
                        for m in range(KD):
                            c = slice(m * P, (m + 1) * P)
                            i = split3(okv[:, 1, m, :], kt_hi[:, c], kt_lo[:, c], v_hi[:, j, c],
                                       v_lo[:, j, c], True, True)
                        i.then_inc(s["KV_full"], 1)
                    elif kind == "YT":
                        pe.wait_ge(s["y_2"], at(n, NT, j + 1))
                        for m in range(KD):
                            i = turned(turn[:, m, :], y2[:, m * P:(m + 1) * P])
                        i.then_inc(s["YT_full"], 1)
                    elif kind == "WO":
                        pe.wait_ge(s["ys_lo"], at(n, NT, j + 1))
                        o = proj.rearrange("p a b -> p (a b)")
                        for k in range(KD):
                            i = split3(o, y_hi[:, k, :], y_lo[:, k, :], wo_hi[:, k, :], wo_lo[:, k, :],
                                       k == 0, k == KD - 1)
                        i.then_inc(s["WO_full"], 1)
                    elif kind == "XT":
                        pe.wait_ge(s["xn2_f"], at(n, NT, j + 1))
                        for m in range(KD):
                            i = turned(turn[:, m, :], xn2[:, m * P:(m + 1) * P])
                        i.then_inc(s["XT_full"], 1)
                    elif kind == "FC":
                        c = slice(j * P, (j + 1) * P)
                        pe.matmul(dst, wu[:, c], low[:, :], start=True, stop=False, skip_group_check=True)
                        for k in range(KD):
                            pe.matmul(dst, tern_fc[:, k, c], xT_hi[:, k, :], start=False, stop=False,
                                      skip_group_check=True)
                            i = pe.matmul(dst, tern_fc[:, k, c], xT_lo[:, k, :], start=False,
                                          stop=k == KD - 1, skip_group_check=True)
                        i.then_inc(s["FC_full"], 1)
                    elif kind == "PJ":
                        pe.wait_ge(s["fc_lo"], at(n, MH, j + 1))
                        if j == 0 and not (isinstance(n, int) and n == 0):
                            pe.wait_ge(s["s_f"], at(n, NT, 0))
                        for t in range(NT):
                            tok = slice(t * P, (t + 1) * P)
                            pe.matmul(tile4(acc, t), ring_hi[:, j % 2, tok], tern_pj[:, j, :],
                                      start=j == 0 and t % 2 == 0, stop=False, skip_group_check=True)
                            i = pe.matmul(tile4(acc, t), ring_lo[:, j % 2, tok], tern_pj[:, j, :],
                                          start=False, stop=j == MH - 1, skip_group_check=True)
                        if j == MH - 1:
                            i.then_inc(s["PJ_full"], 1)
                    elif kind == "W1":
                        if j == 0:
                            pe.wait_ge(s["x2s_lo"], at(n, NT, NT))
                        c = slice(j * P, (j + 1) * P)
                        for k in range(KD):
                            i = split3(dst, w1_hi[:, k, c], w1_lo[:, k, c], x2_hi[:, k, :],
                                       x2_lo[:, k, :], k == 0, k == KD - 1)
                        i.then_inc(s["W1_full"], 1)
                    elif kind == "W2":
                        pe.wait_ge(s["w_lo"], at(n, M1, j + 1))
                        if j == 0:
                            pe.wait_ge(s["f_f"], at(n, NT, NT))
                        for t in range(NT):
                            tok = slice(t * P, (t + 1) * P)
                            i = split3(tile4(acc, t), ring_hi[:, j % 2, tok], ring_lo[:, j % 2, tok],
                                       w2_hi[:, j, :], w2_lo[:, j, :], j == 0 and t % 2 == 0,
                                       j == M1 - 1)
                        if j == M1 - 1:
                            i.then_inc(s["W2_full"], 1)

            step(0, True, False)
            with pe.Fori(1, NB) as n:
                step(n, True, True)
            step(NB, False, True)
            pe.wait_ge(s["f_m"], 1)
            pe.transpose(turn[0:1, 0, :], flag[:, 0:1], ident[:, :]).then_inc(s["f_mt"], 1)
            with if_redo(pe):
                with pe.Fori(NB, 2 * NB) as n:
                    step(n, True, False, chunked=False)
                    step(n + 1, False, True)


_ATTN = ["x", "ln1_w", "ln1_b", "Wq", "Wk", "Wv", "Wg", "Wgk1", "Wgk2", "bgk2", "rms_w", "Wo",
         "ln2_w", "ln2_b", "W1", "b1", "W2", "b2"]
_FFN = ["fast_b", "w_fc", "w_proj", "u", "v", "gate"]
_INS = [f"L0_attn_{n}" for n in _ATTN] + [f"L0_ffn_{n}" for n in _FFN]


def kernel(**inputs):
    import numpy as _np
    import concourse.bacc as _bacc
    from concourse import mybir as _mybir
    from concourse.bass_utils import run_bass_kernel_spmd as _run

    nc = _bacc.Bacc("TRN2", target_bir_lowering=False, num_devices=1)
    arrays, args = {}, []
    for name in _INS:
        a = _np.ascontiguousarray(inputs[name])
        if a.ndim == 0:
            a = a.reshape(1)
        arrays[f"in_{name}"] = a
        args.append(nc.dram_tensor(f"in_{name}", a.shape, _mybir.dt.from_np(a.dtype),
                                   kind="ExternalInput").ap())
    out = nc.dram_tensor("out", (B, T, D), _mybir.dt.float32, kind="ExternalOutput").ap()
    recurrent_block_kernel(nc, *args, out)
    r = _run(nc, [arrays], core_ids=[0])
    return r.results[0]["out"]
```
